# Optimizing a Trainium2 kernel written in Bass

```python
import numpy as np
import jax
import jax.numpy as jnp

def _softmax(x, axis=-1):
    return jax.nn.softmax(x, axis=axis)

def _gelu(x):
    return jax.nn.gelu(x, approximate=True)

def _silu(x):
    return jax.nn.silu(x)

def _sigmoid(x):
    return jax.nn.sigmoid(x)

def _layernorm(x, axis=-1, eps=1e-05):
    m = jnp.mean(x, axis=axis, keepdims=True)
    v = jnp.var(x, axis=axis, keepdims=True)
    return (x - m) / jnp.sqrt(v + eps)

def _scatter_add(tgt, idx, src, axis=0):
    return tgt.at[idx].add(src)

def _segment_sum(src, seg, n):
    return jax.ops.segment_sum(src, seg, n)
kernel_name = 'mk_gnn_preln_d2_gnn_r32_d9e01e'

def setup_inputs(seed: int=0):
    np.random.seed(seed)
    _w = jnp.asarray

    def _rec_inputs():
        import jax
        import jax.numpy as jnp
        _gk = jax.random.key(seed)
        x = -0.0005121 + 1.001 * jax.random.normal(jax.random.fold_in(_gk, 1), (3125, 64), jnp.float32)
        _s = jax.random.randint(jax.random.fold_in(_gk, 2), (50000,), 0, 3125, jnp.int32)
        _d = jax.random.randint(jax.random.fold_in(_gk, 3), (50000,), 0, 3125, jnp.int32)
        _loop = jnp.arange(3125, dtype=jnp.int32)
        src = jnp.concatenate([_s, _d, _loop])
        dst = jnp.concatenate([_d, _s, _loop])
        _o = jnp.argsort(dst, stable=True)
        src = src[_o]
        dst = dst[_o]
        edge_attr_16 = -4.12889e-05 + 1 * jax.random.normal(jax.random.fold_in(_gk, 12), (103125, 16), jnp.float32)
        edge_type_8 = jax.random.randint(jax.random.fold_in(_gk, 14), (103125,), 0, 8, jnp.int32)
        edge_weight1 = jax.random.uniform(jax.random.fold_in(_gk, 15), (103125, 1), jnp.float32, 0.0, 0.999998)
        return (x, src, dst, edge_attr_16, edge_type_8, edge_weight1)
    x, src, dst, edge_attr_16, edge_type_8, edge_weight1 = _rec_inputs()

    def _L0_gnn_setup():
        import jax, jax.numpy as jnp
        import numpy as np
        N, E, R, D_IN, D_OUT = (50000, 25000, 8, 64, 64)
        key = jax.random.key(seed)
        ks = jax.random.split(key, 8)
        feat = jax.random.normal(ks[0], (N, D_IN), dtype=jnp.float32)
        edge_src = jax.random.randint(ks[1], (E,), 0, N, dtype=jnp.int32)
        edge_dst = jax.random.randint(ks[2], (E,), 0, N, dtype=jnp.int32)
        etype = jax.random.randint(ks[3], (E,), 0, R, dtype=jnp.int32)
        attention = jax.random.uniform(ks[4], (E, 1), dtype=jnp.float32)
        weight = jax.random.normal(ks[5], (R, D_IN, D_OUT), dtype=jnp.float32) * (6.0 / (D_IN + D_OUT)) ** 0.5
        h_bias = jnp.zeros((D_OUT,), dtype=jnp.float32)
        loop_weight = jax.random.normal(ks[6], (D_IN, D_OUT), dtype=jnp.float32) * (6.0 / (D_IN + D_OUT)) ** 0.5
        return {'feat': feat, 'edge_src': edge_src, 'edge_dst': edge_dst, 'etype': etype, 'attention': attention, 'weight': weight, 'h_bias': h_bias, 'loop_weight': loop_weight}
    _L0_gnn_all = _L0_gnn_setup()
    _L0_gnn_in = {k: v for k, v in _L0_gnn_all.items() if k in ('weight', 'h_bias', 'loop_weight')}
    del _L0_gnn_all

    def _L1_gnn_setup():
        import jax, jax.numpy as jnp
        import numpy as np
        N_NODES = 50000
        N_EDGES = 12500
        EMB = 64
        EDGE_F = 16
        HEADS = 2
        N_LAYERS = 5
        NEG_SLOPE = 0.2

        def _gat_layer(x, src_f, dst_f, edge_attr_full, W, b, eW, eb, att):
            N = x.shape[0]
            C = EMB
            edge_emb = (edge_attr_full @ eW.T + eb).reshape(-1, HEADS, C)
            xt = x @ W
            x_j = xt[src_f].reshape(-1, HEADS, C) + edge_emb
            x_i = xt[dst_f].reshape(-1, HEADS, C)
            alpha = (jnp.concatenate([x_i, x_j], axis=-1) * att[None]).sum(-1)
            alpha = jax.nn.leaky_relu(alpha, NEG_SLOPE)
            amax = jax.ops.segment_max(alpha, dst_f, num_segments=N)[dst_f]
            ex = jnp.exp(alpha - amax)
            denom = jax.ops.segment_sum(ex, dst_f, num_segments=N)[dst_f] + 1e-16
            a = ex / denom
            out = jax.ops.segment_sum(x_j * a[..., None], dst_f, num_segments=N)
            return out.mean(axis=1) + b
        key = jax.random.key(seed)
        ks = jax.random.split(key, 10)
        x = jax.random.normal(ks[0], (N_NODES, EMB), dtype=jnp.float32)
        src = jax.random.randint(ks[1], (N_EDGES,), 0, N_NODES, dtype=jnp.int32)
        off = jax.random.randint(ks[2], (N_EDGES,), 1, N_NODES, dtype=jnp.int32)
        dst = (src + off) % N_NODES
        edge_index = jnp.stack([src, dst], axis=0)
        edge_attr = jax.random.normal(ks[3], (N_EDGES, EDGE_F), dtype=jnp.float32)
        g = 0.1
        weights = jax.random.normal(ks[4], (N_LAYERS, EMB, HEADS * EMB), dtype=jnp.float32) * g
        biases = jnp.zeros((N_LAYERS, EMB), dtype=jnp.float32)
        edge_ws = jax.random.normal(ks[5], (N_LAYERS, HEADS * EMB, EDGE_F), dtype=jnp.float32) * g
        edge_bs = jnp.zeros((N_LAYERS, HEADS * EMB), dtype=jnp.float32)
        atts = jax.random.normal(ks[6], (N_LAYERS, HEADS, 2 * EMB), dtype=jnp.float32) * g
        return {'x': x, 'edge_index': edge_index, 'edge_attr': edge_attr, 'weights': weights, 'biases': biases, 'edge_ws': edge_ws, 'edge_bs': edge_bs, 'atts': atts}
    _L1_gnn_all = _L1_gnn_setup()
    _L1_gnn_in = {k: v for k, v in _L1_gnn_all.items() if k in ('weights', 'biases', 'edge_ws', 'edge_bs', 'atts')}
    del _L1_gnn_all
    return {'x': x, 'src': src, 'dst': dst, 'edge_attr_16': edge_attr_16, 'edge_type_8': edge_type_8, 'edge_weight1': edge_weight1, 'L0_gnn_weight': _L0_gnn_in['weight'], 'L0_gnn_h_bias': _L0_gnn_in['h_bias'], 'L0_gnn_loop_weight': _L0_gnn_in['loop_weight'], 'L1_gnn_weights': _L1_gnn_in['weights'], 'L1_gnn_biases': _L1_gnn_in['biases'], 'L1_gnn_edge_ws': _L1_gnn_in['edge_ws'], 'L1_gnn_edge_bs': _L1_gnn_in['edge_bs'], 'L1_gnn_atts': _L1_gnn_in['atts']}

def reference(x, src, dst, edge_attr_16, edge_type_8, edge_weight1, L0_gnn_weight, L0_gnn_h_bias, L0_gnn_loop_weight, L1_gnn_weights, L1_gnn_biases, L1_gnn_edge_ws, L1_gnn_edge_bs, L1_gnn_atts):
    import jax
    import jax.numpy as jnp

    def _L0_gnn_ref(feat, edge_src, edge_dst, etype, attention, weight, h_bias, loop_weight):
        import jax, jax.numpy as jnp
        import numpy as np
        N, E, R, D_IN, D_OUT = (50000, 25000, 8, 64, 64)
        proj = jnp.einsum('ni,rio->rno', feat, weight)
        m = (proj[etype, edge_src] + h_bias) * attention
        agg = jax.ops.segment_sum(m, edge_dst, num_segments=feat.shape[0])
        return agg + feat @ loop_weight

    def _L1_gnn_ref(x, edge_index, edge_attr, weights, biases, edge_ws, edge_bs, atts):
        import jax, jax.numpy as jnp
        import numpy as np
        N_NODES = 50000
        N_EDGES = 12500
        EMB = 64
        EDGE_F = 16
        HEADS = 2
        N_LAYERS = 5
        NEG_SLOPE = 0.2

        def _gat_layer(x, src_f, dst_f, edge_attr_full, W, b, eW, eb, att):
            N = x.shape[0]
            C = EMB
            edge_emb = (edge_attr_full @ eW.T + eb).reshape(-1, HEADS, C)
            xt = x @ W
            x_j = xt[src_f].reshape(-1, HEADS, C) + edge_emb
            x_i = xt[dst_f].reshape(-1, HEADS, C)
            alpha = (jnp.concatenate([x_i, x_j], axis=-1) * att[None]).sum(-1)
            alpha = jax.nn.leaky_relu(alpha, NEG_SLOPE)
            amax = jax.ops.segment_max(alpha, dst_f, num_segments=N)[dst_f]
            ex = jnp.exp(alpha - amax)
            denom = jax.ops.segment_sum(ex, dst_f, num_segments=N)[dst_f] + 1e-16
            a = ex / denom
            out = jax.ops.segment_sum(x_j * a[..., None], dst_f, num_segments=N)
            return out.mean(axis=1) + b
        N = x.shape[0]
        loop = jnp.arange(N, dtype=edge_index.dtype)
        src_f = jnp.concatenate([edge_index[0], loop])
        dst_f = jnp.concatenate([edge_index[1], loop])
        edge_attr_full = jnp.concatenate([edge_attr, jnp.zeros((N, edge_attr.shape[1]), edge_attr.dtype)], axis=0)
        h = x
        for l in range(N_LAYERS):
            h = _gat_layer(h, src_f, dst_f, edge_attr_full, weights[l], biases[l], edge_ws[l], edge_bs[l], atts[l])
            if l < N_LAYERS - 1:
                h = jax.nn.relu(h)
        return h
    edge_index = jnp.stack([src, dst])
    h = jnp.maximum(_layernorm(x, axis=-1), 0.0)
    x = x + _L0_gnn_ref(h, src, dst, edge_type_8, edge_weight1, L0_gnn_weight, L0_gnn_h_bias, L0_gnn_loop_weight)
    h = jnp.maximum(_layernorm(x, axis=-1), 0.0)
    x = x + _L1_gnn_ref(h, edge_index, edge_attr_16, L1_gnn_weights, L1_gnn_biases, L1_gnn_edge_ws, L1_gnn_edge_bs, L1_gnn_atts)
    return x

_drawn_inputs = setup_inputs


def setup_inputs(seed=0):
    import zlib

    import numpy as np

    out = dict(_drawn_inputs(seed))
    spreads = {'L0_gnn_h_bias': (0.0, 0.1), 'L1_gnn_biases': (0.0, 0.478), 'L1_gnn_edge_bs': (0.0, 0.71)}
    factors = {'edge_attr_16': 7.166, 'L1_gnn_weights': 8.0, 'L1_gnn_edge_ws': 7.063, 'L1_gnn_atts': 8.0}
    for name, (base, spread) in spreads.items():
        noise = np.random.default_rng([zlib.crc32(name.encode()), seed]).standard_normal(out[name].shape)
        drawn = base * np.exp(spread * noise) if base else spread * noise
        out[name] = jnp.asarray(drawn.astype(out[name].dtype))
    for name, factor in factors.items():
        out[name] = (out[name] * factor).astype(out[name].dtype)
    return out
```

```python
from contextlib import ExitStack, contextmanager

import concourse.bass as bass
from concourse import mybir

ALU = mybir.AluOpType
ACT = mybir.ActivationFunctionType
AX = mybir.AxisListType.X
F32 = mybir.dt.float32
BF16 = mybir.dt.bfloat16
I32 = mybir.dt.int32
U16 = mybir.dt.uint16

P = 128
N, D = 3125, 64
NB = (N + P - 1) // P
NPAD = NB * P
NFULL = N // P
NREST = N - NFULL * P
E = 103125
R = 8
EF = 16
LAYERS, HEADS = 5, 2
NEG_SLOPE = 0.2
LN_EPS = 1e-5
BIG = 1e30

TE, KE = 125, 11
GE = E // (TE * KE)
BUF3 = 3
assert GE * TE * KE == E and GE % BUF3 == 0

G = 8
NG = 104
NT = NG * G
SL = NT * P
GS = G * P
assert NT >= (E + (P - 1) * NB) // P + 1
RING = 8
NIT = NG // RING
assert NIT * RING == NG
RB = 32
NRB = NT // RB
W_PAY = EF + 4
ACC = 98
PER_BANK = 5
BANK = 512
NBANK = NB // PER_BANK
EA1 = EF + 1
XC = HEADS * D + 2 * HEADS
LB = 4
PER_LAYER = 329
XB = (NB + 2) // 3
SB = (NB + 3) // 4
TC = (NT + P - 1) // P
CHUNKS = [(c, min(P, NT - c * P)) for c in range(TC)]
NODE_BATCHES = [(b, min(4, NB - b)) for b in range(0, NB, 4)]


class Order:

    def __init__(self, eng, sem):
        self.eng, self.sem, self.base, self.n = eng, sem, 0, 0

    def step(self, ins):
        self.n += 1
        ins.then_inc(self.sem, 1)

    def settle(self):
        self.eng.wait_ge(self.sem, self.base + self.n)

    def link(self, ins):
        self.step(ins)
        self.settle()

    @contextmanager
    def loop(self, count, per):
        base, n = self.base, self.n
        with self.eng.Fori(0, count) as i:
            self.base, self.n = base + n + i * per, 0
            yield i
            assert self.n == per, (self.n, per)
        self.base, self.n = base, n + count * per


def build_gnn(nc, x, src, dst, edge_attr_16, edge_type_8, edge_weight1, L0_gnn_weight, L0_gnn_h_bias,
              L0_gnn_loop_weight, L1_gnn_weights, L1_gnn_biases, L1_gnn_edge_ws, L1_gnn_edge_bs, L1_gnn_atts, out):
    def dram(name, shape, dt=F32):
        return nc.dram_tensor(name, shape, dt, kind="Internal").ap()

    rows_dram = dram("rows_dram", [GE, 2, TE * KE], U16)
    slots = dram("slots", [SL, W_PAY])
    fill_dram = dram("fill_dram", [SL + NPAD, 4])
    stats_dram = dram("stats_dram", [SL + NPAD, 4])
    ea_dram = dram("ea_dram", [NRB, P, RB * EF])
    ce_dram = dram("ce_dram", [2 * LAYERS, SL])
    lo_dram = dram("lo_dram", [SL], BF16)
    line_dram = dram("line_dram", [HEADS, SL])
    key_dram = dram("key_dram", [SL + 2])
    weight_dram = dram("weight_dram", [HEADS, SL])
    tab0 = dram("tab0", [NPAD, R * D])
    tab1 = dram("tab1", [NPAD, HEADS * D])

    with ExitStack() as ctx:
        def sb(name, shape, dt=F32, where=ctx):
            return where.enter_context(nc.sbuf_tensor(name, shape, dt))

        def sem(name):
            return ctx.enter_context(nc.semaphore(name))

        ps = ctx.enter_context(nc.psum_tensor("ps", [P, 8, BANK], F32))

        FR = (SL + NPAD) * 4 // (4 * P)
        ident = sb("ident", [P, P])
        iota_row = sb("iota_row", [P, P])
        iota_col = sb("iota_col", [P, 1])
        before = sb("before", [P, P])
        ones = sb("ones", [P, P])
        zeros = sb("zeros", [P, FR])
        gate = sb("gate", [P, 1], I32)
        gate2 = sb("gate2", [P, 1])
        gate_act = sb("gate_act", [P, 2])

        x_res = sb("x_res", [P, NB, D])
        h_sb = sb("h_sb", [P, NB, D])
        start_row = sb("start_row", [P, NB], I32)
        rel = sb("rel", [P, NT])
        idx = sb("idx", [P, NT + RING * G], I32)
        tile_off = sb("tile_off", [1, NT], I32)
        tile0 = sb("tile0", [P, NB])
        mean = sb("mean", [P, NB])
        var = sb("var", [P, NB])
        w_ext = sb("w_ext", [D, LAYERS, XC])
        edge_w = sb("edge_w", [HEADS * EA1, LAYERS, D])
        bias_out = sb("bias_out", [P, LAYERS, D])
        att_bias = sb("att_bias", [P, LAYERS, HEADS])
        src_hi = sb("src_hi", [P, NT])

        with ExitStack() as prep:
            edge_i = sb("edge_i", [GE, 3, KE * TE], I32, prep)
            edge_t = sb("edge_t", [GE, 6, KE, TE], F32, prep)
            part_i = sb("part_i", [GE, 2, KE * TE], I32, prep)
            rows16 = sb("rows16", [GE, 2, KE * TE], U16, prep)
            edge_c = sb("edge_c", [TE, 6, GE, KE], F32, prep)
            lo_hot = sb("lo_hot", [TE, BUF3, KE, P], BF16, prep)
            hi_hot = sb("hi_hot", [TE, BUF3, KE, NB], BF16, prep)
            row_in = sb("row_in", [P, BUF3, 2, KE * TE], U16, prep)
            lo_hotT = sb("lo_hotT", [P, BUF3, KE, TE], F32, prep)
            same = sb("same", [TE, BUF3, KE, TE], BF16, prep)
            payload = sb("payload", [TE, BUF3, KE * W_PAY], F32, prep)
            snap = sb("snap", [P, BUF3, KE + 1, NB], F32, prep)
            picked = sb("picked", [TE, KE, NB], F32, prep)
            base_at = sb("base_at", [TE, KE], F32, prep)
            pos = sb("pos", [TE, BUF3, KE], I32, prep)
            hist = sb("hist", [P, NB], F32, prep)
            tiles_i = sb("tiles_i", [P, NB], I32, prep)
            tiles_f = sb("tiles_f", [P, NB], F32, prep)
            tiles_cum = sb("tiles_cum", [P, NB], F32, prep)
            first = sb("first", [P, NB], F32, prep)
            has = sb("has", [P, NB], F32, prep)
            spare_row = sb("spare_row", [P, NB], F32, prep)
            before16 = sb("before16", [P, P], BF16, prep)
            ones16 = sb("ones16", [P, 1], BF16, prep)
            zeros16 = sb("zeros16", [P, BANK], BF16, prep)
            empty_slots = sb("empty_slots", [P, 4, W_PAY], F32, prep)
            empty_stats = sb("empty_stats", [P, NB, 4], F32, prep)

        idx_stage = sb("idx_stage", [P, RING * G], I32)
        ring = sb("ring", [P, RING * G * P])
        onehot = sb("onehot", [P, 2, G, P])
        sums_in = sb("sums_in", [P, 2, G, ACC])
        keep = sb("keep", [NG, GS], BF16)
        keep_neg = sb("keep_neg", [NG, GS], BF16)
        keep_back = sb("keep_back", [NG, GS], BF16)
        last_slot = sb("last_slot", [NG, GS], BF16)
        head_run = sb("head_run", [NG, GS], BF16)
        head_neg = sb("head_neg", [NG, GS], BF16)
        tail_run = sb("tail_run", [NG, GS], BF16)
        row_flags = sb("row_flags", [P, 3, P])
        carry_row = sb("carry_row", [P, P])
        carry_col = sb("carry_col", [P, P])
        carry_in = sb("carry_in", [P, 4])
        turn = sb("turn", [P, HEADS, TC, P])
        with ExitStack() as zero:
            iota_tile = sb("iota_tile", [P, NT], F32, zero)
            pay = sb("pay", [P, 4, NT], F32, zero)
            blk = sb("blk", [P, NT], F32, zero)
            idx0 = sb("idx0", [P, NT + RING * G], I32, zero)
            idx0_f = sb("idx0_f", [P, NT], F32, zero)
            off_f = sb("off_f", [1, 2, NT], F32, zero)
            back = sb("back", [P, 2, RB * W_PAY], F32, zero)
            ea_pack = sb("ea_pack", [P, 2, RB * EF], F32, zero)
            w_types = sb("w_types", [D, R * D], F32, zero)
            w_loop = sb("w_loop", [D, D], F32, zero)
            bias_types = sb("bias_types", [P, D], F32, zero)
            tab0_sb = sb("tab0_sb", [P, 2, R * D], F32, zero)
            hT = sb("hT", [D, NPAD], F32, zero)
            centred = sb("centred", [P, NB, D], F32, zero)
            w_turned = sb("w_turned", [P, LAYERS, D], F32, zero)
            att = sb("att", [P, LAYERS, 2 * HEADS], F32, zero)
            edge_nat = sb("edge_nat", [P, LAYERS, EF], F32, zero)
            edge_bias = sb("edge_bias", [P, LAYERS], F32, zero)
            edge_att = sb("edge_att", [EF, LAYERS * HEADS], F32, zero)
            edge_att8 = sb("edge_att8", [P, G, LAYERS * HEADS], F32, zero)
            ea_back = sb("ea_back", [P, 2, RB * EF], F32, zero)
            ea_turned = sb("ea_turned", [P, 2, BANK], F32, zero)
            ce_sb = sb("ce_sb", [G * LAYERS * HEADS, 2, BANK], F32, zero)
            keys = sb("keys", [NG, GS + 2], F32, zero)
            ends = sb("ends", [1, 2], F32, zero)
            lo_i = sb("lo_i", [P, TC, P], I32, zero)
            hi_i = sb("hi_i", [P, NT], I32, zero)
            lo16 = sb("lo16", [P, TC, P], BF16, zero)
        with ExitStack() as zero:
            scores_all = sb("scores_all", [P, HEADS, GS], F32, zero)
            edge_terms = sb("edge_terms", [NG, HEADS, GS], F32, zero)
            filled = sb("filled", [P, GS, 4], F32, zero)
            run_total = sb("run_total", [P, 2, HEADS, GS], F32, zero)
            xt_sb = sb("xt_sb", [P, NB, XC], F32, zero)
            node_terms = sb("node_terms", [P, NB, 4], F32, zero)
            node_stats = sb("node_stats", [P, NB, 4], F32, zero)
            loop_w = sb("loop_w", [P, 4, NB, HEADS], F32, zero)
            s_src = sb("s_src", [P, 2, HEADS, NB], F32, zero)
            s_src3 = sb("s_src3", [P, 3, HEADS, NB], BF16, zero)
            lo_in_sb = sb("lo_in_sb", [P, LB, GS], BF16, zero)
            lo_hot_n = sb("lo_hot_n", [P, LB, GS], BF16, zero)
            hi_hot_n = sb("hi_hot_n", [P, LB, G, NB], BF16, zero)
            sj_part = sb("sj_part", [P, HEADS, LB * G], F32, zero)
            slot_vals = sb("slot_vals", [P, HEADS, NT], F32, zero)
            weighted = sb("weighted", [P, 2, G, HEADS, D], F32, zero)
            sj_picked = weighted[:].rearrange("p q t h d -> p (q t h d)")[:, 0:LB * G * HEADS * NB].rearrange(
                "p (q u h b) -> p q u h b", q=LB, u=G, h=HEADS)
            ea_in_sb = sb("ea_in_sb", [P, 2, G * EF], F32, zero)
        sums = filled[:].rearrange("p s c -> p (s c)")[:, 0:NB * ACC].rearrange("p (b c) -> p b c", c=ACC)
        scores = scores_all[0:NG]
        tmp_nodes = scores_all[:].rearrange("p h s -> p (h s)")[:, 0:NB * D].rearrange("p (b d) -> p b d", d=D)
        running, total = run_total[0:NG, 0], run_total[0:NG, 1]
        run_flat = run_total[:].rearrange("p a h s -> p (a h s)")[:, 0:NPAD]
        hT_l, sumsT = run_flat[0:D], run_flat[0:HEADS * EA1]

        consts_ready = sem("consts_ready")
        dve_steps = sem("dve_steps")
        act_steps = sem("act_steps")
        pe_steps = sem("pe_steps")
        pool_steps = sem("pool_steps")
        prep_over = sem("prep_over")
        slots_tiled = sem("slots_tiled")
        edges_in = sem("edges_in")
        x_in = sem("x_in")
        rows_out = sem("rows_out")
        edge_rows_ready = sem("edge_rows_ready")
        edge_cols_ready = sem("edge_cols_ready")
        edge_turned = sem("edge_turned")
        edge_turn_used = sem("edge_turn_used")
        hist_onehots = sem("hist_onehots")
        hist_used = sem("hist_used")
        hist_read = sem("hist_read")
        prefix_done = sem("prefix_done")
        scat = [sem(f"scat{q}") for q in range(BUF3)]
        rows_in = [sem(f"rows_in{q}") for q in range(BUF3)]
        pos_onehots = sem("pos_onehots")
        pos_masks = sem("pos_masks")
        counts_ready = sem("counts_ready")
        snap_ready = sem("snap_ready")
        looked_up = sem("looked_up")
        pos_ready = sem("pos_ready")
        back_in = [sem(f"back_in{q}") for q in range(2)]
        back_used = sem("back_used")
        ea_out = [sem(f"ea_out{q}") for q in range(2)]
        staged = sem("staged")
        gathered = [sem(f"gathered{j}") for j in range(RING)]
        sums_ready = sem("sums_ready")
        sums_used = sem("sums_used")
        hT_turned = sem("hT_turned")
        hT_ready = sem("hT_ready")
        w0_in = sem("w0_in")
        h_ready = sem("h_ready")
        loop_done = sem("loop_done")
        acc_read = sem("acc_read")
        back_packed = sem("back_packed")
        row_cols_ready = sem("row_cols_ready")
        tiles_ready = sem("tiles_ready")
        tiles_iota = sem("tiles_iota")
        proj_done = sem("proj_done")
        proj_used = sem("proj_used")
        tab0_out = [sem(f"tab0_out{q}") for q in range(2)]
        tab0_staged = sem("tab0_staged")
        off_ready = sem("off_ready")
        var_ready = sem("var_ready")
        std_ready = sem("std_ready")
        w1_in = sem("w1_in")
        w1_zeroed = sem("w1_zeroed")
        w1_turned = sem("w1_turned")
        w1_copied = sem("w1_copied")
        w1_products = sem("w1_products")
        edge_att_ready = sem("edge_att_ready")
        edge_att8_in = sem("edge_att8_in")
        ea_back_in = [sem(f"ea_back_in{q}") for q in range(2)]
        ea_back_turned = sem("ea_back_turned")
        ea_turned_ready = sem("ea_turned_ready")
        ce_done = sem("ce_done")
        ce_ready = sem("ce_ready")
        ce_out = [sem(f"ce_out{q}") for q in range(2)]
        ce_free = sem("ce_free")
        keys_turned = sem("keys_turned")
        keys_ready = sem("keys_ready")
        keys_out = sem("keys_out")
        keys_in = sem("keys_in")
        flags_cols = sem("flags_cols")
        flags_turned = sem("flags_turned")
        xt_done = sem("xt_done")
        xt_copied = sem("xt_copied")
        tab1_out = sem("tab1_out")
        fill_ready = sem("fill_ready")
        fill_out = sem("fill_out")
        fill_in = sem("fill_in")
        edge_terms_in = sem("edge_terms_in")
        s_src_ready = sem("s_src_ready")
        lo_in = [sem(f"lo_in{q}") for q in range(LB)]
        lo_used = sem("lo_used")
        sj_onehots = sem("sj_onehots")
        sj_done = sem("sj_done")
        vals_ready = sem("vals_ready")
        vals_turned = sem("vals_turned")
        vals_copied = sem("vals_copied")
        line_out = sem("line_out")
        scores_in = sem("scores_in")
        carry_cols = sem("carry_cols")
        carry_turned = sem("carry_turned")
        carry_rows = sem("carry_rows")
        carry_back = sem("carry_back")
        shifted = sem("shifted")
        exp_done = sem("exp_done")
        weights_ready = sem("weights_ready")
        weights_out = sem("weights_out")
        weights_in = sem("weights_in")
        stats_ready = sem("stats_ready")
        stats_out = sem("stats_out")
        node_stats_in = sem("node_stats_in")
        wturned = sem("wturned")
        wcopied = sem("wcopied")
        ea_in = [sem(f"ea_in{q}") for q in range(2)]
        loop_shifted = sem("loop_shifted")
        loop_exp = sem("loop_exp")
        sums_copied = sem("sums_copied")
        sums_turned = sem("sums_turned")
        sumsT_ready = sem("sumsT_ready")
        edge_out_done = sem("edge_out_done")
        out_done = sem("out_done")
        init_out = sem("init_out")
        payload_free = sem("payload_free")
        x_done = sem("x_done")
        empty_ready = sem("empty_ready")

        block = ctx.enter_context(nc.Block())

        nodes_in = [x[0:NFULL * P].rearrange("(b p) d -> p b d", p=P), x[NFULL * P:N]]
        slots_by_tile = slots.rearrange("(r t e) w -> r e t w", t=RB, e=P)
        tab0_rows = tab0.rearrange("n (r d) -> (n r) d", d=D)
        tab0_blocks = tab0.rearrange("(b p) c -> b p c", p=P)
        ring_rows = ring[:].rearrange("p (t c) -> p t c", c=P)

        lines_by_group = line_dram.rearrange("h (g s) -> g h s", g=NG)
        weights_by_group = weight_dram.rearrange("h (g s) -> g h s", g=NG)
        ce_rounds = ce_dram.rearrange("c (r g k e) -> r k c g e", r=NRB, g=RB // G, k=G)
        ce_by_group = ce_dram.rearrange("(l h) (g s) -> l g h s", h=HEADS, g=NG)

        def by_tile(line):
            whole = (NT // P) * P * P
            return (line[0:whole].rearrange("(c t e) -> t c e", t=P, e=P),
                    line[whole:SL].rearrange("(t e) -> t e", e=P))

        def bank(b, rows, cols, start=0):
            return ps[0:rows, b, start:start + cols]

        def acc_all(c0, c1):
            return ps[:, 0:NBANK, 0:PER_BANK * ACC].rearrange("p k (b c) -> p k b c", c=ACC)[:, :, :, c0:c1]

        @block.gpsimd
        def _(pool):
            order = Order(pool, pool_steps)
            nc.gpsimd.iota(iota_row[:], [[1, P]], base=0, channel_multiplier=0,
                           allow_small_or_imprecise_dtypes=True)
            nc.gpsimd.iota(iota_col[:], [[1, 1]], base=0, channel_multiplier=1,
                           allow_small_or_imprecise_dtypes=True)
            nc.gpsimd.iota(spare_row[:], [[P, NB]], base=SL, channel_multiplier=1,
                           allow_small_or_imprecise_dtypes=True)
            nc.gpsimd.memset(ones[:], 1.0)
            nc.gpsimd.memset(ones16[:], 1.0)
            nc.gpsimd.memset(zeros[:], 0.0)
            nc.gpsimd.memset(zeros16[:], 0.0)
            order.step(nc.gpsimd.memset(gate[:], 0))
            nc.gpsimd.memset(empty_slots[:], 0.0)
            nc.gpsimd.memset(x_res[:, NFULL, :], 0.0).then_inc(consts_ready, 1)
            pool.wait_ge(init_out, 48)
            def arrived(semaphore, value):
                pool.wait_ge(semaphore, value)
                order.settle()
                order.step(nc.gpsimd.tensor_tensor(gate[:], gate[:], gate[:], ALU.add))

            with order.loop(GE // BUF3, BUF3) as i:
                for q in range(BUF3):
                    arrived(pos_ready, i * BUF3 + q + 1)
                    for k in range(KE):
                        pool.indirect_dma_start(
                            slots, bass.IndirectOffsetOnAxis(ap=pos[:, q, k:k + 1], axis=0),
                            payload[:, q, k * W_PAY:(k + 1) * W_PAY], None).then_inc(scat[q], 16)
            pool.wait_ge(prep_over, 1)
            nc.gpsimd.iota(iota_tile[:], [[1, NT]], base=0, channel_multiplier=0,
                           allow_small_or_imprecise_dtypes=True).then_inc(tiles_iota, 1)

            def gather(table, width, it):
                for j in range(RING):
                    arrived(staged, it * RING + j + 1)
                    for t in range(j * G, (j + 1) * G):
                        pool.indirect_dma_start(
                            ring_rows[:, t, 0:width], None, table,
                            bass.IndirectOffsetOnAxis(ap=idx_stage[:, t:t + 1], axis=0),
                        ).then_inc(gathered[j], 16)

            pool.wait_ge(tab0_out[0], 16 * ((NB + 1) // 2))
            pool.wait_ge(tab0_out[1], 16 * (NB // 2))
            with order.loop(NIT, RING) as i:
                gather(tab0_rows, D, i)

            with order.loop(LAYERS, 2 + NG + 1) as l:
                arrived(fill_ready, l + 1)
                for b in range(NB):
                    pool.indirect_dma_start(
                        fill_dram, bass.IndirectOffsetOnAxis(ap=start_row[:, b:b + 1], axis=0),
                        node_terms[:, b, :], None).then_inc(fill_out, 16)
                arrived(tab1_out, l * 16 + 16)
                with order.loop(NIT - 1, RING) as i:
                    gather(tab1, HEADS * D, (l + 1) * NIT + i)
                arrived(stats_out, l * 16 + 16)
                for b in range(NB):
                    pool.indirect_dma_start(
                        node_stats[:, b, :], None, stats_dram,
                        bass.IndirectOffsetOnAxis(ap=start_row[:, b:b + 1], axis=0)).then_inc(node_stats_in, 16)
                gather(tab1, HEADS * D, (l + 1) * NIT + NIT - 1)

        @block.sync
        def _(sp):
            sp.dma_start(edge_i[:, 0, :], dst.rearrange("(g k) -> g k", g=GE)).then_inc(edges_in, 16)
            sp.dma_start(edge_i[:, 1, :], src.rearrange("(g k) -> g k", g=GE)).then_inc(edges_in, 16)
            sp.dma_start(edge_i[:, 2, :], edge_type_8.rearrange("(g k) -> g k", g=GE)).then_inc(edges_in, 16)
            sp.dma_start(edge_t[:, 0, :, :].rearrange("g k e -> g (k e)"),
                         edge_weight1.rearrange("(g k) o -> g (k o)", g=GE)).then_inc(edges_in, 16)
            sp.wait_ge(consts_ready, 1)
            sp.dma_start(x_res[:, 0:NFULL, :], nodes_in[0]).then_inc(x_in, 16)
            sp.dma_start(x_res[0:NREST, NFULL, :], nodes_in[1]).then_inc(x_in, 16)
            sp.wait_ge(empty_ready, 1)
            sp.dma_start(slots.rearrange("(p r c) w -> p r (c w)", p=P, c=4),
                         empty_slots[:].rearrange("p c w -> p (c w)").unsqueeze(1)
                         .to_broadcast([P, SL // (4 * P), 4 * W_PAY])).then_inc(init_out, 16)
            sp.dma_start(fill_dram.rearrange("(p r) c -> p (r c)", p=P).rearrange("p (a c) -> p a c", a=4),
                         zeros[:].unsqueeze(1).to_broadcast([P, 4, FR])).then_inc(init_out, 16)
            sp.dma_start(stats_dram[SL:SL + NPAD].rearrange("(p b) c -> p (b c)", p=P),
                         empty_stats[:].rearrange("p b c -> p (b c)")).then_inc(init_out, 16)
            sp.wait_ge(edge_rows_ready, 2)
            sp.dma_start(rows_dram.rearrange("g a k -> g (a k)"),
                         rows16[:].rearrange("g a k -> g (a k)")).then_inc(rows_out, 16)
            sp.wait_ge(rows_out, 16)
            rows_flat = rows_dram.rearrange("g a k -> (g a k)")
            with sp.Fori(0, GE // BUF3) as i:
                for q in range(BUF3):
                    sp.wait_ge(payload_free, i * BUF3 + q + 1)
                    sp.dma_start(row_in[:, q, :, :].rearrange("p a k -> p (a k)"),
                                 rows_flat[bass.ds((i * BUF3 + q) * (2 * KE * TE), 2 * KE * TE)]
                                 .partition_broadcast(P)).then_inc(rows_in[q], 16)
                    sp.dma_start(payload[:, q, :].rearrange("e (k w) -> e k w", w=W_PAY)[:, :, 0:EF],
                                 edge_attr_16.rearrange("(g k e) f -> g e k f", k=KE, e=TE)
                                 [bass.ds(i * BUF3 + q, 1)].rearrange("o e k f -> (o e) k f")
                                 ).then_inc(rows_in[q], 16)
            sp.wait_ge(prep_over, 1)
            sp.dma_start(w_types[:].rearrange("i (r o) -> i r o", r=R),
                         L0_gnn_weight.rearrange("r i o -> i r o")).then_inc(ea_out[0], 16)
            sp.dma_start(w_loop[:], L0_gnn_loop_weight).then_inc(ea_out[1], 16)
            sp.dma_start(bias_types[:], L0_gnn_h_bias.partition_broadcast(P)).then_inc(w0_in, 16)
            with sp.Fori(0, NRB // 2) as i:
                for q in range(2):
                    sp.wait_ge(back_packed, i * 2 + q + 1)
                    sp.wait_ge(ea_out[q], i * 16 + 16)
                    sp.dma_start(back[:, q, :].rearrange("e (t w) -> e t w", w=W_PAY),
                                 slots_by_tile[bass.ds(i * 2 + q, 1)].rearrange("o e t w -> (o e) t w")
                                 ).then_inc(back_in[q], 16)
                    sp.wait_ge(back_packed, i * 2 + q + 3)
                    sp.dma_start(ea_dram[bass.ds(i * 2 + q, 1)].rearrange("o e c -> (o e) c"),
                                 ea_pack[:, q, :]).then_inc(ea_out[q], 16)
            sp.wait_ge(w1_zeroed, 1)
            sp.dma_start(w_ext[:, :, 0:HEADS * D], L1_gnn_weights.rearrange("l i o -> i l o")).then_inc(w1_in, 16)
            sp.dma_start(edge_nat[:], L1_gnn_edge_ws.rearrange("l c f -> c l f")).then_inc(w1_in, 16)
            sp.dma_start(bias_out[:], L1_gnn_biases.rearrange("l c -> (l c)").partition_broadcast(P)).then_inc(w1_in, 16)
            with nc.allow_non_contiguous_dma(reason="small weights, turned"):
                sp.dma_start(edge_bias[:], L1_gnn_edge_bs.rearrange("l c -> c l")).then_inc(w1_in, 16)
                for h in range(HEADS):
                    for side in range(2):
                        sp.dma_start(att[h * D:(h + 1) * D, :, side * HEADS + h],
                                     L1_gnn_atts[:, h, side * D:(side + 1) * D].rearrange("l c -> c l")).then_inc(w1_in, 16)
                    for l in range(LAYERS):
                        sp.dma_start(edge_w[h * EA1:h * EA1 + EF, l, :],
                                     L1_gnn_edge_ws[l, h * D:(h + 1) * D, :].rearrange("c f -> f c")).then_inc(w1_in, 16)
                    sp.dma_start(edge_w[h * EA1 + EF:(h + 1) * EA1, :, :],
                                 L1_gnn_edge_bs[:, h * D:(h + 1) * D].unsqueeze(0)).then_inc(w1_in, 16)
            sp.wait_ge(edge_att_ready, 1)
            for k in range(G):
                sp.dma_start(edge_att8[k * EF:(k + 1) * EF, k, :], edge_att[:]).then_inc(edge_att8_in, 16)
            sp.wait_ge(keys_ready, 1)
            whole, left = by_tile(key_dram[1:SL + 1])
            sp.dma_start(whole, turn[:, 0, 0:NT // P, :]).then_inc(keys_out, 16)
            sp.dma_start(left, turn[0:NT % P, 0, NT // P, :]).then_inc(keys_out, 16)
            sp.dma_start(key_dram[0:1].unsqueeze(0), ends[:, 0:1]).then_inc(keys_out, 16)
            sp.dma_start(key_dram[SL + 1:SL + 2].unsqueeze(0), ends[:, 1:2]).then_inc(keys_out, 16)
            whole, left = by_tile(lo_dram)
            sp.dma_start(whole, lo16[:, 0:NT // P, :]).then_inc(keys_out, 16)
            sp.dma_start(left, lo16[0:NT % P, NT // P, :]).then_inc(keys_out, 16)
            sp.wait_ge(keys_out, 96)
            with nc.allow_non_contiguous_dma(reason="the slots beside each row"):
                sp.dma_start(keys[:, 0:1], key_dram[0:SL].rearrange("(g s) -> g s", g=NG)[:, 0:1]).then_inc(keys_in, 16)
                sp.dma_start(keys[:, 1:GS + 1], key_dram[1:SL + 1].rearrange("(g s) -> g s", g=NG)).then_inc(keys_in, 16)
                sp.dma_start(keys[:, GS + 1:GS + 2],
                             key_dram[2:SL + 2].rearrange("(g s) -> g s", g=NG)[:, GS - 1:GS]).then_inc(keys_in, 16)
            sp.wait_ge(ea_out[0], 16 * (NRB // 2 + 1))
            sp.wait_ge(ea_out[1], 16 * (NRB // 2 + 1))
            with sp.Fori(0, NRB // 2) as i:
                for q in range(2):
                    sp.wait_ge(ce_free, i * 2 + q + 1)
                    sp.dma_start(ea_back[:, q, :],
                                 ea_dram[bass.ds(i * 2 + q, 1)].rearrange("o e c -> (o e) c")).then_inc(ea_back_in[q], 16)
            lo_rows = lo_dram.rearrange("(g s) -> g s", g=NG)
            with sp.Fori(0, LAYERS) as l:
                with sp.Fori(0, NG // LB) as i:
                    for q in range(LB):
                        sp.wait_ge(lo_used, l * NG + i * LB + q + 1)
                        sp.dma_start(lo_in_sb[:, q, :], lo_rows[bass.ds(i * LB + q, 1)].rearrange("o s -> (o s)")
                                     .partition_broadcast(P)).then_inc(lo_in[q], 16)
                for h in range(HEADS):
                    sp.wait_ge(vals_copied, l * HEADS + h + 1)
                    whole, left = by_tile(line_dram[h])
                    sp.dma_start(whole, turn[:, h, 0:NT // P, :]).then_inc(line_out, 16)
                    sp.dma_start(left, turn[0:NT % P, h, NT // P, :]).then_inc(line_out, 16)
                sp.wait_ge(line_out, l * 64 + 64)
                sp.dma_start(scores, lines_by_group).then_inc(scores_in, 16)
                sp.wait_ge(weights_ready, l + 1)
                sp.dma_start(weights_by_group, scores).then_inc(weights_out, 16)
                sp.wait_ge(weights_out, l * 16 + 16)
                for h in range(HEADS):
                    whole, left = by_tile(weight_dram[h])
                    sp.dma_start(turn[:, h, 0:NT // P, :], whole).then_inc(weights_in, 16)
                    sp.dma_start(turn[0:NT % P, h, NT // P, :], left).then_inc(weights_in, 16)
                with sp.Fori(0, NIT) as i:
                    for j in range(RING):
                        sp.wait_ge(sums_ready, (l + 1) * NG + i * RING + j - 1)
                        sp.dma_start(ea_in_sb[:, j % 2, :],
                                     ea_dram[bass.ds(i * 2 + j // 4, 1)].rearrange("o e c -> (o e) c")
                                     [:, (j % 4) * G * EF:(j % 4 + 1) * G * EF]).then_inc(ea_in[j % 2], 16)
            sp.wait_ge(x_done, 1)
            sp.dma_start(out[0:NFULL * P].rearrange("(b p) d -> p b d", p=P), x_res[:, 0:NFULL, :]).then_inc(out_done, 16)
            sp.dma_start(out[NFULL * P:N], x_res[0:NREST, NFULL, :]).then_inc(out_done, 16)
            sp.wait_ge(out_done, 32)

        @block.tensor
        def _(pe):
            order = Order(pe, pe_steps)
            pe.wait_ge(consts_ready, 1)
            pe.wait_ge(edge_cols_ready, 1)
            for k in range(KE):
                if k >= 2:
                    pe.wait_ge(edge_turn_used, k - 1)
                for a in range(6):
                    mm = nc.tensor.transpose(bank(k % 2, TE, GE, a * GE), edge_t[:, a, k, :], ident[0:GE, 0:GE])
                mm.then_inc(edge_turned, 1)
            nc.tensor.matmul(bank(6, P, NB), zeros16[:, 0:P], zeros16[:, 0:NB],
                             start=True, stop=True).then_inc(hist_used, 1)
            with pe.Fori(0, GE // BUF3) as i:
                for q in range(BUF3):
                    pe.wait_ge(hist_onehots, i * BUF3 + q + 1)
                    for k in range(KE):
                        mm = nc.tensor.matmul(bank(6, P, NB), lo_hot[:, q, k, :], hi_hot[:, q, k, :],
                                              start=False, stop=True, skip_group_check=True)
                    mm.then_inc(hist_used, 1)
            pe.wait_ge(hist_read, 1)
            nc.tensor.matmul(bank(7, P, NB), before[:], hist[:], start=True, stop=True)
            nc.tensor.matmul(bank(7, P, NB, 32), ones[:], hist[:], start=True, stop=True).then_inc(prefix_done, 1)
            with pe.Fori(0, GE // BUF3) as i:
                for q in range(BUF3):
                    pe.wait_ge(pos_onehots, i * BUF3 + q + 1)
                    nc.tensor.matmul(bank(q, P, (KE + 1) * NB), zeros16[:, 0:P], zeros16[:, 0:(KE + 1) * NB],
                                     start=True, stop=True)
                    for k in range(KE):
                        mm = nc.tensor.matmul(
                            bank(q, P, (KE - k) * NB, (k + 1) * NB).rearrange("p (a b) -> p a b", b=NB),
                            lo_hot[:, q, k, :], hi_hot[:, q, k:k + 1, :].to_broadcast([TE, KE - k, NB]),
                            start=False, stop=True, skip_group_check=True)
                    mm.then_inc(counts_ready, 1)
                    pe.wait_ge(pos_masks, i * BUF3 + q + 1)
                    for k in range(KE):
                        nc.tensor.matmul(bank(3 + q, TE, 1, KE * NB + k), same[:, q, k, :], ones16[0:TE, :],
                                         start=True, stop=True)
                    pe.wait_ge(snap_ready, i * BUF3 + q + 2)
                    for k in range(KE):
                        mm = nc.tensor.matmul(bank(3 + q, TE, NB, k * NB), lo_hotT[:, q, k, :],
                                              snap[:, q, k, :], start=True, stop=True)
                    mm.then_inc(looked_up, 1)

            def turn_lines(columns, b0, done):
                for c, rows in CHUNKS:
                    mm = nc.tensor.transpose(bank(b0 + c // 4, rows, P, (c % 4) * P), columns[:, c * P:c * P + rows], ident[:])
                mm.then_inc(done, 1)

            def arrived(semaphore, value, b):
                pe.wait_ge(semaphore, value)
                nc.tensor.matmul(bank(b, P, 1), zeros[:, 0:P], zeros[:, 0:1], start=True, stop=True)

            def turn_nodes(base):
                for n, (b0, nb) in enumerate(NODE_BATCHES):
                    if n >= 2:
                        pe.wait_ge(hT_ready, base + n - 1)
                    for b in range(b0, b0 + nb):
                        mm = nc.tensor.transpose(bank(5 + n % 2, D, P, (b - b0) * P), h_sb[:, b, :], ident[:])
                    mm.then_inc(hT_turned, 1)

            pe.wait_ge(prep_over, 1)
            pe.wait_ge(ea_out[0], 16)
            pe.wait_ge(ea_out[1], 16)
            pe.wait_ge(h_ready, 1)
            turn_nodes(0)
            pe.wait_ge(hT_ready, len(NODE_BATCHES))
            for b in range(NB):
                mm = nc.tensor.matmul(bank(b // 8, P, D, (b % 8) * D), hT[:, b * P:(b + 1) * P], w_loop[:],
                                      start=True, stop=True)
            mm.then_inc(loop_done, 1)
            for b in range(NB):
                if b >= 2:
                    pe.wait_ge(tab0_staged, b - 1)
                nc.tensor.matmul(bank(5 + b % 2, P, R * D), hT[:, b * P:(b + 1) * P], w_types[:],
                                 start=True, stop=True).then_inc(proj_done, 1)

            def zero_acc(waits):
                pe.wait_ge(acc_read, waits)
                for k in range(NBANK):
                    mm = nc.tensor.matmul(bank(k, P, PER_BANK * ACC), zeros[:, 0:P], zeros[:, 0:PER_BANK * ACC],
                                          start=True, stop=True)
                mm.then_inc(sums_used, 2)

            def add_up(width, turn, i):
                for j in range(RING):
                    q = j % 2
                    _, offs = nc.values_load_multi_w_load_instructions(
                        tile_off[0:1, bass.ds(i * (RING * G) + j * G, G)], engines=[mybir.EngineType.PE],
                        min_val=0, max_val=(NBANK - 1) * BANK + (PER_BANK - 1) * ACC)
                    pe.wait_ge(sums_ready, turn * RING + j + 1)
                    for u in range(G):
                        mm = nc.tensor.matmul(
                            ps[:].rearrange("p k c -> p (k c)")[:, bass.ds(offs[u], width)],
                            onehot[:, q, u, :], sums_in[:, q, u, 0:width],
                            start=False, stop=True, skip_group_check=True)
                    mm.then_inc(sums_used, 1)

            pe.wait_ge(w1_in, 16 * (4 + 2 * HEADS + HEADS * (LAYERS + 1)))
            pe.wait_ge(tab0_staged, NB)
            for l in range(LAYERS):
                mm = nc.tensor.transpose(bank(5, P, D, l * D), w_ext[:, l, 0:HEADS * D], ident[0:D, 0:D])
            mm.then_inc(w1_turned, 1)
            pe.wait_ge(w1_copied, 1)
            for l in range(LAYERS):
                nc.tensor.matmul(bank(6, D, 2 * HEADS, l * 2 * HEADS), w_turned[:, l, :], att[:, l, :], start=True, stop=True)
                nc.tensor.matmul(bank(6, EF, HEADS, 32 + l * HEADS), edge_nat[:, l, :], att[:, l, HEADS:2 * HEADS],
                                 start=True, stop=True)
                mm = nc.tensor.matmul(bank(6, P, HEADS, 64 + l * HEADS), edge_bias[:, l:l + 1].to_broadcast([P, P]),
                                      att[:, l, HEADS:2 * HEADS], start=True, stop=True)
            mm.then_inc(w1_products, 1)
            pe.wait_ge(acc_read, 1)
            pe.wait_ge(back_packed, NRB + 2)
            turn_lines(pay[:, 1, :], 0, keys_turned)
            turn_lines(pay[:, 2, :], 2, keys_turned)
            pe.wait_ge(edge_att8_in, 16 * G)
            with pe.Fori(0, NRB // 2) as i:
                for q in range(2):
                    pe.wait_ge(ea_back_in[q], i * 16 + 16)
                    for k in range(RB // G):
                        mm = nc.tensor.transpose(bank(4 + q, P, P, k * P), ea_back[:, q, k * P:(k + 1) * P], ident[:])
                    mm.then_inc(ea_back_turned, 1)
                    pe.wait_ge(ea_turned_ready, i * 2 + q + 1)
                    nc.tensor.matmul(bank(6 + q, G * LAYERS * HEADS, BANK),
                                     edge_att8[:].rearrange("p k c -> p (k c)"), ea_turned[:, q, :],
                                     start=True, stop=True).then_inc(ce_done, 1)
            for k in range(2):
                pe.wait_ge(flags_cols, k + 1)
                nc.tensor.transpose(bank(7, 4, P, k * P), carry_col[:, 0:4], ident[:]).then_inc(flags_turned, 1)

            pe.wait_ge(keys_ready, 1)
            pe.wait_ge(ce_ready, NRB)
            zero_acc(1)
            pe.wait_ge(tiles_ready, 1)
            with pe.Fori(0, NIT) as i:
                add_up(D, i, i)

            with pe.Fori(0, LAYERS) as l:
                arrived(h_ready, l + 2, 5)
                for n, (b0, nb) in enumerate(NODE_BATCHES):
                    if n >= 2:
                        arrived(hT_ready, (l + 1) * len(NODE_BATCHES) + n - 1, 5 + n % 2)
                    for b in range(b0, b0 + nb):
                        mm = nc.tensor.transpose(bank(5 + n % 2, D, P, (b - b0) * P), h_sb[:, b, :], ident[:])
                    mm.then_inc(hT_turned, 1)
                arrived(hT_ready, (l + 2) * len(NODE_BATCHES), 0)
                for n in range(XB):
                    if n >= 4:
                        arrived(xt_copied, l * XB + n - 3, n % 4)
                    for b in range(n * 3, min(NB, n * 3 + 3)):
                        mm = nc.tensor.matmul(bank(n % 4, P, XC, (b - n * 3) * XC), hT_l[:, b * P:(b + 1) * P],
                                              w_ext[:, bass.ds(l, 1), :].rearrange("i o c -> i (o c)"),
                                              start=True, stop=True)
                    mm.then_inc(xt_done, 1)
                arrived(s_src_ready, l + 1, 4)
                with pe.Fori(0, NG // LB) as i:
                    for q in range(LB):
                        pe.wait_ge(sj_onehots, l * NG + i * LB + q + 1)
                        for u in range(G):
                            for k in range(3):
                                mm = nc.tensor.matmul(bank(4 + q, P, HEADS * NB, u * HEADS * NB),
                                                      lo_hot_n[:, q, u * P:(u + 1) * P],
                                                      s_src3[:, k, :, :].rearrange("p h b -> p (h b)"),
                                                      start=(k == 0), stop=(k == 2))
                        mm.then_inc(sj_done, 1)
                arrived(vals_ready, l + 1, 0)
                for h in range(HEADS):
                    turn_lines(slot_vals[:, h, :], 2 * h, vals_turned)
                for r in range(5):
                    pe.wait_ge(carry_cols, l * 5 + r + 1)
                    nc.tensor.transpose(bank(7, P, P), carry_col[:], ident[:]).then_inc(carry_turned, 1)
                    pe.wait_ge(carry_rows, l * 5 + r + 1)
                    nc.tensor.transpose(bank(7, P, P, P), carry_row[:], ident[:]).then_inc(carry_back, 1)
                arrived(weights_in, l * 64 + 64, 0)
                for h in range(HEADS):
                    for c, rows in CHUNKS:
                        mm = nc.tensor.transpose(bank(2 * h + c // 4, P, rows, (c % 4) * P), turn[0:rows, h, c, :],
                                                 ident[0:rows, 0:rows])
                    mm.then_inc(wturned, 1)
                arrived(wcopied, l * HEADS + HEADS, 0)
                for k in range(NBANK):
                    nc.tensor.matmul(bank(k, P, PER_BANK * ACC), zeros[:, 0:P], zeros[:, 0:PER_BANK * ACC],
                                     start=True, stop=True)
                with pe.Fori(0, NIT) as i:
                    add_up(ACC, (l + 1) * NIT + i, i)
                for n in range(NB):
                    if n == 0:
                        arrived(sums_copied, l + 1, 5)
                    if n >= 8 and n % 4 == 0:
                        arrived(sumsT_ready, l * SB + n // 4 - 1, 5 + (n // 4) % 2)
                    mm = nc.tensor.transpose(bank(5 + (n // 4) % 2, HEADS * EA1, P, (n % 4) * P),
                                             sums[:, n, D:ACC], ident[:])
                    if n % 4 == 3 or n == NB - 1:
                        mm.then_inc(sums_turned, 1)
                arrived(sumsT_ready, (l + 1) * SB, 0)
                for b in range(NB):
                    mm = nc.tensor.matmul(bank(b // 8, P, D, (b % 8) * D), sumsT[:, b * P:(b + 1) * P],
                                          edge_w[:, bass.ds(l, 1), :].rearrange("k o c -> k (o c)"),
                                          start=True, stop=True)
                mm.then_inc(edge_out_done, 1)

        @block.vector
        def _(dve):
            order = Order(dve, dve_steps)
            V = nc.vector
            V.memset(empty_stats[:, :, 2:4], 0.0)
            V.memset(empty_stats[:, :, 0:2], -BIG)
            dve.wait_ge(consts_ready, 1)
            order.step(V.tensor_scalar(ident[:], iota_row[:], iota_col[:, 0:1], None, ALU.is_equal))
            order.step(V.tensor_scalar(before[:], iota_row[:], iota_col[:, 0:1], None, ALU.is_gt))
            order.link(V.tensor_scalar(before16[:], iota_row[:], iota_col[:, 0:1], None, ALU.is_gt))
            V.memset(empty_slots[:, :, EF + 1:EF + 2], -9999.0).then_inc(empty_ready, 1)
            dve.wait_ge(edges_in, 64)
            order.step(V.tensor_scalar(part_i[:, 0, :], edge_i[:, 0, :], P - 1, None, ALU.bitwise_and))
            order.link(V.tensor_scalar(part_i[:, 1, :], edge_i[:, 0, :], 7, None, ALU.arith_shift_right))
            V.tensor_copy(rows16[:, 0, :], edge_i[:, 0, :]).then_inc(edge_rows_ready, 1)
            V.tensor_copy(rows16[:, 1, :], part_i[:, 0, :]).then_inc(edge_rows_ready, 1)
            V.tensor_copy(edge_t[:, 1:4, :, :].rearrange("g a k e -> g a (k e)"), edge_i[:])
            V.tensor_copy(edge_t[:, 4:6, :, :].rearrange("g a k e -> g a (k e)"), part_i[:]).then_inc(edge_cols_ready, 1)
            for k in range(KE):
                dve.wait_ge(edge_turned, k + 1)
                last = V.tensor_copy(edge_c[:, :, :, k],
                                     bank(k % 2, TE, 6 * GE).rearrange("e (a g) -> e a g", a=6))
                last.then_inc(edge_turn_used, 1)
            dve.wait_ge(edge_turn_used, KE)

            def edge_onehots(g, q):
                V.tensor_tensor(lo_hot[:, q, :, :], iota_row[0:TE, :].unsqueeze(1).to_broadcast([TE, KE, P]),
                                edge_c[:, 4, bass.ds(g, 1), :].rearrange("e o k -> e (o k)")
                                .unsqueeze(2).to_broadcast([TE, KE, P]), ALU.is_equal)
                return V.tensor_tensor(hi_hot[:, q, :, :], iota_row[0:TE, 0:NB].unsqueeze(1).to_broadcast([TE, KE, NB]),
                                       edge_c[:, 5, bass.ds(g, 1), :].rearrange("e o k -> e (o k)")
                                       .unsqueeze(2).to_broadcast([TE, KE, NB]), ALU.is_equal)

            with dve.Fori(0, GE // BUF3) as i:
                for q in range(BUF3):
                    dve.wait_ge(hist_used, i * BUF3 + q + 1)
                    edge_onehots(i * BUF3 + q, q).then_inc(hist_onehots, 1)
            dve.wait_ge(hist_used, GE + 1)
            V.tensor_copy(hist[:], bank(6, P, NB)).then_inc(hist_read, 1)
            dve.wait_ge(prefix_done, 1)
            order.link(V.tensor_scalar(tiles_f[:], bank(7, P, NB, 32), float(P - 1), None, ALU.add))
            order.link(V.tensor_copy(tiles_i[:], tiles_f[:]))
            order.link(V.tensor_scalar(tiles_i[:], tiles_i[:], 7, None, ALU.arith_shift_right))
            order.link(V.tensor_copy(tiles_f[:], tiles_i[:]))
            order.link(V.tensor_tensor_scan(tiles_cum[:], ones[:, 0:NB], tiles_f[:], 0.0, ALU.mult, ALU.add))
            order.link(V.tensor_tensor(tile0[:], tiles_cum[:], tiles_f[:], ALU.subtract))
            order.link(V.scalar_tensor_tensor(out=first[:], in0=tile0[:], scalar=float(P), in1=bank(7, P, NB),
                                              op0=ALU.mult, op1=ALU.add))
            order.step(V.tensor_scalar(has[:], hist[:], 0.0, None, ALU.is_gt))
            order.link(V.tensor_tensor(tiles_cum[:], first[:], spare_row[:], ALU.subtract))
            order.link(V.tensor_tensor(tiles_cum[:], tiles_cum[:], has[:], ALU.mult))
            order.link(V.tensor_tensor(start_row[:], tiles_cum[:], spare_row[:], ALU.add))
            V.tensor_copy(snap[:, BUF3 - 1, KE, :], first[:]).then_inc(snap_ready, 1)
            with order.loop(GE // BUF3, 3 * BUF3) as i:
                for q in range(BUF3):
                    g = i * BUF3 + q
                    prev = (q - 1) % BUF3
                    edge_onehots(g, q).then_inc(pos_onehots, 1)
                    dve.wait_ge(rows_in[q], i * 32 + 32)
                    V.tensor_scalar(lo_hotT[:, q, :, :].rearrange("p k e -> p (k e)"), row_in[:, q, 1, :],
                                    iota_col[:, 0:1], None, ALU.is_equal)
                    order.link(V.tensor_tensor(same[:, q, :, :],
                                               row_in[0:TE, q, 0, :].rearrange("p (k e) -> p k e", e=TE),
                                               edge_c[:, 1, bass.ds(g, 1), :].rearrange("e o k -> e (o k)")
                                               .unsqueeze(2).to_broadcast([TE, KE, TE]), ALU.is_equal))
                    V.tensor_tensor(same[:, q, :, :], same[:, q, :, :],
                                    before16[0:TE, 0:TE].unsqueeze(1).to_broadcast([TE, KE, TE]),
                                    ALU.mult).then_inc(pos_masks, 1)
                    V.tensor_copy(payload[:, q, :].rearrange("e (k w) -> e k w", w=W_PAY)[:, :, EF:W_PAY],
                                  edge_c[:, 0:4, bass.ds(g, 1), :].rearrange("e a o k -> e (o k) a"))
                    dve.wait_ge(counts_ready, g + 1)
                    dve.wait_ge(snap_ready, g + 1)
                    V.tensor_tensor(snap[:, q, :, :], bank(q, P, (KE + 1) * NB).rearrange("p (k b) -> p k b", b=NB),
                                    snap[:, prev, KE:KE + 1, :].to_broadcast([P, KE + 1, NB]),
                                    ALU.add).then_inc(snap_ready, 1)
                    dve.wait_ge(looked_up, g + 1)
                    order.link(V.tensor_tensor(picked[:], bank(3 + q, TE, KE * NB).rearrange("e (k b) -> e k b", b=NB),
                                               hi_hot[:, q, :, :], ALU.mult))
                    order.link(V.tensor_reduce(base_at[:], picked[:], AX, ALU.add))
                    V.tensor_tensor(pos[:, q, :], base_at[:], bank(3 + q, TE, KE, KE * NB),
                                    ALU.add).then_inc(pos_ready, 1)

            for q in range(BUF3):
                dve.wait_ge(scat[q], GE // BUF3 * 16 * KE)
            order.link(V.memset(gate2[:], 0.0))
            V.memset(gate2[:], 0.0).then_inc(prep_over, 1)
            dve.wait_ge(prep_over, 1)
            V.memset(edge_att8[:], 0.0)
            V.memset(att[:], 0.0).then_inc(w1_zeroed, 1)

            def layernorm(x_sums, h_out, n):
                order.link(V.tensor_reduce(mean[:], x_sums[:], AX, ALU.add))
                order.link(V.tensor_scalar(mean[:], mean[:], -1.0 / D, None, ALU.mult))
                order.link(V.tensor_tensor(centred[:], x_sums[:], mean[:].unsqueeze(2).to_broadcast([P, NB, D]), ALU.add))
                order.link(V.tensor_tensor(h_out[:], centred[:], centred[:], ALU.mult))
                order.link(V.tensor_reduce(var[:], h_out[:], AX, ALU.add))
                V.tensor_scalar(var[:], var[:], 1.0 / D, LN_EPS, ALU.mult, ALU.add).then_inc(var_ready, 1)
                dve.wait_ge(std_ready, n)
                order.link(V.reciprocal(var[:], var[:]))
                order.link(V.tensor_tensor(centred[:], centred[:], var[:].unsqueeze(2).to_broadcast([P, NB, D]), ALU.mult))
                last = V.tensor_scalar(h_out[:], centred[:], 0.0, None, ALU.max)
                if n == 1:
                    last.then_inc(h_ready, 1)
                else:
                    order.link(last)

            dve.wait_ge(x_in, 32)
            layernorm(x_res, h_sb, 1)
            for n, (b0, nb) in enumerate(NODE_BATCHES):
                dve.wait_ge(hT_turned, n + 1)
                V.tensor_copy(hT[:, b0 * P:(b0 + nb) * P], bank(5 + n % 2, D, nb * P)).then_inc(hT_ready, 1)
            dve.wait_ge(loop_done, 1)
            V.tensor_tensor(x_res[:].rearrange("p b d -> p (b d)"), x_res[:].rearrange("p b d -> p (b d)"),
                            ps[:].rearrange("p k c -> p (k c)")[:, 0:NB * D], ALU.add).then_inc(acc_read, 1)
            dve.wait_ge(w0_in, 16)
            for b in range(NB):
                dve.wait_ge(proj_done, b + 1)
                if b >= 2:
                    dve.wait_ge(tab0_out[b % 2], 16 * (b // 2))
                V.tensor_tensor(tab0_sb[:, b % 2, :].rearrange("p (r d) -> p r d", d=D),
                                bank(5 + b % 2, P, R * D).rearrange("p (r d) -> p r d", d=D),
                                bias_types[:].unsqueeze(1).to_broadcast([P, R, D]), ALU.add).then_inc(tab0_staged, 1)
            V.memset(gate2[:], 0.0).then_inc(back_packed, 2)
            with dve.Fori(0, NRB // 2) as i:
                for q in range(2):
                    dve.wait_ge(back_in[q], i * 16 + 16)
                    rows = back[:, q, :].rearrange("e (t w) -> e t w", w=W_PAY)
                    V.tensor_copy(pay[:, :, bass.ds((i * 2 + q) * RB, RB)].rearrange("e a t -> e t a"), rows[:, :, EF:W_PAY])
                    V.tensor_copy(ea_pack[:, q, :].rearrange("e (t f) -> e t f", f=EF), rows[:, :, 0:EF]).then_inc(back_packed, 1)
            dve.wait_ge(back_packed, NRB + 2)
            order.step(V.scalar_tensor_tensor(out=idx0_f[:], in0=pay[:, 2, :], scalar=float(R), in1=pay[:, 3, :],
                                              op0=ALU.mult, op1=ALU.add))
            order.step(V.tensor_copy(idx[:, 0:NT], pay[:, 2, :]))
            order.step(V.tensor_copy(idx[:, NT:], pay[:, 2, 0:RING * G]))
            order.link(V.tensor_copy(idx0[:, NT:], pay[:, 2, 0:RING * G]))
            order.link(V.tensor_copy(idx0[:, 0:NT], idx0_f[:]))
            V.tensor_copy(idx_stage[:], idx0[:, 0:RING * G]).then_inc(staged, RING)
            dve.wait_ge(tiles_iota, 1)
            order.link(V.tensor_scalar(blk[:], iota_tile[:], tile0[:, 1:2], None, ALU.is_ge))
            for b in range(2, NB):
                order.link(V.scalar_tensor_tensor(out=blk[:], in0=iota_tile[:], scalar=tile0[:, b:b + 1], in1=blk[:],
                                                  op0=ALU.is_ge, op1=ALU.add))
            order.step(V.scalar_tensor_tensor(out=rel[:], in0=blk[:], scalar=-float(P), in1=pay[:, 1, :],
                                              op0=ALU.mult, op1=ALU.add))
            order.link(V.tensor_scalar(off_f[:, 0, :], blk[0:1, :], float(PER_BANK), None, ALU.is_ge))
            for k in range(2, NBANK):
                order.link(V.scalar_tensor_tensor(out=off_f[:, 0, :], in0=blk[0:1, :], scalar=float(PER_BANK * k),
                                                  in1=off_f[:, 0, :], op0=ALU.is_ge, op1=ALU.add))
            order.link(V.tensor_scalar(off_f[:, 0, :], off_f[:, 0, :], float(BANK - PER_BANK * ACC), None, ALU.mult))
            order.link(V.scalar_tensor_tensor(out=off_f[:, 1, :], in0=blk[0:1, :], scalar=float(ACC),
                                              in1=off_f[:, 0, :], op0=ALU.mult, op1=ALU.add))
            V.tensor_copy(tile_off[:], off_f[:, 1, :]).then_inc(tiles_ready, 1)

            dve.wait_ge(w1_turned, 1)
            V.tensor_copy(w_turned[:].rearrange("p l d -> p (l d)"), bank(5, P, LAYERS * D)).then_inc(w1_copied, 1)
            dve.wait_ge(w1_products, 1)
            V.tensor_copy(w_ext[:, :, HEADS * D:XC], bank(6, D, LAYERS * 2 * HEADS).rearrange("p (l c) -> p l c", l=LAYERS))
            V.tensor_copy(att_bias[:].rearrange("p l h -> p (l h)"), bank(6, P, LAYERS * HEADS, 64))
            V.tensor_copy(edge_att[:], bank(6, EF, LAYERS * HEADS, 32)).then_inc(edge_att_ready, 1)
            order.step(V.memset(ends[:], -1.0))
            order.link(V.tensor_scalar(hi_i[:], idx[:, 0:NT], 7, None, ALU.arith_shift_right))
            order.step(V.tensor_copy(src_hi[:], hi_i[:]))
            dve.wait_ge(keys_turned, 2)
            cols = [ps[:, b:b + 2, :].rearrange("p k c -> p (k c)").rearrange("p (c e) -> p c e", e=P) for b in (0, 2)]
            for n, (c0, c1, rows) in enumerate(((0, NT // P, P), (NT // P, TC, NT % P))):
                order.step(V.tensor_copy(turn[0:rows, 0, c0:c1, :], cols[0][0:rows, c0:c1, :]))
                order.step(V.tensor_copy(lo_i[0:rows, c0:c1, :], cols[1][0:rows, c0:c1, :]))
            order.settle()
            for n, (c0, c1, rows) in enumerate(((0, NT // P, P), (NT // P, TC, NT % P))):
                order.link(V.tensor_scalar(lo_i[0:rows, c0:c1, :], lo_i[0:rows, c0:c1, :], P - 1, None, ALU.bitwise_and))
                order.link(V.tensor_copy(lo16[0:rows, c0:c1, :], lo_i[0:rows, c0:c1, :]))
            V.memset(gate2[:], 0.0).then_inc(keys_ready, 1)
            dve.wait_ge(keys_ready, 1)
            V.memset(gate2[:], 0.0).then_inc(ce_free, 2)
            with dve.Fori(0, NRB // 2) as i:
                for q in range(2):
                    dve.wait_ge(ea_back_turned, i * 2 + q + 1)
                    V.tensor_copy(ea_turned[:, q, :], bank(4 + q, P, BANK)).then_inc(ea_turned_ready, 1)
                    dve.wait_ge(ce_done, i * 2 + q + 1)
                    V.tensor_copy(ce_sb[:, q, :], bank(6 + q, G * LAYERS * HEADS, BANK)).then_inc(ce_ready, 1)
            dve.wait_ge(keys_in, 48)
            mine = keys[:, 1:GS + 1]
            order.step(V.tensor_tensor(keep[:], mine, keys[:, 0:GS], ALU.is_equal))
            order.step(V.tensor_tensor(keep_back[:], mine, keys[:, 2:GS + 2], ALU.is_equal))
            order.step(V.tensor_tensor(last_slot[:], mine, keys[:, 2:GS + 2], ALU.not_equal))
            order.settle()
            order.step(V.tensor_scalar(keep_neg[:], keep[:], -1.0, BIG, ALU.add, ALU.mult))
            order.step(V.tensor_tensor_scan(head_run[:], keep[:], keep[:], 1.0, ALU.mult, ALU.mult))
            order.step(V.tensor_tensor_scan(tail_run[:, ::-1], keep_back[:, ::-1], keep_back[:, ::-1], 1.0, ALU.mult, ALU.mult))
            order.step(V.memset(carry_row[:], 0.0))
            order.link(V.memset(carry_col[:], 0.0))
            order.step(V.tensor_scalar(head_neg[:], head_run[:], -1.0, BIG, ALU.add, ALU.mult))
            for k, flags in enumerate((head_run[:, GS - 1:GS], tail_run[:, 0:1])):
                V.tensor_copy(carry_col[0:NG, 0:4], flags.to_broadcast([NG, 4])).then_inc(flags_cols, 1)
                dve.wait_ge(flags_turned, k + 1)
                order.link(V.tensor_copy(row_flags[0:4, 2 * k, :], bank(7, 4, P, k * P)))
            order.link(V.tensor_scalar(row_flags[0:4, 1, :], row_flags[0:4, 0, :], -1.0, BIG, ALU.add, ALU.mult))

            with dve.Fori(0, NIT) as i:
                for j in range(RING):
                    q = j % 2
                    t0 = i * (RING * G) + j * G
                    dve.wait_ge(sums_used, i * RING + j + 1)
                    V.tensor_tensor(onehot[:, q, :, :], iota_row[:].unsqueeze(1).to_broadcast([P, G, P]),
                                    rel[:, bass.ds(t0, G)].unsqueeze(2).to_broadcast([P, G, P]), ALU.is_equal)
                    dve.wait_ge(gathered[j], i * (16 * G) + 16 * G)
                    V.tensor_tensor(sums_in[:, q, :, 0:D], ring_rows[:, j * G:(j + 1) * G, 0:D],
                                    pay[:, 0, bass.ds(t0, G)].unsqueeze(2).to_broadcast([P, G, D]),
                                    ALU.mult).then_inc(sums_ready, 1)
                    V.tensor_copy(idx_stage[:, j * G:(j + 1) * G],
                                  idx0[:, bass.ds(t0 + RING * G, G)]).then_inc(staged, 1)
            dve.wait_ge(sums_used, NG + 2)
            order.link(V.tensor_copy(centred[:].rearrange("p (k b) d -> p k b d", b=PER_BANK), acc_all(0, D)))
            order.link(V.tensor_tensor(x_res[:], x_res[:], centred[:], ALU.add))
            layernorm(x_res, h_sb, 2)
            V.memset(gate2[:], 0.0).then_inc(lo_used, LB)

            def carry(columns, n, flags, backward, nothing, r, l):
                V.tensor_copy(carry_col[0:NG, 0:n], columns).then_inc(carry_cols, 1)
                dve.wait_ge(carry_turned, l * 5 + r + 1)
                rows = bank(7, n, NG)
                if backward:
                    order.step(V.memset(carry_row[0:n, NG - 1:NG], nothing))
                    order.link(V.tensor_tensor_scan(carry_row[0:n, 0:NG - 1][:, ::-1], row_flags[0:n, flags, 1:NG][:, ::-1],
                                                    rows[:, 1:NG][:, ::-1], nothing, ALU.mult, ALU.add))
                else:
                    ops = (ALU.add, ALU.max) if nothing else (ALU.mult, ALU.add)
                    order.step(V.memset(carry_row[0:n, 0:1], nothing))
                    order.link(V.tensor_tensor_scan(carry_row[0:n, 1:NG], row_flags[0:n, flags, 0:NG - 1],
                                                    rows[:, 0:NG - 1], nothing, *ops))
                V.memset(gate2[:], 0.0).then_inc(carry_rows, 1)
                dve.wait_ge(carry_back, l * 5 + r + 1)
                order.link(V.tensor_copy(carry_in[0:NG, 0:n], bank(7, NG, n, P)))

            def spread_back(values, spread, r, l):
                order.link(V.tensor_tensor(values, values, last_slot[:].unsqueeze(1).to_broadcast([NG, HEADS, GS]), ALU.mult))
                for h in range(HEADS):
                    order.step(V.tensor_tensor_scan(spread[:, h, ::-1], keep_back[:, ::-1], values[:, h, ::-1], 0.0,
                                                    ALU.mult, ALU.add))
                order.settle()
                carry(spread[:, :, 0], HEADS, 2, True, 0.0, r, l)
                for h in range(HEADS):
                    order.step(V.scalar_tensor_tensor(out=spread[:, h, :], in0=tail_run[:], scalar=carry_in[0:NG, h:h + 1],
                                                      in1=spread[:, h, :], op0=ALU.mult, op1=ALU.add))
                order.settle()

            with order.loop(LAYERS, PER_LAYER) as l:
                V.tensor_scalar(h_sb[:], h_sb[:], 0.0, None, ALU.max).then_inc(h_ready, 1)
                for n, (b0, nb) in enumerate(NODE_BATCHES):
                    dve.wait_ge(hT_turned, (l + 1) * len(NODE_BATCHES) + n + 1)
                    V.tensor_copy(hT_l[:, b0 * P:(b0 + nb) * P], bank(5 + n % 2, D, nb * P)).then_inc(hT_ready, 1)
                for n in range(XB):
                    nb = min(NB, n * 3 + 3) - n * 3
                    dve.wait_ge(xt_done, l * XB + n + 1)
                    V.tensor_copy(xt_sb[:, n * 3:n * 3 + nb, :].rearrange("p b c -> p (b c)"),
                                  bank(n % 4, P, nb * XC)).then_inc(xt_copied, 1)
                dve.wait_ge(xt_copied, l * XB + XB)
                at_dst, at_src = xt_sb[:, :, HEADS * D:HEADS * D + HEADS], xt_sb[:, :, HEADS * D + HEADS:XC]
                order.link(V.tensor_tensor(node_terms[:, :, 0:HEADS], at_dst,
                                           att_bias[:, bass.ds(l, 1), :].to_broadcast([P, NB, HEADS]), ALU.add))
                order.link(V.tensor_tensor(loop_w[:, 0, :, :], node_terms[:, :, 0:HEADS], at_src, ALU.add))
                V.scalar_tensor_tensor(out=node_terms[:, :, HEADS:], in0=loop_w[:, 0, :, :], scalar=NEG_SLOPE,
                                       in1=loop_w[:, 0, :, :], op0=ALU.mult, op1=ALU.max).then_inc(fill_ready, 1)
                at_src_t = at_src.rearrange("p b h -> p h b")
                order.link(V.tensor_copy(s_src3[:, 0, :, :], at_src_t))
                order.link(V.tensor_tensor(s_src[:, 0, :, :], at_src_t, s_src3[:, 0, :, :], ALU.subtract))
                order.link(V.tensor_copy(s_src3[:, 1, :, :], s_src[:, 0, :, :]))
                order.link(V.tensor_tensor(s_src[:, 1, :, :], s_src[:, 0, :, :], s_src3[:, 1, :, :], ALU.subtract))
                V.tensor_copy(s_src3[:, 2, :, :], s_src[:, 1, :, :]).then_inc(s_src_ready, 1)
                with order.loop(NG // LB, LB + 2) as i:
                    for q in range(LB):
                        dve.wait_ge(lo_in[q], l * (16 * (NG // LB)) + i * 16 + 16)
                        V.tensor_scalar(lo_hot_n[:, q, :], lo_in_sb[:, q, :], iota_col[:, 0:1], None,
                                        ALU.is_equal).then_inc(lo_used, 1)
                        V.tensor_tensor(hi_hot_n[:, q, :, :], iota_row[:, 0:NB].unsqueeze(1).to_broadcast([P, G, NB]),
                                        src_hi[:, bass.ds(i * (LB * G) + q * G, G)].unsqueeze(2).to_broadcast([P, G, NB]),
                                        ALU.is_equal).then_inc(sj_onehots, 1)
                    for q in range(LB):
                        dve.wait_ge(sj_done, l * NG + i * LB + q + 1)
                        order.step(V.tensor_tensor(
                            sj_picked[:, q, :, :, :],
                            bank(4 + q, P, G * HEADS * NB).rearrange("p (u h b) -> p u h b", u=G, h=HEADS),
                            hi_hot_n[:, q, :, :].unsqueeze(2).to_broadcast([P, G, HEADS, NB]), ALU.mult))
                    order.settle()
                    order.link(V.tensor_reduce(sj_part[:].rearrange("p h t -> p t h"),
                                               sj_picked.rearrange("p q u h b -> p (q u) h b"), AX, ALU.add))
                    order.step(V.tensor_scalar(slot_vals[:, :, bass.ds(i * (LB * G), LB * G)], sj_part[:], 0.0, None, ALU.add))
                order.settle()
                V.memset(gate2[:], 0.0).then_inc(vals_ready, 1)
                for h in range(HEADS):
                    dve.wait_ge(vals_turned, l * HEADS + h + 1)
                    rows_of = ps[:, 2 * h:2 * h + 2, :].rearrange("p k c -> p (k c)").rearrange("p (c e) -> p c e", e=P)
                    order.step(V.tensor_copy(turn[:, h, 0:NT // P, :], rows_of[:, 0:NT // P, :]))
                    V.tensor_copy(turn[0:NT % P, h, NT // P:, :], rows_of[0:NT % P, NT // P:TC, :]).then_inc(vals_copied, 1)

                dve.wait_ge(fill_in, l * 16 + 16)
                terms = filled[0:NG]
                for c in range(4):
                    order.step(V.tensor_tensor_scan(terms[:, :, c], keep[:], terms[:, :, c], 0.0, ALU.mult, ALU.add))
                order.settle()
                carry(terms[:, GS - 1, :], 4, 0, False, 0.0, 0, l)
                for c in range(4):
                    order.step(V.scalar_tensor_tensor(out=terms[:, :, c], in0=head_run[:], scalar=carry_in[0:NG, c:c + 1],
                                                      in1=terms[:, :, c], op0=ALU.mult, op1=ALU.add))
                order.settle()
                dve.wait_ge(scores_in, l * 16 + 16)
                dve.wait_ge(edge_terms_in, l * 16 + 16)
                order.link(V.tensor_tensor(scores, scores, edge_terms[:], ALU.add))
                order.link(V.tensor_tensor(scores, scores, terms[:, :, 0:HEADS].rearrange("g s h -> g h s"), ALU.add))
                order.link(V.scalar_tensor_tensor(out=scores, in0=scores, scalar=NEG_SLOPE, in1=scores,
                                                  op0=ALU.mult, op1=ALU.max))
                loops = terms[:, :, HEADS:].rearrange("g s h -> g h s")
                order.link(V.tensor_tensor(running, scores, loops, ALU.max))
                for h in range(HEADS):
                    order.step(V.tensor_tensor_scan(running[:, h, :], keep_neg[:], running[:, h, :], -BIG, ALU.add, ALU.max))
                order.settle()
                carry(running[:, :, GS - 1], HEADS, 1, False, -BIG, 1, l)
                for h in range(HEADS):
                    order.step(V.scalar_tensor_tensor(out=running[:, h, :], in0=head_neg[:], scalar=carry_in[0:NG, h:h + 1],
                                                      in1=running[:, h, :], op0=ALU.add, op1=ALU.max))
                order.settle()
                spread_back(running, total, 2, l)
                order.step(V.tensor_tensor(scores, scores, total, ALU.subtract))
                order.link(V.tensor_tensor(running, loops, total, ALU.subtract))
                V.memset(gate2[:], 0.0).then_inc(shifted, 1)
                order.link(V.tensor_copy(terms[:, :, 0:HEADS].rearrange("g s h -> g h s"), total))
                dve.wait_ge(exp_done, l + 1)
                for h in range(HEADS):
                    order.step(V.tensor_tensor_scan(edge_terms[:, h, :], keep[:], scores[:, h, :], 0.0, ALU.mult, ALU.add))
                order.settle()
                carry(edge_terms[:, :, GS - 1], HEADS, 0, False, 0.0, 3, l)
                for h in range(HEADS):
                    order.step(V.scalar_tensor_tensor(out=edge_terms[:, h, :], in0=head_run[:], scalar=carry_in[0:NG, h:h + 1],
                                                      in1=edge_terms[:, h, :], op0=ALU.mult, op1=ALU.add))
                order.settle()
                spread_back(edge_terms[:], total, 4, l)
                order.link(V.scalar_tensor_tensor(out=running, in0=running, scalar=1e-16, in1=total, op0=ALU.add, op1=ALU.add))
                order.link(V.reciprocal(running, running))
                V.tensor_tensor(scores, scores, running, ALU.mult).then_inc(weights_ready, 1)
                V.tensor_copy(terms[:, :, HEADS:].rearrange("g s h -> g h s"), total).then_inc(stats_ready, 1)
                for h in range(HEADS):
                    dve.wait_ge(wturned, l * HEADS + h + 1)
                    V.tensor_copy(slot_vals[:, h, :], ps[:, 2 * h:2 * h + 2, :].rearrange("p k c -> p (k c)")[:, 0:NT]
                                  ).then_inc(wcopied, 1)
                with order.loop(NIT, RING) as i:
                    for j in range(RING):
                        q = j % 2
                        t0 = i * (RING * G) + j * G
                        w = slot_vals[:, :, bass.ds(t0, G)].rearrange("p h t -> p t h")
                        if j == 0:
                            dve.wait_ge(wcopied, l * HEADS + HEADS)
                        dve.wait_ge(sums_used, (l + 1) * NG + i * RING + j + 1)
                        dve.wait_ge(gathered[j], l * (16 * G * NIT) + i * (16 * G) + 16 * G * (NIT + 1))
                        order.step(V.tensor_tensor(
                            weighted[:, q], ring_rows[:, j * G:(j + 1) * G, :].rearrange("p t (h d) -> p t h d", h=HEADS),
                            w.unsqueeze(3).to_broadcast([P, G, HEADS, D]), ALU.mult))
                        V.tensor_tensor(onehot[:, q, :, :], iota_row[:].unsqueeze(1).to_broadcast([P, G, P]),
                                        rel[:, bass.ds(t0, G)].unsqueeze(2).to_broadcast([P, G, P]), ALU.is_equal)
                        dve.wait_ge(ea_in[q], l * (16 * NG // 2) + i * (16 * RING // 2) + 16 * (j // 2 + 1))
                        edge_sums = sums_in[:, q, :, D:ACC].rearrange("p t (h f) -> p t h f", h=HEADS)
                        V.tensor_tensor(edge_sums[:, :, :, 0:EF],
                                        ea_in_sb[:, q, :].rearrange("p (t f) -> p t f", t=G).unsqueeze(2)
                                        .to_broadcast([P, G, HEADS, EF]),
                                        w.unsqueeze(3).to_broadcast([P, G, HEADS, EF]), ALU.mult)
                        V.tensor_copy(edge_sums[:, :, :, EF], w)
                        order.settle()
                        V.tensor_tensor(sums_in[:, q, :, 0:D], weighted[:, q, :, 0, :], weighted[:, q, :, 1, :],
                                        ALU.add).then_inc(sums_ready, 1)
                        V.tensor_copy(idx_stage[:, j * G:(j + 1) * G],
                                      idx[:, bass.ds(t0 + RING * G, G)]).then_inc(staged, 1)
                dve.wait_ge(sums_used, (l + 1) * NG + NG + 2)
                order.link(V.tensor_copy(sums.rearrange("p (k b) c -> p k b c", b=PER_BANK), acc_all(0, ACC)))
                dve.wait_ge(node_stats_in, l * (16 * NB) + 16 * NB)
                order.link(V.tensor_tensor(loop_w[:, 0, :, :], node_stats[:, :, 0:HEADS], node_terms[:, :, HEADS:], ALU.max))
                V.tensor_tensor(loop_w[:, 1, :, :], node_terms[:, :, HEADS:], loop_w[:, 0, :, :],
                                ALU.subtract).then_inc(loop_shifted, 1)
                dve.wait_ge(loop_exp, l + 1)
                order.link(V.scalar_tensor_tensor(out=loop_w[:, 3, :, :], in0=loop_w[:, 2, :, :], scalar=1e-16,
                                                  in1=node_stats[:, :, HEADS:], op0=ALU.add, op1=ALU.add))
                order.link(V.reciprocal(loop_w[:, 3, :, :], loop_w[:, 3, :, :]))
                order.link(V.tensor_tensor(loop_w[:, 1, :, :], loop_w[:, 2, :, :], loop_w[:, 3, :, :], ALU.mult))
                weight_sums = sums[:, :, D:ACC].rearrange("p b (h f) -> p b h f", h=HEADS)[:, :, :, EF]
                V.tensor_tensor(weight_sums, weight_sums, loop_w[:, 1, :, :], ALU.add).then_inc(sums_copied, 1)
                for n, (b0, nb) in enumerate(NODE_BATCHES):
                    dve.wait_ge(sums_turned, l * SB + n + 1)
                    V.tensor_copy(sumsT[:, b0 * P:(b0 + nb) * P], bank(5 + n % 2, HEADS * EA1, nb * P)).then_inc(sumsT_ready, 1)
                for h in range(HEADS):
                    order.link(V.tensor_tensor(tmp_nodes, xt_sb[:, :, h * D:(h + 1) * D],
                                               loop_w[:, 1, :, h:h + 1].to_broadcast([P, NB, D]), ALU.mult))
                    order.link(V.tensor_tensor(sums[:, :, 0:D], sums[:, :, 0:D], tmp_nodes, ALU.add))
                dve.wait_ge(edge_out_done, l + 1)
                order.link(V.tensor_tensor(tmp_nodes, ps[:].rearrange("p k c -> p (k c)")[:, 0:NB * D]
                                           .rearrange("p (b d) -> p b d", d=D), sums[:, :, 0:D], ALU.add))
                order.link(V.scalar_tensor_tensor(out=h_sb[:], in0=tmp_nodes, scalar=1.0 / HEADS,
                                                  in1=bias_out[:, bass.ds(l, 1), :].to_broadcast([P, NB, D]),
                                                  op0=ALU.mult, op1=ALU.add))
            V.tensor_tensor(x_res[:], x_res[:], h_sb[:], ALU.add).then_inc(x_done, 1)

        @block.scalar
        def _(act):
            order = Order(act, act_steps)
            act.wait_ge(consts_ready, 1)
            order.link(nc.scalar.copy(gate_act[:, 0:1], ones[:, 0:1]))
            nc.scalar.copy(gate_act[:, 1:2], gate_act[:, 0:1]).then_inc(payload_free, BUF3)
            with act.Fori(0, GE // BUF3) as i:
                for q in range(BUF3):
                    act.wait_ge(payload_free, i * BUF3 + q + BUF3)
                    act.wait_ge(scat[q], i * (16 * KE) + 16 * KE)
                    nc.scalar.copy(gate_act[:, 1:2], gate_act[:, 0:1]).then_inc(payload_free, 1)
            act.wait_ge(var_ready, 1)
            nc.scalar.activation(var[:], var[:], ACT.Sqrt).then_inc(std_ready, 1)
            for b in range(NB):
                act.wait_ge(tab0_staged, b + 1)
                act.dma_start(tab0_blocks[b], tab0_sb[:, b % 2, :]).then_inc(tab0_out[b % 2], 16)
            with act.Fori(0, NRB // 2) as i:
                for q in range(2):
                    act.wait_ge(ce_ready, i * 2 + q + 1)
                    for k in range(G):
                        act.dma_start(ce_rounds[bass.ds(i * 2 + q, 1), k].rearrange("o c g e -> (o c) g e"),
                                      ce_sb[k * LAYERS * HEADS:(k + 1) * LAYERS * HEADS, q, :]
                                      .rearrange("c (g e) -> c g e", e=P)).then_inc(ce_out[q], 16)
                    act.wait_ge(ce_free, i * 2 + q + 2)
                    act.wait_ge(ce_out[q], i * (16 * G) + 16 * G)
                    nc.scalar.copy(gate_act[:, 1:2], gate_act[:, 0:1]).then_inc(ce_free, 1)
            act.wait_ge(var_ready, 2)
            nc.scalar.activation(var[:], var[:], ACT.Sqrt).then_inc(std_ready, 1)

            def arrived(semaphore, value):
                act.wait_ge(semaphore, value)
                order.settle()
                order.step(nc.scalar.copy(gate_act[:, 1:2], gate_act[:, 0:1]))

            with order.loop(LAYERS, 2) as l:
                act.wait_ge(xt_copied, l * XB + XB)
                act.dma_start(tab1.rearrange("(b p) c -> p b c", p=P), xt_sb[:, :, 0:HEADS * D]).then_inc(tab1_out, 16)
                act.dma_start(edge_terms[:], ce_by_group[bass.ds(l, 1)].rearrange("o g h s -> (o g) h s")
                              ).then_inc(edge_terms_in, 16)
                act.wait_ge(fill_out, l * (16 * NB) + 16 * NB)
                act.dma_start(filled[0:NG].rearrange("g s c -> g (s c)"),
                              fill_dram[0:SL].rearrange("(g s) c -> g (s c)", g=NG)).then_inc(fill_in, 16)
                arrived(shifted, l + 1)
                nc.scalar.activation(scores, scores, ACT.Exp)
                nc.scalar.activation(running, running, ACT.Exp).then_inc(exp_done, 1)
                act.wait_ge(stats_ready, l + 1)
                act.dma_start(stats_dram[0:SL].rearrange("(g s) c -> g (s c)", g=NG),
                              filled[0:NG].rearrange("g s c -> g (s c)")).then_inc(stats_out, 16)
                arrived(loop_shifted, l + 1)
                nc.scalar.activation(loop_w[:, 2, :, :], loop_w[:, 1, :, :], ACT.Exp).then_inc(loop_exp, 1)


_OUTS = [((N, D), "float32")]
_INS = ["x", "src", "dst", "edge_attr_16", "edge_type_8", "edge_weight1", "L0_gnn_weight", "L0_gnn_h_bias",
        "L0_gnn_loop_weight", "L1_gnn_weights", "L1_gnn_biases", "L1_gnn_edge_ws", "L1_gnn_edge_bs", "L1_gnn_atts"]


def kernel(**inputs):
    import numpy as _np
    import concourse.bacc as _bacc
    from concourse import mybir as _mybir
    from concourse.bass_utils import run_bass_kernel_spmd as _run

    nc = _bacc.Bacc("TRN2", target_bir_lowering=False, num_devices=1)
    arrays, args = {}, []
    for name in _INS:
        a = _np.ascontiguousarray(inputs[name])
        arrays[f"in_{name}_dram"] = a
        args.append(nc.dram_tensor(f"in_{name}_dram", a.shape, _mybir.dt.from_np(a.dtype), kind="ExternalInput").ap())
    for i, (shape, dtype) in enumerate(_OUTS):
        dt = _mybir.dt.from_np(_np.dtype(dtype))
        args.append(nc.dram_tensor(f"out_{i}_dram", shape, dt, kind="ExternalOutput").ap())
    build_gnn(nc, *args)
    r = _run(nc, [arrays], core_ids=[0])
    return r.results[0]["out_0_dram"]
```

```python
from contextlib import ExitStack, contextmanager

import concourse.bass as bass
from concourse import mybir

ALU = mybir.AluOpType
ACT = mybir.ActivationFunctionType
AX = mybir.AxisListType.X
F32 = mybir.dt.float32
BF16 = mybir.dt.bfloat16
I32 = mybir.dt.int32
U16 = mybir.dt.uint16

P = 128
N, D = 3125, 64
NB = (N + P - 1) // P
NPAD = NB * P
NFULL = N // P
NREST = N - NFULL * P
E = 103125
R = 8
EF = 16
LAYERS, HEADS = 5, 2
NEG_SLOPE = 0.2
LN_EPS = 1e-5
BIG = 1e30

TE, KE = 125, 11
GE = E // (TE * KE)
BUF3 = 3
assert GE * TE * KE == E and GE % BUF3 == 0

G = 8
NG = 104
NT = NG * G
SL = NT * P
GS = G * P
assert NT >= (E + (P - 1) * NB) // P + 1
RING = 13
TURN = 2 * RING
NIT = NG // TURN
assert NIT * TURN == NG
RB = NG // 2
NRB = NT // RB
W_PAY = EF + 4
ACC = 98
PER_BANK = 5
BANK = 512
NBANK = NB // PER_BANK
EA1 = EF + 1
XC = HEADS * D + 2 * HEADS
LB = 8
LH = LB // 2
PER_LAYER = 220
FILL_ROWS = SL // P // 16
XB = (NB + 2) // 3
SB = (NB + 3) // 4
TC = (NT + P - 1) // P
CHUNKS = [(c, min(P, NT - c * P)) for c in range(TC)]
NODE_BATCHES = [(b, min(4, NB - b)) for b in range(0, NB, 4)]


class Order:

    def __init__(self, eng, sem):
        self.eng, self.sem, self.base, self.n = eng, sem, 0, 0

    def step(self, ins):
        self.n += 1
        ins.then_inc(self.sem, 1)

    def settle(self):
        self.eng.wait_ge(self.sem, self.base + self.n)

    def link(self, ins):
        self.step(ins)
        self.settle()

    @contextmanager
    def loop(self, count, per):
        base, n = self.base, self.n
        with self.eng.Fori(0, count) as i:
            self.base, self.n = base + n + i * per, 0
            yield i
            assert self.n == per, (self.n, per)
        self.base, self.n = base, n + count * per


def build_gnn(nc, x, src, dst, edge_attr_16, edge_type_8, edge_weight1, L0_gnn_weight, L0_gnn_h_bias,
              L0_gnn_loop_weight, L1_gnn_weights, L1_gnn_biases, L1_gnn_edge_ws, L1_gnn_edge_bs, L1_gnn_atts, out):
    def dram(name, shape, dt=F32):
        return nc.dram_tensor(name, shape, dt, kind="Internal").ap()

    rows_dram = dram("rows_dram", [GE, 2, TE * KE], U16)
    slots = dram("slots", [SL, W_PAY])
    fill_dram = dram("fill_dram", [SL + NPAD, 4])
    stats_dram = dram("stats_dram", [SL + NPAD, 4])
    ea_dram = dram("ea_dram", [P, NT * EF])
    ce_dram = dram("ce_dram", [LAYERS, P, HEADS * NT])
    lohot_dram = dram("lohot_dram", [NG, P, GS], BF16)
    hihot_dram = dram("hihot_dram", [NG, P, G * NB], BF16)
    lo_dram = dram("lo_dram", [SL], BF16)
    tab0 = dram("tab0", [NPAD, R * D])
    tab1 = dram("tab1", [NPAD, HEADS * D])

    with ExitStack() as ctx:
        def sb(name, shape, dt=F32, where=ctx):
            return where.enter_context(nc.sbuf_tensor(name, shape, dt))

        def sem(name):
            return ctx.enter_context(nc.semaphore(name))

        ps = ctx.enter_context(nc.psum_tensor("ps", [P, 8, BANK], F32))

        ident = sb("ident", [P, P])
        iota_row = sb("iota_row", [P, P])
        iota_col = sb("iota_col", [P, 1])
        before = sb("before", [P, P])
        ones = sb("ones", [P, P])
        zeros = sb("zeros", [P, BANK])
        gate = sb("gate", [P, 1], I32)
        gate2 = sb("gate2", [P, 1])
        gate_act = sb("gate_act", [P, 2])

        x_res = sb("x_res", [P, NB, D])
        h_sb = sb("h_sb", [P, NB, D])
        start_row = sb("start_row", [P, NB], I32)
        rel = sb("rel", [P, NT])
        idx = sb("idx", [P, NT + RING * G], I32)
        tile_off = sb("tile_off", [1, NT], I32)
        tile0 = sb("tile0", [P, NB])
        mean = sb("mean", [P, NB])
        var = sb("var", [P, NB])
        w_ext = sb("w_ext", [D, LAYERS, XC])
        edge_w = sb("edge_w", [HEADS * EA1, LAYERS, D])
        bias_out = sb("bias_out", [P, LAYERS, D])
        att_bias = sb("att_bias", [P, LAYERS, HEADS])
        src_hi = sb("src_hi", [P, NT])

        with ExitStack() as prep:
            edge_i = sb("edge_i", [GE, 3, KE * TE], I32, prep)
            edge_t = sb("edge_t", [GE, 6, KE, TE], F32, prep)
            part_i = sb("part_i", [GE, 2, KE * TE], I32, prep)
            rows16 = sb("rows16", [GE, 2, KE * TE], U16, prep)
            edge_c = sb("edge_c", [TE, 6, GE, KE], F32, prep)
            lo_hot = sb("lo_hot", [TE, BUF3, KE, P], BF16, prep)
            hi_hot = sb("hi_hot", [TE, BUF3, KE, NB], BF16, prep)
            row_in = sb("row_in", [P, BUF3, 2, KE * TE], U16, prep)
            lo_hotT = sb("lo_hotT", [P, BUF3, KE, TE], F32, prep)
            same = sb("same", [TE, BUF3, KE, TE], BF16, prep)
            payload = sb("payload", [TE, BUF3, KE * W_PAY], F32, prep)
            snap = sb("snap", [P, BUF3, KE + 1, NB], F32, prep)
            picked = sb("picked", [TE, KE, NB], F32, prep)
            base_at = sb("base_at", [TE, KE], F32, prep)
            pos = sb("pos", [TE, BUF3, KE], I32, prep)
            hist = sb("hist", [P, NB], F32, prep)
            tiles_i = sb("tiles_i", [P, NB], I32, prep)
            tiles_f = sb("tiles_f", [P, NB], F32, prep)
            tiles_cum = sb("tiles_cum", [P, NB], F32, prep)
            first = sb("first", [P, NB], F32, prep)
            has = sb("has", [P, NB], F32, prep)
            spare_row = sb("spare_row", [P, NB], F32, prep)
            before16 = sb("before16", [P, P], BF16, prep)
            ones16 = sb("ones16", [P, 1], BF16, prep)
            zeros16 = sb("zeros16", [P, BANK], BF16, prep)
            empty_slots = sb("empty_slots", [P, 4, W_PAY], F32, prep)
            empty_fill = sb("empty_fill", [P, FILL_ROWS, 4], F32, prep)
            empty_stats = sb("empty_stats", [P, NB, 4], F32, prep)

        idx_stage = sb("idx_stage", [P, RING * G], I32)
        ring = sb("ring", [P, RING * G * P])
        hT = ring[0:D, 0:NPAD]
        tab0_sb = ring[:, NPAD:NPAD + 2 * R * D].rearrange("p (q c) -> p q c", q=2)
        back = ring[:, NPAD + 2 * R * D:NPAD + 2 * R * D + 2 * RB * W_PAY].rearrange("p (q c) -> p q c", q=2)
        onehot = sb("onehot", [P, 2, G, P])
        ea_in_sb = sb("ea_in_sb", [P, 2, G * EF])
        lo_hot_n = sb("lo_hot_n", [P, LB, GS], BF16)
        hi_hot_n = sb("hi_hot_n", [P, LB, G * NB], BF16)
        sums_in = sb("sums_in", [P, 2, G, ACC])
        keep = sb("keep", [NG, GS], BF16)
        keep_neg = sb("keep_neg", [NG, GS], BF16)
        keep_back_neg = sb("keep_back_neg", [NG, GS], BF16)
        head_run = sb("head_run", [NG, GS], BF16)
        head_neg = sb("head_neg", [NG, GS], BF16)
        tail_neg = sb("tail_neg", [NG, GS], BF16)
        row_flags = sb("row_flags", [P, 3, P])
        carry_row = sb("carry_row", [P, P])
        carry_col = sb("carry_col", [P, P])
        carry_in = sb("carry_in", [P, 4])
        with ExitStack() as zero:
            pay = sb("pay", [P, 4, NT], F32, zero)
            idx0 = sb("idx0", [P, NT + RING * G], I32, zero)
            w_loop = sb("w_loop", [D, D], F32, zero)
            bias_types = sb("bias_types", [P, D], F32, zero)
            centred = sb("centred", [P, NB, D], F32, zero)
            w_turned = sb("w_turned", [P, LAYERS, D], F32, zero)
            att = sb("att", [P, LAYERS, 2 * HEADS], F32, zero)
            edge_nat = sb("edge_nat", [P, LAYERS, EF], F32, zero)
            edge_bias = sb("edge_bias", [P, LAYERS], F32, zero)
            edge_att = sb("edge_att", [EF, LAYERS * HEADS], F32, zero)
            edge_att8 = sb("edge_att8", [P, G, LAYERS * HEADS], F32, zero)
            with ExitStack() as early:
                iota_tile = sb("iota_tile", [P, NT], F32, early)
                blk = sb("blk", [P, NT], F32, early)
                idx0_f = sb("idx0_f", [P, NT], F32, early)
                off_f = sb("off_f", [1, 2, NT], F32, early)
                ea_pack = sb("ea_pack", [P, 2, RB * EF], F32, early)
                w_types = sb("w_types", [D, R * D], F32, early)
                keys = sb("keys", [NG, GS + 2], F32, early)
                keep_back = sb("keep_back", [NG, GS], BF16, early)
                tail_run = sb("tail_run", [NG, GS], BF16, early)
                lo_i = sb("lo_i", [P, TC, P], I32, early)
                hi_i = sb("hi_i", [P, NT], I32, early)
                lo16 = sb("lo16", [P, TC, P], BF16, early)
            ea_turned = sb("ea_turned", [P, 2, P], F32, zero)
            ce_sb = sb("ce_sb", [P, LAYERS * HEADS, NT], F32, zero)
            lo_in_sb = sb("lo_in_sb", [P, 2, GS], BF16, zero)
        with ExitStack() as zero:
            scores_all = sb("scores_all", [P, HEADS, GS], F32, zero)
            filled = sb("filled", [P, GS, 4], F32, zero)
            run_total = sb("run_total", [P, 2, HEADS, GS], F32, zero)
            xt_sb = sb("xt_sb", [P, NB, XC], F32, zero)
            node_terms = sb("node_terms", [P, NB, 4], F32, zero)
            node_stats = sb("node_stats", [P, NB, 4], F32, zero)
            loop_w = sb("loop_w", [P, 4, NB, HEADS], F32, zero)
            s_src = sb("s_src", [P, 2, HEADS, NB], F32, zero)
            s_src3 = sb("s_src3", [P, 3, HEADS, NB], BF16, zero)
            sj_part = sb("sj_part", [P, HEADS, LH * G], F32, zero)
            slot_vals = sb("slot_vals", [P, HEADS, NT], F32, zero)
            weighted = sb("weighted", [P, 2, G, HEADS, D], F32, zero)
            sj_picked = weighted[:].rearrange("p q t h d -> p (q t h d)")[:, 0:LH * G * HEADS * NB].rearrange(
                "p (q u h b) -> p q u h b", q=LH, u=G, h=HEADS)
        sums = filled[:].rearrange("p s c -> p (s c)")[:, 0:NB * ACC].rearrange("p (b c) -> p b c", c=ACC)
        scores = scores_all[0:NG]
        tmp_nodes = scores_all[:].rearrange("p h s -> p (h s)")[:, 0:NB * D].rearrange("p (b d) -> p b d", d=D)
        running, total = run_total[0:NG, 0], run_total[0:NG, 1]
        run_flat = run_total[:].rearrange("p a h s -> p (a h s)")[:, 0:NPAD]
        hT_l, sumsT = run_flat[0:D], run_flat[0:HEADS * EA1]

        consts_ready = sem("consts_ready")
        dve_steps = sem("dve_steps")
        act_steps = sem("act_steps")
        pe_steps = sem("pe_steps")
        pool_steps = sem("pool_steps")
        prep_over = sem("prep_over")
        slots_tiled = sem("slots_tiled")
        edges_in = sem("edges_in")
        x_in = sem("x_in")
        rows_out = sem("rows_out")
        edge_rows_ready = sem("edge_rows_ready")
        edge_cols_ready = sem("edge_cols_ready")
        edge_turned = sem("edge_turned")
        edge_turn_used = sem("edge_turn_used")
        hist_onehots = sem("hist_onehots")
        hist_used = sem("hist_used")
        hist_read = sem("hist_read")
        prefix_done = sem("prefix_done")
        scat = [sem(f"scat{q}") for q in range(BUF3)]
        rows_in = [sem(f"rows_in{q}") for q in range(BUF3)]
        pos_onehots = sem("pos_onehots")
        pos_masks = sem("pos_masks")
        counts_ready = sem("counts_ready")
        snap_ready = sem("snap_ready")
        looked_up = sem("looked_up")
        pos_ready = sem("pos_ready")
        back_in = [sem(f"back_in{q}") for q in range(2)]
        back_used = sem("back_used")
        ea_out = [sem(f"ea_out{q}") for q in range(2)]
        staged = sem("staged")
        gathered = [sem(f"gathered{j}") for j in range(RING)]
        sums_ready = sem("sums_ready")
        sums_used = sem("sums_used")
        hT_turned = sem("hT_turned")
        hT_ready = sem("hT_ready")
        w0_in = sem("w0_in")
        h_ready = sem("h_ready")
        loop_done = sem("loop_done")
        acc_read = sem("acc_read")
        back_packed = sem("back_packed")
        row_cols_ready = sem("row_cols_ready")
        tiles_ready = sem("tiles_ready")
        tiles_iota = sem("tiles_iota")
        proj_done = sem("proj_done")
        tab0_out = [sem(f"tab0_out{q}") for q in range(2)]
        tab0_staged = sem("tab0_staged")
        off_ready = sem("off_ready")
        var_ready = sem("var_ready")
        std_ready = sem("std_ready")
        w1_in = sem("w1_in")
        w1_zeroed = sem("w1_zeroed")
        w1_turned = sem("w1_turned")
        w1_copied = sem("w1_copied")
        w1_products = sem("w1_products")
        edge_att_ready = sem("edge_att_ready")
        edge_att8_in = sem("edge_att8_in")
        ea_back_turned = sem("ea_back_turned")
        ea_turned_ready = sem("ea_turned_ready")
        ce_done = sem("ce_done")
        ce_filled = sem("ce_filled")
        ce_out = sem("ce_out")
        ce_in = sem("ce_in")
        ea_used = sem("ea_used")
        lo_in = [sem(f"lo_in{q}") for q in range(2)]
        hots_made = sem("hots_made")
        hots_out = [sem(f"hots_out{q}") for q in range(2)]
        hots_in = [sem(f"hots_in{q}") for q in range(LB // 2)]
        dens_ready = sem("dens_ready")
        keys_turned = sem("keys_turned")
        keys_ready = sem("keys_ready")
        keys_out = sem("keys_out")
        keys_in = sem("keys_in")
        flags_cols = sem("flags_cols")
        flags_turned = sem("flags_turned")
        xt_done = sem("xt_done")
        xt_copied = sem("xt_copied")
        tab1_out = sem("tab1_out")
        fill_ready = sem("fill_ready")
        fill_out = sem("fill_out")
        fill_in = sem("fill_in")
        s_src_ready = sem("s_src_ready")
        sj_done = sem("sj_done")
        sj_read = sem("sj_read")
        vals_ready = sem("vals_ready")
        vals_turned = sem("vals_turned")
        carry_cols = sem("carry_cols")
        carry_turned = sem("carry_turned")
        carry_rows = sem("carry_rows")
        carry_back = sem("carry_back")
        shifted = sem("shifted")
        exp_done = sem("exp_done")
        weights_ready = sem("weights_ready")
        stats_ready = sem("stats_ready")
        stats_out = sem("stats_out")
        node_stats_in = sem("node_stats_in")
        wturned = sem("wturned")
        wcopied = sem("wcopied")
        ea_in = [sem(f"ea_in{q}") for q in range(2)]
        loop_shifted = sem("loop_shifted")
        loop_exp = sem("loop_exp")
        sums_copied = sem("sums_copied")
        sums_turned = sem("sums_turned")
        sumsT_ready = sem("sumsT_ready")
        edge_out_done = sem("edge_out_done")
        out_done = sem("out_done")
        init_out = sem("init_out")
        payload_free = sem("payload_free")
        x_done = sem("x_done")
        empty_ready = sem("empty_ready")

        block = ctx.enter_context(nc.Block())

        nodes_in = [x[0:NFULL * P].rearrange("(b p) d -> p b d", p=P), x[NFULL * P:N]]
        slots_by_tile = slots.rearrange("(v g u e) w -> u v e g w", v=2, u=G, e=P)
        tab0_rows = tab0.rearrange("n (r d) -> (n r) d", d=D)
        tab0_blocks = tab0.rearrange("(b p) c -> b p c", p=P)
        ring_rows = ring[:].rearrange("p (t c) -> p t c", c=P)

        def by_tile(line):
            whole = (NT // P) * P * P
            return (line[0:whole].rearrange("(c t e) -> t c e", t=P, e=P),
                    line[whole:SL].rearrange("(t e) -> t e", e=P))

        def bank(b, rows, cols, start=0):
            return ps[0:rows, b, start:start + cols]

        def acc_all(c0, c1):
            return ps[:, 0:NBANK, 0:PER_BANK * ACC].rearrange("p k (b c) -> p k b c", c=ACC)[:, :, :, c0:c1]

        @block.gpsimd
        def _(pool):
            order = Order(pool, pool_steps)
            nc.gpsimd.iota(iota_row[:], [[1, P]], base=0, channel_multiplier=0,
                           allow_small_or_imprecise_dtypes=True)
            nc.gpsimd.iota(iota_col[:], [[1, 1]], base=0, channel_multiplier=1,
                           allow_small_or_imprecise_dtypes=True)
            nc.gpsimd.iota(spare_row[:], [[P, NB]], base=SL, channel_multiplier=1,
                           allow_small_or_imprecise_dtypes=True)
            nc.gpsimd.memset(ones[:], 1.0)
            nc.gpsimd.memset(ones16[:], 1.0)
            nc.gpsimd.memset(zeros[:], 0.0)
            nc.gpsimd.memset(zeros16[:], 0.0)
            order.step(nc.gpsimd.memset(gate[:], 0))
            nc.gpsimd.memset(empty_slots[:], 0.0)
            nc.gpsimd.memset(x_res[:, NFULL, :], 0.0).then_inc(consts_ready, 1)
            pool.wait_ge(init_out, 48)
            def arrived(semaphore, value):
                pool.wait_ge(semaphore, value)
                order.settle()
                order.step(nc.gpsimd.tensor_tensor(gate[:], gate[:], gate[:], ALU.add))

            with order.loop(GE // BUF3, BUF3) as i:
                for q in range(BUF3):
                    arrived(pos_ready, i * BUF3 + q + 1)
                    for k in range(KE):
                        pool.indirect_dma_start(
                            slots, bass.IndirectOffsetOnAxis(ap=pos[:, q, k:k + 1], axis=0),
                            payload[:, q, k * W_PAY:(k + 1) * W_PAY], None).then_inc(scat[q], 16)
            pool.wait_ge(prep_over, 1)
            nc.gpsimd.iota(iota_tile[:], [[1, G], [G, NG]], base=0, channel_multiplier=0,
                           allow_small_or_imprecise_dtypes=True).then_inc(tiles_iota, 1)

            def gather(table, width, it):
                for j in range(TURN):
                    arrived(staged, it * TURN + j + 1)
                    for t in range(j % RING * G, (j % RING + 1) * G):
                        pool.indirect_dma_start(
                            ring_rows[:, t, 0:width], None, table,
                            bass.IndirectOffsetOnAxis(ap=idx_stage[:, t:t + 1], axis=0),
                        ).then_inc(gathered[j % RING], 16)

            pool.wait_ge(tab0_out[0], 16 * ((NB + 1) // 2))
            pool.wait_ge(tab0_out[1], 16 * (NB // 2))
            with order.loop(NIT, TURN) as i:
                gather(tab0_rows, D, i)

            with order.loop(LAYERS, 2 + NG + 1) as l:
                arrived(fill_ready, l + 1)
                for b in range(NB):
                    pool.indirect_dma_start(
                        fill_dram, bass.IndirectOffsetOnAxis(ap=start_row[:, b:b + 1], axis=0),
                        node_terms[:, b, :], None).then_inc(fill_out, 16)
                arrived(tab1_out, l * 16 + 16)
                with order.loop(NIT - 1, TURN) as i:
                    gather(tab1, HEADS * D, (l + 1) * NIT + i)
                arrived(stats_out, l * 16 + 16)
                for b in range(NB):
                    pool.indirect_dma_start(
                        node_stats[:, b, :], None, stats_dram,
                        bass.IndirectOffsetOnAxis(ap=start_row[:, b:b + 1], axis=0)).then_inc(node_stats_in, 16)
                gather(tab1, HEADS * D, (l + 1) * NIT + NIT - 1)

        @block.sync
        def _(sp):
            sp.dma_start(edge_i[:, 0, :], dst.rearrange("(g k) -> g k", g=GE)).then_inc(edges_in, 16)
            sp.dma_start(edge_i[:, 1, :], src.rearrange("(g k) -> g k", g=GE)).then_inc(edges_in, 16)
            sp.dma_start(edge_i[:, 2, :], edge_type_8.rearrange("(g k) -> g k", g=GE)).then_inc(edges_in, 16)
            sp.dma_start(edge_t[:, 0, :, :].rearrange("g k e -> g (k e)"),
                         edge_weight1.rearrange("(g k) o -> g (k o)", g=GE)).then_inc(edges_in, 16)
            sp.wait_ge(consts_ready, 1)
            sp.dma_start(x_res[:, 0:NFULL, :], nodes_in[0]).then_inc(x_in, 16)
            sp.dma_start(x_res[0:NREST, NFULL, :], nodes_in[1]).then_inc(x_in, 16)
            sp.wait_ge(empty_ready, 1)
            sp.dma_start(slots.rearrange("(p r c) w -> p r (c w)", p=P, c=4),
                         empty_slots[:].rearrange("p c w -> p (c w)").unsqueeze(1)
                         .to_broadcast([P, SL // (4 * P), 4 * W_PAY])).then_inc(init_out, 16)
            sp.dma_start(fill_dram[0:SL].rearrange("(p a r) c -> p a (r c)", p=P, r=FILL_ROWS),
                         empty_fill[:].rearrange("p r c -> p (r c)").unsqueeze(1)
                         .to_broadcast([P, SL // P // FILL_ROWS, FILL_ROWS * 4])).then_inc(init_out, 16)
            sp.dma_start(stats_dram[SL:SL + NPAD].rearrange("(p b) c -> p (b c)", p=P),
                         empty_stats[:].rearrange("p b c -> p (b c)")).then_inc(init_out, 16)
            sp.wait_ge(edge_rows_ready, 2)
            sp.dma_start(rows_dram.rearrange("g a k -> g (a k)"),
                         rows16[:].rearrange("g a k -> g (a k)")).then_inc(rows_out, 16)
            sp.wait_ge(rows_out, 16)
            rows_flat = rows_dram.rearrange("g a k -> (g a k)")
            with sp.Fori(0, GE // BUF3) as i:
                for q in range(BUF3):
                    sp.wait_ge(payload_free, i * BUF3 + q + 1)
                    sp.dma_start(row_in[:, q, :, :].rearrange("p a k -> p (a k)"),
                                 rows_flat[bass.ds((i * BUF3 + q) * (2 * KE * TE), 2 * KE * TE)]
                                 .partition_broadcast(P)).then_inc(rows_in[q], 16)
                    sp.dma_start(payload[:, q, :].rearrange("e (k w) -> e k w", w=W_PAY)[:, :, 0:EF],
                                 edge_attr_16.rearrange("(g k e) f -> g e k f", k=KE, e=TE)
                                 [bass.ds(i * BUF3 + q, 1)].rearrange("o e k f -> (o e) k f")
                                 ).then_inc(rows_in[q], 16)
            sp.wait_ge(prep_over, 1)
            sp.dma_start(w_types[:].rearrange("i (r o) -> i r o", r=R),
                         L0_gnn_weight.rearrange("r i o -> i r o")).then_inc(ea_out[0], 16)
            sp.dma_start(w_loop[:], L0_gnn_loop_weight).then_inc(ea_out[1], 16)
            sp.dma_start(bias_types[:], L0_gnn_h_bias.partition_broadcast(P)).then_inc(w0_in, 16)
            with sp.Fori(0, NRB // 2) as i:
                for q in range(2):
                    sp.wait_ge(back_packed, i * 2 + q + 1)
                    sp.wait_ge(ea_out[q], i * 16 + 16)
                    sp.dma_start(back[:, q, :].rearrange("e (t w) -> e t w", w=W_PAY),
                                 slots_by_tile[bass.ds(i, 1), q].rearrange("o e t w -> (o e) t w")
                                 ).then_inc(back_in[q], 16)
                    sp.wait_ge(back_packed, i * 2 + q + 3)
                    sp.dma_start(ea_dram[:, bass.ds((i * 2 + q) * (RB * EF), RB * EF)],
                                 ea_pack[:, q, :]).then_inc(ea_out[q], 16)
            sp.wait_ge(w1_zeroed, 1)
            sp.dma_start(w_ext[:, :, 0:HEADS * D], L1_gnn_weights.rearrange("l i o -> i l o")).then_inc(w1_in, 16)
            sp.dma_start(edge_nat[:], L1_gnn_edge_ws.rearrange("l c f -> c l f")).then_inc(w1_in, 16)
            sp.dma_start(bias_out[:], L1_gnn_biases.rearrange("l c -> (l c)").partition_broadcast(P)).then_inc(w1_in, 16)
            with nc.allow_non_contiguous_dma(reason="small weights, turned"):
                sp.dma_start(edge_bias[:], L1_gnn_edge_bs.rearrange("l c -> c l")).then_inc(w1_in, 16)
                for h in range(HEADS):
                    for side in range(2):
                        sp.dma_start(att[h * D:(h + 1) * D, :, side * HEADS + h],
                                     L1_gnn_atts[:, h, side * D:(side + 1) * D].rearrange("l c -> c l")).then_inc(w1_in, 16)
                    for l in range(LAYERS):
                        sp.dma_start(edge_w[h * EA1:h * EA1 + EF, l, :],
                                     L1_gnn_edge_ws[l, h * D:(h + 1) * D, :].rearrange("c f -> f c")).then_inc(w1_in, 16)
                    sp.dma_start(edge_w[h * EA1 + EF:(h + 1) * EA1, :, :],
                                 L1_gnn_edge_bs[:, h * D:(h + 1) * D].unsqueeze(0)).then_inc(w1_in, 16)
            sp.wait_ge(edge_att_ready, 1)
            for k in range(G):
                sp.dma_start(edge_att8[k * EF:(k + 1) * EF, k, :], edge_att[:]).then_inc(edge_att8_in, 16)
            sp.wait_ge(keys_ready, 1)
            whole, left = by_tile(lo_dram)
            sp.dma_start(whole, lo16[:, 0:NT // P, :]).then_inc(keys_out, 16)
            sp.dma_start(left, lo16[0:NT % P, NT // P, :]).then_inc(keys_out, 16)
            with nc.allow_non_contiguous_dma(reason="the slots beside each row"):
                sp.dma_start(keys[1:NG, 0:1], keys[0:NG - 1, GS:GS + 1]).then_inc(keys_in, 16)
                sp.dma_start(keys[0:NG - 1, GS + 1:GS + 2], keys[1:NG, 1:2]).then_inc(keys_in, 16)

            def load_features(turns, i, j):
                sp.wait_ge(ea_used, turns * TURN + j + 1)
                sp.dma_start(ea_in_sb[:, j % 2, :],
                             ea_dram[:, bass.ds(i * (TURN * G * EF) + j * G * EF, G * EF)]).then_inc(ea_in[j % 2], 16)

            lo_rows = lo_dram.rearrange("(g s) -> g s", g=NG)
            sp.wait_ge(keys_out, 32)
            sp.wait_ge(ea_out[0], 16 * (NRB // 2 + 1))
            sp.wait_ge(ea_out[1], 16 * (NRB // 2 + 1))
            with sp.Fori(0, NIT) as i:
                for j in range(TURN):
                    sp.wait_ge(hots_made, i * TURN + j + 1)
                    sp.dma_start(lo_in_sb[:, j % 2, :], lo_rows[bass.ds(i * TURN + j, 1)].rearrange("o s -> (o s)")
                                 .partition_broadcast(P)).then_inc(lo_in[j % 2], 16)
                    load_features(i, i, j)
            sp.wait_ge(hots_out[0], 16 + 32 * (NG // 2))
            sp.wait_ge(hots_out[1], 16 + 32 * (NG // 2))
            with sp.Fori(0, LAYERS) as l:
                with sp.Fori(0, NG // LB) as i:
                    for q in range(LB // 2):
                        sp.wait_ge(sj_read, l * NG + i * LB + 2 * q + 2)
                        pair = slice(2 * q, 2 * q + 2)
                        sp.dma_start(lo_hot_n[:, pair, :],
                                     lohot_dram[bass.ds(i * LB + 2 * q, 2)].rearrange("g p s -> p g s")
                                     ).then_inc(hots_in[q], 16)
                        sp.dma_start(hi_hot_n[:, pair, :],
                                     hihot_dram[bass.ds(i * LB + 2 * q, 2)].rearrange("g p s -> p g s")
                                     ).then_inc(hots_in[q], 16)
                with sp.Fori(0, NIT) as i:
                    for j in range(TURN):
                        load_features((l + 1) * NIT + i, i, j)
            sp.wait_ge(x_done, 1)
            sp.dma_start(out[0:NFULL * P].rearrange("(b p) d -> p b d", p=P), x_res[:, 0:NFULL, :]).then_inc(out_done, 16)
            sp.dma_start(out[NFULL * P:N], x_res[0:NREST, NFULL, :]).then_inc(out_done, 16)
            sp.wait_ge(out_done, 32)

        @block.tensor
        def _(pe):
            order = Order(pe, pe_steps)
            pe.wait_ge(consts_ready, 1)
            pe.wait_ge(edge_cols_ready, 1)
            for k in range(KE):
                if k >= 2:
                    pe.wait_ge(edge_turn_used, k - 1)
                for a in range(6):
                    mm = nc.tensor.transpose(bank(k % 2, TE, GE, a * GE), edge_t[:, a, k, :], ident[0:GE, 0:GE])
                mm.then_inc(edge_turned, 1)
            nc.tensor.matmul(bank(6, P, NB), zeros16[:, 0:P], zeros16[:, 0:NB],
                             start=True, stop=True).then_inc(hist_used, 1)
            with pe.Fori(0, GE // BUF3) as i:
                for q in range(BUF3):
                    pe.wait_ge(hist_onehots, i * BUF3 + q + 1)
                    for k in range(KE):
                        mm = nc.tensor.matmul(bank(6, P, NB), lo_hot[:, q, k, :], hi_hot[:, q, k, :],
                                              start=False, stop=True, skip_group_check=True)
                    mm.then_inc(hist_used, 1)
            pe.wait_ge(hist_read, 1)
            nc.tensor.matmul(bank(7, P, NB), before[:], hist[:], start=True, stop=True)
            nc.tensor.matmul(bank(7, P, NB, 32), ones[:], hist[:], start=True, stop=True).then_inc(prefix_done, 1)
            with pe.Fori(0, GE // BUF3) as i:
                for q in range(BUF3):
                    pe.wait_ge(pos_onehots, i * BUF3 + q + 1)
                    nc.tensor.matmul(bank(q, P, (KE + 1) * NB), zeros16[:, 0:P], zeros16[:, 0:(KE + 1) * NB],
                                     start=True, stop=True)
                    for k in range(KE):
                        mm = nc.tensor.matmul(
                            bank(q, P, (KE - k) * NB, (k + 1) * NB).rearrange("p (a b) -> p a b", b=NB),
                            lo_hot[:, q, k, :], hi_hot[:, q, k:k + 1, :].to_broadcast([TE, KE - k, NB]),
                            start=False, stop=True, skip_group_check=True)
                    mm.then_inc(counts_ready, 1)
                    pe.wait_ge(pos_masks, i * BUF3 + q + 1)
                    for k in range(KE):
                        nc.tensor.matmul(bank(3 + q, TE, 1, KE * NB + k), same[:, q, k, :], ones16[0:TE, :],
                                         start=True, stop=True)
                    pe.wait_ge(snap_ready, i * BUF3 + q + 2)
                    for k in range(KE):
                        mm = nc.tensor.matmul(bank(3 + q, TE, NB, k * NB), lo_hotT[:, q, k, :],
                                              snap[:, q, k, :], start=True, stop=True)
                    mm.then_inc(looked_up, 1)

            def turn_lines(columns, b0, done):
                for c, rows in CHUNKS:
                    mm = nc.tensor.transpose(bank(b0 + c // 4, rows, P, (c % 4) * P), columns[:, c * P:c * P + rows], ident[:])
                mm.then_inc(done, 1)

            def turn_rows(columns, b0, done):
                for u in range(G):
                    mm = nc.tensor.transpose(bank(b0 + u // 4, NG, P, (u % 4) * P), columns[:, u * NG:(u + 1) * NG], ident[:])
                mm.then_inc(done, 1)

            def arrived(semaphore, value, b):
                pe.wait_ge(semaphore, value)
                nc.tensor.matmul(bank(b, P, 1), zeros[:, 0:P], zeros[:, 0:1], start=True, stop=True)

            def turn_nodes(base):
                for n, (b0, nb) in enumerate(NODE_BATCHES):
                    if n >= 2:
                        pe.wait_ge(hT_ready, base + n - 1)
                    for b in range(b0, b0 + nb):
                        mm = nc.tensor.transpose(bank(5 + n % 2, D, P, (b - b0) * P), h_sb[:, b, :], ident[:])
                    mm.then_inc(hT_turned, 1)

            pe.wait_ge(prep_over, 1)
            pe.wait_ge(ea_out[0], 16)
            pe.wait_ge(ea_out[1], 16)
            pe.wait_ge(h_ready, 1)
            turn_nodes(0)
            pe.wait_ge(hT_ready, len(NODE_BATCHES))
            for b in range(NB):
                mm = nc.tensor.matmul(bank(b // 8, P, D, (b % 8) * D), hT[:, b * P:(b + 1) * P], w_loop[:],
                                      start=True, stop=True)
            mm.then_inc(loop_done, 1)
            for b in range(NB):
                if b >= 2:
                    pe.wait_ge(tab0_staged, b - 1)
                nc.tensor.matmul(bank(5 + b % 2, P, R * D), hT[:, b * P:(b + 1) * P], w_types[:],
                                 start=True, stop=True).then_inc(proj_done, 1)

            def zero_acc(waits):
                pe.wait_ge(acc_read, waits)
                for k in range(NBANK):
                    mm = nc.tensor.matmul(bank(k, P, PER_BANK * ACC), zeros[:, 0:P], zeros[:, 0:PER_BANK * ACC],
                                          start=True, stop=True)
                mm.then_inc(sums_used, 2)

            def edge_products(i, j):
                q = j % 2
                pe.wait_ge(ea_in[q], i * (16 * RING) + (j // 2 + 1) * 16)
                nc.tensor.transpose(bank(5, P, P, q * P), ea_in_sb[:, q, :], ident[:]).then_inc(ea_back_turned, 1)
                arrived(ea_turned_ready, i * TURN + j + 1, 6)
                nc.tensor.matmul(bank(6, P, G * LAYERS * HEADS, q * P), ea_turned[:, q, :],
                                 edge_att8[:].rearrange("p k c -> p (k c)"), start=True, stop=True).then_inc(ce_done, 1)

            def add_up(width, turn, i):
                for j in range(TURN):
                    q = j % 2
                    if width == D:
                        edge_products(i, j)
                    _, offs = nc.values_load_multi_w_load_instructions(
                        tile_off[0:1, bass.ds(i * (TURN * G) + j * G, G)], engines=[mybir.EngineType.PE],
                        min_val=0, max_val=(NBANK - 1) * BANK + (PER_BANK - 1) * ACC)
                    pe.wait_ge(sums_ready, turn * TURN + j + 1)
                    for u in range(G):
                        mm = nc.tensor.matmul(
                            ps[:].rearrange("p k c -> p (k c)")[:, bass.ds(offs[u], width)],
                            onehot[:, q, u, :], sums_in[:, q, u, 0:width],
                            start=False, stop=True, skip_group_check=True)
                    mm.then_inc(sums_used, 1)

            pe.wait_ge(w1_in, 16 * (4 + 2 * HEADS + HEADS * (LAYERS + 1)))
            pe.wait_ge(tab0_staged, NB)
            for l in range(LAYERS):
                mm = nc.tensor.transpose(bank(5, P, D, l * D), w_ext[:, l, 0:HEADS * D], ident[0:D, 0:D])
            mm.then_inc(w1_turned, 1)
            pe.wait_ge(w1_copied, 1)
            for l in range(LAYERS):
                nc.tensor.matmul(bank(6, D, 2 * HEADS, l * 2 * HEADS), w_turned[:, l, :], att[:, l, :], start=True, stop=True)
                nc.tensor.matmul(bank(6, EF, HEADS, 32 + l * HEADS), edge_nat[:, l, :], att[:, l, HEADS:2 * HEADS],
                                 start=True, stop=True)
                mm = nc.tensor.matmul(bank(6, P, HEADS, 64 + l * HEADS), edge_bias[:, l:l + 1].to_broadcast([P, P]),
                                      att[:, l, HEADS:2 * HEADS], start=True, stop=True)
            mm.then_inc(w1_products, 1)
            pe.wait_ge(acc_read, 1)
            pe.wait_ge(back_packed, NRB + 2)
            turn_rows(pay[:, 1, :], 0, keys_turned)
            turn_lines(pay[:, 2, :], 2, keys_turned)
            pe.wait_ge(edge_att8_in, 16 * G)
            for k in range(2):
                pe.wait_ge(flags_cols, k + 1)
                nc.tensor.transpose(bank(7, 4, P, k * P), carry_col[:, 0:4], ident[:]).then_inc(flags_turned, 1)

            pe.wait_ge(keys_ready, 1)
            zero_acc(1)
            pe.wait_ge(tiles_ready, 1)
            with pe.Fori(0, NIT) as i:
                add_up(D, i, i)

            with pe.Fori(0, LAYERS) as l:
                arrived(h_ready, l + 2, 5)
                for n, (b0, nb) in enumerate(NODE_BATCHES):
                    if n >= 2:
                        arrived(hT_ready, (l + 1) * len(NODE_BATCHES) + n - 1, 5 + n % 2)
                    for b in range(b0, b0 + nb):
                        mm = nc.tensor.transpose(bank(5 + n % 2, D, P, (b - b0) * P), h_sb[:, b, :], ident[:])
                    mm.then_inc(hT_turned, 1)
                arrived(hT_ready, (l + 2) * len(NODE_BATCHES), 0)
                for n in range(XB):
                    if n >= 4:
                        arrived(xt_copied, l * XB + n - 3, n % 4)
                    for b in range(n * 3, min(NB, n * 3 + 3)):
                        mm = nc.tensor.matmul(bank(n % 4, P, XC, (b - n * 3) * XC), hT_l[:, b * P:(b + 1) * P],
                                              w_ext[:, bass.ds(l, 1), :].rearrange("i o c -> i (o c)"),
                                              start=True, stop=True)
                    mm.then_inc(xt_done, 1)
                arrived(s_src_ready, l + 1, 4)
                with pe.Fori(0, NG // LB) as i:
                    for q in range(LB):
                        if q % 2 == 0:
                            pe.wait_ge(hots_in[q // 2], l * (32 * (NG // LB)) + i * 32 + 32)
                        pe.wait_ge(sj_read, l * NG + i * LB + q + 1 + LH)
                        for u in range(G):
                            for k in range(3):
                                mm = nc.tensor.matmul(bank(4 + q % LH, P, HEADS * NB, u * HEADS * NB),
                                                      lo_hot_n[:, q, u * P:(u + 1) * P],
                                                      s_src3[:, k, :, :].rearrange("p h b -> p (h b)"),
                                                      start=(k == 0), stop=(k == 2))
                        mm.then_inc(sj_done, 1)
                arrived(vals_ready, l + 1, 0)
                for h in range(HEADS):
                    turn_rows(slot_vals[:, h, :], 2 * h, vals_turned)
                for r in range(5):
                    pe.wait_ge(carry_cols, l * 5 + r + 1)
                    nc.tensor.transpose(bank(7, P, P), carry_col[:], ident[:]).then_inc(carry_turned, 1)
                    pe.wait_ge(carry_rows, l * 5 + r + 1)
                    nc.tensor.transpose(bank(7, P, P, P), carry_row[:], ident[:]).then_inc(carry_back, 1)
                for h in range(HEADS):
                    arrived(weights_ready, l * HEADS + h + 1, 2 * h)
                    for u in range(G):
                        mm = nc.tensor.transpose(bank(2 * h + u // 4, P, NG, (u % 4) * NG), scores[:, h, u * P:(u + 1) * P],
                                                 ident[0:NG, 0:NG])
                    mm.then_inc(wturned, 1)
                arrived(wcopied, l * HEADS + HEADS, 0)
                for k in range(NBANK):
                    nc.tensor.matmul(bank(k, P, PER_BANK * ACC), zeros[:, 0:P], zeros[:, 0:PER_BANK * ACC],
                                     start=True, stop=True)
                with pe.Fori(0, NIT) as i:
                    add_up(ACC, (l + 1) * NIT + i, i)
                for n in range(NB):
                    if n == 0:
                        arrived(sums_copied, l + 1, 5)
                    if n >= 8 and n % 4 == 0:
                        arrived(sumsT_ready, l * SB + n // 4 - 1, 5 + (n // 4) % 2)
                    mm = nc.tensor.transpose(bank(5 + (n // 4) % 2, HEADS * EA1, P, (n % 4) * P),
                                             sums[:, n, D:ACC], ident[:])
                    if n % 4 == 3 or n == NB - 1:
                        mm.then_inc(sums_turned, 1)
                arrived(sumsT_ready, (l + 1) * SB, 0)
                for b in range(NB):
                    mm = nc.tensor.matmul(bank(b // 8, P, D, (b % 8) * D), sumsT[:, b * P:(b + 1) * P],
                                          edge_w[:, bass.ds(l, 1), :].rearrange("k o c -> k (o c)"),
                                          start=True, stop=True)
                mm.then_inc(edge_out_done, 1)

        @block.vector
        def _(dve):
            order = Order(dve, dve_steps)
            V = nc.vector
            V.memset(empty_stats[:, :, 2:4], 1.0)
            V.memset(empty_fill[:, :, 0:2], 0.0)
            V.memset(empty_fill[:, :, 2:4], -BIG)
            V.memset(empty_stats[:, :, 0:2], -BIG)
            dve.wait_ge(consts_ready, 1)
            order.step(V.tensor_scalar(ident[:], iota_row[:], iota_col[:, 0:1], None, ALU.is_equal))
            order.step(V.tensor_scalar(before[:], iota_row[:], iota_col[:, 0:1], None, ALU.is_gt))
            order.link(V.tensor_scalar(before16[:], iota_row[:], iota_col[:, 0:1], None, ALU.is_gt))
            V.memset(empty_slots[:, :, EF + 1:EF + 2], -9999.0).then_inc(empty_ready, 1)
            dve.wait_ge(edges_in, 64)
            order.step(V.tensor_scalar(part_i[:, 0, :], edge_i[:, 0, :], P - 1, None, ALU.bitwise_and))
            order.link(V.tensor_scalar(part_i[:, 1, :], edge_i[:, 0, :], 7, None, ALU.arith_shift_right))
            V.tensor_copy(rows16[:, 0, :], edge_i[:, 0, :]).then_inc(edge_rows_ready, 1)
            V.tensor_copy(rows16[:, 1, :], part_i[:, 0, :]).then_inc(edge_rows_ready, 1)
            V.tensor_copy(edge_t[:, 1:4, :, :].rearrange("g a k e -> g a (k e)"), edge_i[:])
            V.tensor_copy(edge_t[:, 4:6, :, :].rearrange("g a k e -> g a (k e)"), part_i[:]).then_inc(edge_cols_ready, 1)
            for k in range(KE):
                dve.wait_ge(edge_turned, k + 1)
                last = V.tensor_copy(edge_c[:, :, :, k],
                                     bank(k % 2, TE, 6 * GE).rearrange("e (a g) -> e a g", a=6))
                last.then_inc(edge_turn_used, 1)
            dve.wait_ge(edge_turn_used, KE)

            def edge_onehots(g, q):
                V.tensor_tensor(lo_hot[:, q, :, :], iota_row[0:TE, :].unsqueeze(1).to_broadcast([TE, KE, P]),
                                edge_c[:, 4, bass.ds(g, 1), :].rearrange("e o k -> e (o k)")
                                .unsqueeze(2).to_broadcast([TE, KE, P]), ALU.is_equal)
                return V.tensor_tensor(hi_hot[:, q, :, :], iota_row[0:TE, 0:NB].unsqueeze(1).to_broadcast([TE, KE, NB]),
                                       edge_c[:, 5, bass.ds(g, 1), :].rearrange("e o k -> e (o k)")
                                       .unsqueeze(2).to_broadcast([TE, KE, NB]), ALU.is_equal)

            with dve.Fori(0, GE // BUF3) as i:
                for q in range(BUF3):
                    dve.wait_ge(hist_used, i * BUF3 + q + 1)
                    edge_onehots(i * BUF3 + q, q).then_inc(hist_onehots, 1)
            dve.wait_ge(hist_used, GE + 1)
            V.tensor_copy(hist[:], bank(6, P, NB)).then_inc(hist_read, 1)
            dve.wait_ge(prefix_done, 1)
            order.link(V.tensor_scalar(tiles_f[:], bank(7, P, NB, 32), float(P - 1), None, ALU.add))
            order.link(V.tensor_copy(tiles_i[:], tiles_f[:]))
            order.link(V.tensor_scalar(tiles_i[:], tiles_i[:], 7, None, ALU.arith_shift_right))
            order.link(V.tensor_copy(tiles_f[:], tiles_i[:]))
            order.link(V.tensor_tensor_scan(tiles_cum[:], ones[:, 0:NB], tiles_f[:], 0.0, ALU.mult, ALU.add))
            order.link(V.tensor_tensor(tile0[:], tiles_cum[:], tiles_f[:], ALU.subtract))
            order.link(V.scalar_tensor_tensor(out=first[:], in0=tile0[:], scalar=float(P), in1=bank(7, P, NB),
                                              op0=ALU.mult, op1=ALU.add))
            order.step(V.tensor_scalar(has[:], hist[:], 0.0, None, ALU.is_gt))
            order.link(V.tensor_tensor(tiles_cum[:], first[:], spare_row[:], ALU.subtract))
            order.link(V.tensor_tensor(tiles_cum[:], tiles_cum[:], has[:], ALU.mult))
            order.link(V.tensor_tensor(start_row[:], tiles_cum[:], spare_row[:], ALU.add))
            V.tensor_copy(snap[:, BUF3 - 1, KE, :], first[:]).then_inc(snap_ready, 1)
            with order.loop(GE // BUF3, 3 * BUF3) as i:
                for q in range(BUF3):
                    g = i * BUF3 + q
                    prev = (q - 1) % BUF3
                    edge_onehots(g, q).then_inc(pos_onehots, 1)
                    dve.wait_ge(rows_in[q], i * 32 + 32)
                    V.tensor_scalar(lo_hotT[:, q, :, :].rearrange("p k e -> p (k e)"), row_in[:, q, 1, :],
                                    iota_col[:, 0:1], None, ALU.is_equal)
                    order.link(V.tensor_tensor(same[:, q, :, :],
                                               row_in[0:TE, q, 0, :].rearrange("p (k e) -> p k e", e=TE),
                                               edge_c[:, 1, bass.ds(g, 1), :].rearrange("e o k -> e (o k)")
                                               .unsqueeze(2).to_broadcast([TE, KE, TE]), ALU.is_equal))
                    V.tensor_tensor(same[:, q, :, :], same[:, q, :, :],
                                    before16[0:TE, 0:TE].unsqueeze(1).to_broadcast([TE, KE, TE]),
                                    ALU.mult).then_inc(pos_masks, 1)
                    V.tensor_copy(payload[:, q, :].rearrange("e (k w) -> e k w", w=W_PAY)[:, :, EF:W_PAY],
                                  edge_c[:, 0:4, bass.ds(g, 1), :].rearrange("e a o k -> e (o k) a"))
                    dve.wait_ge(counts_ready, g + 1)
                    dve.wait_ge(snap_ready, g + 1)
                    V.tensor_tensor(snap[:, q, :, :], bank(q, P, (KE + 1) * NB).rearrange("p (k b) -> p k b", b=NB),
                                    snap[:, prev, KE:KE + 1, :].to_broadcast([P, KE + 1, NB]),
                                    ALU.add).then_inc(snap_ready, 1)
                    dve.wait_ge(looked_up, g + 1)
                    order.link(V.tensor_tensor(picked[:], bank(3 + q, TE, KE * NB).rearrange("e (k b) -> e k b", b=NB),
                                               hi_hot[:, q, :, :], ALU.mult))
                    order.link(V.tensor_reduce(base_at[:], picked[:], AX, ALU.add))
                    V.tensor_tensor(pos[:, q, :], base_at[:], bank(3 + q, TE, KE, KE * NB),
                                    ALU.add).then_inc(pos_ready, 1)

            for q in range(BUF3):
                dve.wait_ge(scat[q], GE // BUF3 * 16 * KE)
            order.link(V.memset(gate2[:], 0.0))
            V.memset(gate2[:], 0.0).then_inc(prep_over, 1)
            dve.wait_ge(prep_over, 1)
            V.memset(edge_att8[:], 0.0)
            V.memset(att[:], 0.0).then_inc(w1_zeroed, 1)

            def layernorm(x_sums, h_out, n):
                order.link(V.tensor_reduce(mean[:], x_sums[:], AX, ALU.add))
                order.link(V.tensor_scalar(mean[:], mean[:], -1.0 / D, None, ALU.mult))
                order.link(V.tensor_tensor(centred[:], x_sums[:], mean[:].unsqueeze(2).to_broadcast([P, NB, D]), ALU.add))
                order.link(V.tensor_tensor(h_out[:], centred[:], centred[:], ALU.mult))
                order.link(V.tensor_reduce(var[:], h_out[:], AX, ALU.add))
                V.tensor_scalar(var[:], var[:], 1.0 / D, LN_EPS, ALU.mult, ALU.add).then_inc(var_ready, 1)
                dve.wait_ge(std_ready, n)
                order.link(V.reciprocal(var[:], var[:]))
                order.link(V.tensor_tensor(centred[:], centred[:], var[:].unsqueeze(2).to_broadcast([P, NB, D]), ALU.mult))
                last = V.tensor_scalar(h_out[:], centred[:], 0.0, None, ALU.max)
                if n == 1:
                    last.then_inc(h_ready, 1)
                else:
                    order.link(last)

            dve.wait_ge(x_in, 32)
            layernorm(x_res, h_sb, 1)
            for n, (b0, nb) in enumerate(NODE_BATCHES):
                dve.wait_ge(hT_turned, n + 1)
                V.tensor_copy(hT[:, b0 * P:(b0 + nb) * P], bank(5 + n % 2, D, nb * P)).then_inc(hT_ready, 1)
            dve.wait_ge(loop_done, 1)
            V.tensor_tensor(x_res[:].rearrange("p b d -> p (b d)"), x_res[:].rearrange("p b d -> p (b d)"),
                            ps[:].rearrange("p k c -> p (k c)")[:, 0:NB * D], ALU.add).then_inc(acc_read, 1)
            dve.wait_ge(w0_in, 16)
            for b in range(NB):
                dve.wait_ge(proj_done, b + 1)
                if b >= 2:
                    dve.wait_ge(tab0_out[b % 2], 16 * (b // 2))
                V.tensor_tensor(tab0_sb[:, b % 2, :].rearrange("p (r d) -> p r d", d=D),
                                bank(5 + b % 2, P, R * D).rearrange("p (r d) -> p r d", d=D),
                                bias_types[:].unsqueeze(1).to_broadcast([P, R, D]), ALU.add).then_inc(tab0_staged, 1)
            V.memset(gate2[:], 0.0).then_inc(back_packed, 2)
            with dve.Fori(0, NRB // 2) as i:
                for q in range(2):
                    dve.wait_ge(back_in[q], i * 16 + 16)
                    rows = back[:, q, :].rearrange("e (t w) -> e t w", w=W_PAY)
                    V.tensor_copy(pay[:, :, bass.ds((i * 2 + q) * RB, RB)].rearrange("e a t -> e t a"), rows[:, :, EF:W_PAY])
                    V.tensor_copy(ea_pack[:, q, :].rearrange("e (t f) -> e t f", f=EF), rows[:, :, 0:EF]).then_inc(back_packed, 1)
            dve.wait_ge(back_packed, NRB + 2)
            order.step(V.scalar_tensor_tensor(out=idx0_f[:], in0=pay[:, 2, :], scalar=float(R), in1=pay[:, 3, :],
                                              op0=ALU.mult, op1=ALU.add))
            order.step(V.tensor_copy(idx[:, 0:NT], pay[:, 2, :]))
            order.step(V.tensor_copy(idx[:, NT:], pay[:, 2, 0:RING * G]))
            order.link(V.tensor_copy(idx0[:, NT:], pay[:, 2, 0:RING * G]))
            order.link(V.tensor_copy(idx0[:, 0:NT], idx0_f[:]))
            V.tensor_copy(idx_stage[:], idx0[:, 0:RING * G]).then_inc(staged, RING)
            dve.wait_ge(tiles_iota, 1)
            order.link(V.tensor_scalar(blk[:], iota_tile[:], tile0[:, 1:2], None, ALU.is_ge))
            for b in range(2, NB):
                order.link(V.scalar_tensor_tensor(out=blk[:], in0=iota_tile[:], scalar=tile0[:, b:b + 1], in1=blk[:],
                                                  op0=ALU.is_ge, op1=ALU.add))
            order.step(V.scalar_tensor_tensor(out=rel[:], in0=blk[:], scalar=-float(P), in1=pay[:, 1, :],
                                              op0=ALU.mult, op1=ALU.add))
            order.link(V.tensor_scalar(off_f[:, 0, :], blk[0:1, :], float(PER_BANK), None, ALU.is_ge))
            for k in range(2, NBANK):
                order.link(V.scalar_tensor_tensor(out=off_f[:, 0, :], in0=blk[0:1, :], scalar=float(PER_BANK * k),
                                                  in1=off_f[:, 0, :], op0=ALU.is_ge, op1=ALU.add))
            order.link(V.tensor_scalar(off_f[:, 0, :], off_f[:, 0, :], float(BANK - PER_BANK * ACC), None, ALU.mult))
            order.link(V.scalar_tensor_tensor(out=off_f[:, 1, :], in0=blk[0:1, :], scalar=float(ACC),
                                              in1=off_f[:, 0, :], op0=ALU.mult, op1=ALU.add))
            V.tensor_copy(tile_off[:], off_f[:, 1, :]).then_inc(tiles_ready, 1)

            dve.wait_ge(w1_turned, 1)
            V.tensor_copy(w_turned[:].rearrange("p l d -> p (l d)"), bank(5, P, LAYERS * D)).then_inc(w1_copied, 1)
            dve.wait_ge(w1_products, 1)
            V.tensor_copy(w_ext[:, :, HEADS * D:XC], bank(6, D, LAYERS * 2 * HEADS).rearrange("p (l c) -> p l c", l=LAYERS))
            V.tensor_copy(att_bias[:].rearrange("p l h -> p (l h)"), bank(6, P, LAYERS * HEADS, 64))
            V.tensor_copy(edge_att[:], bank(6, EF, LAYERS * HEADS, 32)).then_inc(edge_att_ready, 1)
            order.step(V.memset(keys[:], -1.0))
            order.link(V.tensor_scalar(hi_i[:], idx[:, 0:NT], 7, None, ALU.arith_shift_right))
            order.step(V.tensor_copy(src_hi[:], hi_i[:]))
            dve.wait_ge(keys_turned, 2)
            mine = keys[:, 1:GS + 1]
            order.step(V.tensor_copy(mine.rearrange("g (k c) -> g k c", k=2), ps[0:NG, 0:2, :]))
            rows_of = ps[:, 2:4, :].rearrange("p k c -> p (k c)").rearrange("p (c e) -> p c e", e=P)
            for n, (c0, c1, rows) in enumerate(((0, NT // P, P), (NT // P, TC, NT % P))):
                order.link(V.tensor_copy(lo_i[0:rows, c0:c1, :], rows_of[0:rows, c0:c1, :]))
                order.link(V.tensor_scalar(lo_i[0:rows, c0:c1, :], lo_i[0:rows, c0:c1, :], P - 1, None, ALU.bitwise_and))
                order.link(V.tensor_copy(lo16[0:rows, c0:c1, :], lo_i[0:rows, c0:c1, :]))
            V.memset(gate2[:], 0.0).then_inc(keys_ready, 1)
            dve.wait_ge(keys_in, 32)
            order.step(V.tensor_tensor(keep[:], mine, keys[:, 0:GS], ALU.is_equal))
            order.link(V.tensor_tensor(keep_back[:], mine, keys[:, 2:GS + 2], ALU.is_equal))
            order.step(V.tensor_scalar(keep_neg[:], keep[:], -1.0, BIG, ALU.add, ALU.mult))
            order.step(V.tensor_scalar(keep_back_neg[:], keep_back[:], -1.0, BIG, ALU.add, ALU.mult))
            order.step(V.tensor_tensor_scan(head_run[:], keep[:], keep[:], 1.0, ALU.mult, ALU.mult))
            order.step(V.tensor_tensor_scan(tail_run[:, ::-1], keep_back[:, ::-1], keep_back[:, ::-1], 1.0, ALU.mult, ALU.mult))
            order.step(V.memset(carry_row[:], 0.0))
            order.link(V.memset(carry_col[:], 0.0))
            order.step(V.tensor_scalar(head_neg[:], head_run[:], -1.0, BIG, ALU.add, ALU.mult))
            order.step(V.tensor_scalar(tail_neg[:], tail_run[:], -1.0, BIG, ALU.add, ALU.mult))
            for k, flags in enumerate((head_run[:, GS - 1:GS], tail_run[:, 0:1])):
                V.tensor_copy(carry_col[0:NG, 0:4], flags.to_broadcast([NG, 4])).then_inc(flags_cols, 1)
                dve.wait_ge(flags_turned, k + 1)
                order.link(V.tensor_copy(row_flags[0:4, 2 * k, :], bank(7, 4, P, k * P)))
            order.step(V.tensor_scalar(row_flags[0:4, 1, :], row_flags[0:4, 0, :], -1.0, BIG, ALU.add, ALU.mult))
            order.link(V.tensor_scalar(row_flags[0:4, 2, :], row_flags[0:4, 2, :], -1.0, BIG, ALU.add, ALU.mult))
            for free, count in ((ea_used, 2), (hots_made, 2), (hots_out[0], 16), (hots_out[1], 16)):
                V.memset(gate2[:], 0.0).then_inc(free, count)
                dve.wait_ge(free, count)

            with dve.Fori(0, NIT) as i:
                for j in range(TURN):
                    q = j % 2
                    t0 = i * (TURN * G) + j * G
                    dve.wait_ge(ea_back_turned, i * TURN + j + 1)
                    V.tensor_copy(ea_turned[:, q, :], bank(5, P, P, q * P)).then_inc(ea_turned_ready, 1)
                    dve.wait_ge(lo_in[q], i * (16 * RING) + (j // 2 + 1) * 16)
                    dve.wait_ge(hots_out[q], i * (32 * RING) + (j // 2) * 32 + 16)
                    V.tensor_scalar(lo_hot_n[:, q, :], lo_in_sb[:, q, :], iota_col[:, 0:1], None, ALU.is_equal)
                    V.tensor_tensor(hi_hot_n[:, q, :].rearrange("p (u b) -> p u b", u=G),
                                    iota_row[:, 0:NB].unsqueeze(1).to_broadcast([P, G, NB]),
                                    src_hi[:, bass.ds(t0, G)].unsqueeze(2).to_broadcast([P, G, NB]),
                                    ALU.is_equal).then_inc(hots_made, 1)
                    dve.wait_ge(sums_used, i * TURN + j + 1)
                    V.tensor_tensor(onehot[:, q, :, :], iota_row[:].unsqueeze(1).to_broadcast([P, G, P]),
                                    rel[:, bass.ds(t0, G)].unsqueeze(2).to_broadcast([P, G, P]), ALU.is_equal)
                    dve.wait_ge(ce_done, i * TURN + j + 1)
                    V.tensor_scalar(ce_sb[:, :, bass.ds(t0, G)],
                                    bank(6, P, G * LAYERS * HEADS, q * P).rearrange("p (u c) -> p c u", u=G),
                                    0.0, None, ALU.add).then_inc(ea_used, 1)
                    r = j % RING * G
                    dve.wait_ge(gathered[j % RING], i * (32 * G) + 16 * G * (j // RING + 1))
                    V.tensor_tensor(sums_in[:, q, :, 0:D], ring_rows[:, r:r + G, 0:D],
                                    pay[:, 0, bass.ds(t0, G)].unsqueeze(2).to_broadcast([P, G, D]),
                                    ALU.mult).then_inc(sums_ready, 1)
                    V.tensor_copy(idx_stage[:, r:r + G], idx0[:, bass.ds(t0 + RING * G, G)]).then_inc(staged, 1)
            V.memset(gate2[:], 0.0).then_inc(ce_filled, 1)
            dve.wait_ge(sums_used, NG + 2)
            order.link(V.tensor_copy(centred[:].rearrange("p (k b) d -> p k b d", b=PER_BANK), acc_all(0, D)))
            order.link(V.tensor_tensor(x_res[:], x_res[:], centred[:], ALU.add))
            layernorm(x_res, h_sb, 2)
            dve.wait_ge(ce_out, 16)
            V.memset(gate2[:], 0.0).then_inc(sj_read, LB)

            def carry(columns, n, flags, backward, nothing, r, l):
                V.tensor_copy(carry_col[0:NG, 0:n], columns).then_inc(carry_cols, 1)
                dve.wait_ge(carry_turned, l * 5 + r + 1)
                rows = bank(7, n, NG)
                ops = (ALU.add, ALU.max) if nothing else (ALU.mult, ALU.add)
                if backward:
                    order.step(V.memset(carry_row[0:n, NG - 1:NG], nothing))
                    order.link(V.tensor_tensor_scan(carry_row[0:n, 0:NG - 1][:, ::-1], row_flags[0:n, flags, 1:NG][:, ::-1],
                                                    rows[:, 1:NG][:, ::-1], nothing, *ops))
                else:
                    order.step(V.memset(carry_row[0:n, 0:1], nothing))
                    order.link(V.tensor_tensor_scan(carry_row[0:n, 1:NG], row_flags[0:n, flags, 0:NG - 1],
                                                    rows[:, 0:NG - 1], nothing, *ops))
                V.memset(gate2[:], 0.0).then_inc(carry_rows, 1)
                dve.wait_ge(carry_back, l * 5 + r + 1)
                order.link(V.tensor_copy(carry_in[0:NG, 0:n], bank(7, NG, n, P)))

            def spread_back(values, spread, r, l):
                for h in range(HEADS):
                    order.step(V.tensor_tensor_scan(spread[:, h, ::-1], keep_back_neg[:, ::-1], values[:, h, ::-1], -BIG,
                                                    ALU.add, ALU.max))
                order.settle()
                carry(spread[:, :, 0], HEADS, 2, True, -BIG, r, l)
                for h in range(HEADS):
                    order.step(V.scalar_tensor_tensor(out=spread[:, h, :], in0=tail_neg[:], scalar=carry_in[0:NG, h:h + 1],
                                                      in1=spread[:, h, :], op0=ALU.add, op1=ALU.max))
                order.settle()

            with order.loop(LAYERS, PER_LAYER) as l:
                V.tensor_scalar(h_sb[:], h_sb[:], 0.0, None, ALU.max).then_inc(h_ready, 1)
                for n, (b0, nb) in enumerate(NODE_BATCHES):
                    dve.wait_ge(hT_turned, (l + 1) * len(NODE_BATCHES) + n + 1)
                    V.tensor_copy(hT_l[:, b0 * P:(b0 + nb) * P], bank(5 + n % 2, D, nb * P)).then_inc(hT_ready, 1)
                for n in range(XB):
                    nb = min(NB, n * 3 + 3) - n * 3
                    dve.wait_ge(xt_done, l * XB + n + 1)
                    V.tensor_copy(xt_sb[:, n * 3:n * 3 + nb, :].rearrange("p b c -> p (b c)"),
                                  bank(n % 4, P, nb * XC)).then_inc(xt_copied, 1)
                dve.wait_ge(xt_copied, l * XB + XB)
                at_dst, at_src = xt_sb[:, :, HEADS * D:HEADS * D + HEADS], xt_sb[:, :, HEADS * D + HEADS:XC]
                order.link(V.tensor_tensor(node_terms[:, :, 0:HEADS], at_dst,
                                           att_bias[:, bass.ds(l, 1), :].to_broadcast([P, NB, HEADS]), ALU.add))
                order.link(V.tensor_tensor(loop_w[:, 0, :, :], node_terms[:, :, 0:HEADS], at_src, ALU.add))
                V.scalar_tensor_tensor(out=node_terms[:, :, HEADS:], in0=loop_w[:, 0, :, :], scalar=NEG_SLOPE,
                                       in1=loop_w[:, 0, :, :], op0=ALU.mult, op1=ALU.max).then_inc(fill_ready, 1)
                at_src_t = at_src.rearrange("p b h -> p h b")
                order.link(V.tensor_copy(s_src3[:, 0, :, :], at_src_t))
                order.link(V.tensor_tensor(s_src[:, 0, :, :], at_src_t, s_src3[:, 0, :, :], ALU.subtract))
                order.link(V.tensor_copy(s_src3[:, 1, :, :], s_src[:, 0, :, :]))
                order.link(V.tensor_tensor(s_src[:, 1, :, :], s_src[:, 0, :, :], s_src3[:, 1, :, :], ALU.subtract))
                dve.wait_ge(ce_in, l * 16 + 16)
                V.tensor_copy(s_src3[:, 2, :, :], s_src[:, 1, :, :]).then_inc(s_src_ready, 1)
                with order.loop(NG // LB, 4) as i:
                    for half in range(2):
                        for q in range(half * LH, half * LH + LH):
                            dve.wait_ge(sj_done, l * NG + i * LB + q + 1)
                            if q % 2 == 0:
                                dve.wait_ge(hots_in[q // 2], l * (32 * (NG // LB)) + i * 32 + 32)
                            V.tensor_tensor(
                                sj_picked[:, q % LH, :, :, :],
                                bank(4 + q % LH, P, G * HEADS * NB).rearrange("p (u h b) -> p u h b", u=G, h=HEADS),
                                hi_hot_n[:, q, :].rearrange("p (u b) -> p u b", u=G).unsqueeze(2)
                                .to_broadcast([P, G, HEADS, NB]), ALU.mult).then_inc(sj_read, 1)
                        dve.wait_ge(sj_read, l * NG + i * LB + half * LH + LH + LB)
                        order.link(V.tensor_reduce(sj_part[:].rearrange("p h t -> p t h"),
                                                   sj_picked.rearrange("p q u h b -> p (q u) h b"), AX, ALU.add))
                        t0 = i * (LB * G) + half * (LH * G)
                        order.step(V.tensor_tensor(slot_vals[:, :, bass.ds(t0, LH * G)], sj_part[:],
                                                   slot_vals[:, :, bass.ds(t0, LH * G)], ALU.add))
                order.settle()
                V.memset(gate2[:], 0.0).then_inc(vals_ready, 1)

                dve.wait_ge(fill_in, l * 16 + 16)
                terms = filled[0:NG]
                for c in range(HEADS):
                    order.step(V.tensor_tensor_scan(terms[:, :, c], keep[:], terms[:, :, c], 0.0, ALU.mult, ALU.add))
                order.settle()
                carry(terms[:, GS - 1, 0:HEADS], HEADS, 0, False, 0.0, 0, l)
                for c in range(HEADS):
                    order.step(V.scalar_tensor_tensor(out=terms[:, :, c], in0=head_run[:], scalar=carry_in[0:NG, c:c + 1],
                                                      in1=terms[:, :, c], op0=ALU.mult, op1=ALU.add))
                order.settle()
                for h in range(HEADS):
                    dve.wait_ge(vals_turned, l * HEADS + h + 1)
                    order.step(V.tensor_tensor(scores[:, h, :], ps[0:NG, 2 * h:2 * h + 2, :].rearrange("p k c -> p (k c)"),
                                               terms[:, :, h], ALU.add))
                order.settle()
                order.link(V.scalar_tensor_tensor(out=scores, in0=scores, scalar=NEG_SLOPE, in1=scores,
                                                  op0=ALU.mult, op1=ALU.max))
                loops = terms[:, :, HEADS:].rearrange("g s h -> g h s")
                order.link(V.tensor_tensor(running, scores, loops, ALU.max))
                for h in range(HEADS):
                    order.step(V.tensor_tensor_scan(running[:, h, :], keep_neg[:], running[:, h, :], -BIG, ALU.add, ALU.max))
                order.settle()
                carry(running[:, :, GS - 1], HEADS, 1, False, -BIG, 1, l)
                for h in range(HEADS):
                    order.step(V.scalar_tensor_tensor(out=running[:, h, :], in0=head_neg[:], scalar=carry_in[0:NG, h:h + 1],
                                                      in1=running[:, h, :], op0=ALU.add, op1=ALU.max))
                order.settle()
                spread_back(running, total, 2, l)
                order.step(V.tensor_tensor(scores, scores, total, ALU.subtract))
                order.link(V.tensor_tensor(running, loops, total, ALU.subtract))
                V.memset(gate2[:], 0.0).then_inc(shifted, 1)
                order.step(V.tensor_copy(terms[:, :, 0:HEADS].rearrange("g s h -> g h s"), total))
                dve.wait_ge(exp_done, l + 1)
                order.link(V.tensor_tensor(running, running, scores, ALU.add))
                for h in range(HEADS):
                    order.step(V.tensor_tensor_scan(running[:, h, :], keep[:], running[:, h, :], 0.0, ALU.mult, ALU.add))
                order.settle()
                carry(running[:, :, GS - 1], HEADS, 0, False, 0.0, 3, l)
                for h in range(HEADS):
                    order.step(V.scalar_tensor_tensor(out=running[:, h, :], in0=head_run[:], scalar=carry_in[0:NG, h:h + 1],
                                                      in1=running[:, h, :], op0=ALU.mult, op1=ALU.add))
                order.settle()
                spread_back(running, total, 4, l)
                for h in range(HEADS):
                    order.link(V.tensor_scalar(running[:, h, :], total[:, h, :], 1e-16, None, ALU.add))
                    order.link(V.reciprocal(running[:, h, :], running[:, h, :]))
                    V.tensor_tensor(scores[:, h, :], scores[:, h, :], running[:, h, :],
                                    ALU.mult).then_inc(weights_ready, 1)
                V.memset(gate2[:], 0.0).then_inc(dens_ready, 1)
                for h in range(HEADS):
                    dve.wait_ge(wturned, l * HEADS + h + 1)
                    V.tensor_copy(slot_vals[:, h, :].rearrange("p (k c) -> p k c", k=2), ps[:, 2 * h:2 * h + 2, 0:NT // 2]
                                  ).then_inc(wcopied, 1)
                with order.loop(NIT, TURN) as i:
                    for j in range(TURN):
                        q = j % 2
                        t0 = i * (TURN * G) + j * G
                        r = j % RING * G
                        w = slot_vals[:, :, bass.ds(t0, G)].rearrange("p h t -> p t h")
                        if j == 0:
                            dve.wait_ge(wcopied, l * HEADS + HEADS)
                        dve.wait_ge(sums_used, (l + 1) * NG + i * TURN + j + 1)
                        dve.wait_ge(gathered[j % RING], l * (32 * G * NIT) + i * (32 * G) + 16 * G * (2 * NIT + j // RING + 1))
                        order.step(V.tensor_tensor(
                            weighted[:, q], ring_rows[:, r:r + G, :].rearrange("p t (h d) -> p t h d", h=HEADS),
                            w.unsqueeze(3).to_broadcast([P, G, HEADS, D]), ALU.mult))
                        V.tensor_tensor(onehot[:, q, :, :], iota_row[:].unsqueeze(1).to_broadcast([P, G, P]),
                                        rel[:, bass.ds(t0, G)].unsqueeze(2).to_broadcast([P, G, P]), ALU.is_equal)
                        dve.wait_ge(ea_in[q], (l + 1) * (16 * NG // 2) + i * (16 * RING) + 16 * (j // 2 + 1))
                        edge_sums = sums_in[:, q, :, D:ACC].rearrange("p t (h f) -> p t h f", h=HEADS)
                        V.tensor_tensor(edge_sums[:, :, :, 0:EF],
                                        ea_in_sb[:, q, :].rearrange("p (t f) -> p t f", t=G).unsqueeze(2)
                                        .to_broadcast([P, G, HEADS, EF]),
                                        w.unsqueeze(3).to_broadcast([P, G, HEADS, EF]), ALU.mult).then_inc(ea_used, 1)
                        V.tensor_copy(edge_sums[:, :, :, EF], w)
                        order.settle()
                        V.tensor_tensor(sums_in[:, q, :, 0:D], weighted[:, q, :, 0, :], weighted[:, q, :, 1, :],
                                        ALU.add).then_inc(sums_ready, 1)
                        V.tensor_copy(idx_stage[:, r:r + G],
                                      idx[:, bass.ds(t0 + RING * G, G)]).then_inc(staged, 1)
                dve.wait_ge(sums_used, (l + 1) * NG + NG + 2)
                order.link(V.tensor_copy(sums.rearrange("p (k b) c -> p k b c", b=PER_BANK), acc_all(0, ACC)))
                dve.wait_ge(node_stats_in, l * (16 * NB) + 16 * NB)
                order.link(V.tensor_tensor(loop_w[:, 0, :, :], node_stats[:, :, 0:HEADS], node_terms[:, :, HEADS:], ALU.max))
                V.tensor_tensor(loop_w[:, 1, :, :], node_terms[:, :, HEADS:], loop_w[:, 0, :, :],
                                ALU.subtract).then_inc(loop_shifted, 1)
                dve.wait_ge(loop_exp, l + 1)
                order.link(V.tensor_scalar(loop_w[:, 3, :, :], node_stats[:, :, HEADS:], 1e-16, None, ALU.add))
                order.link(V.reciprocal(loop_w[:, 3, :, :], loop_w[:, 3, :, :]))
                order.link(V.tensor_tensor(loop_w[:, 1, :, :], loop_w[:, 2, :, :], loop_w[:, 3, :, :], ALU.mult))
                weight_sums = sums[:, :, D:ACC].rearrange("p b (h f) -> p b h f", h=HEADS)[:, :, :, EF]
                V.tensor_tensor(weight_sums, weight_sums, loop_w[:, 1, :, :], ALU.add).then_inc(sums_copied, 1)
                for n, (b0, nb) in enumerate(NODE_BATCHES):
                    dve.wait_ge(sums_turned, l * SB + n + 1)
                    V.tensor_copy(sumsT[:, b0 * P:(b0 + nb) * P], bank(5 + n % 2, HEADS * EA1, nb * P)).then_inc(sumsT_ready, 1)
                for h in range(HEADS):
                    order.link(V.tensor_tensor(tmp_nodes, xt_sb[:, :, h * D:(h + 1) * D],
                                               loop_w[:, 1, :, h:h + 1].to_broadcast([P, NB, D]), ALU.mult))
                    order.link(V.tensor_tensor(sums[:, :, 0:D], sums[:, :, 0:D], tmp_nodes, ALU.add))
                dve.wait_ge(edge_out_done, l + 1)
                order.link(V.tensor_tensor(tmp_nodes, ps[:].rearrange("p k c -> p (k c)")[:, 0:NB * D]
                                           .rearrange("p (b d) -> p b d", d=D), sums[:, :, 0:D], ALU.add))
                order.link(V.scalar_tensor_tensor(out=h_sb[:], in0=tmp_nodes, scalar=1.0 / HEADS,
                                                  in1=bias_out[:, bass.ds(l, 1), :].to_broadcast([P, NB, D]),
                                                  op0=ALU.mult, op1=ALU.add))
            V.tensor_tensor(x_res[:], x_res[:], h_sb[:], ALU.add).then_inc(x_done, 1)

        @block.scalar
        def _(act):
            order = Order(act, act_steps)
            act.wait_ge(consts_ready, 1)
            order.link(nc.scalar.copy(gate_act[:, 0:1], ones[:, 0:1]))
            nc.scalar.copy(gate_act[:, 1:2], gate_act[:, 0:1]).then_inc(payload_free, BUF3)
            with act.Fori(0, GE // BUF3) as i:
                for q in range(BUF3):
                    act.wait_ge(payload_free, i * BUF3 + q + BUF3)
                    act.wait_ge(scat[q], i * (16 * KE) + 16 * KE)
                    nc.scalar.copy(gate_act[:, 1:2], gate_act[:, 0:1]).then_inc(payload_free, 1)
            act.wait_ge(var_ready, 1)
            nc.scalar.activation(var[:], var[:], ACT.Sqrt).then_inc(std_ready, 1)
            for b in range(NB):
                act.wait_ge(tab0_staged, b + 1)
                act.dma_start(tab0_blocks[b], tab0_sb[:, b % 2, :]).then_inc(tab0_out[b % 2], 16)
            with act.Fori(0, NIT) as i:
                for j in range(TURN):
                    act.wait_ge(hots_made, i * TURN + j + 3)
                    act.dma_start(lohot_dram[bass.ds(i * TURN + j, 1)].rearrange("o p s -> (o p) s"),
                                  lo_hot_n[:, j % 2, :]).then_inc(hots_out[j % 2], 16)
                    act.dma_start(hihot_dram[bass.ds(i * TURN + j, 1)].rearrange("o p s -> (o p) s"),
                                  hi_hot_n[:, j % 2, :]).then_inc(hots_out[j % 2], 16)
            act.wait_ge(ce_filled, 1)
            act.dma_start(ce_dram.rearrange("l p c -> p l c"),
                          ce_sb[:].rearrange("p (l h) t -> p l (h t)", h=HEADS)).then_inc(ce_out, 16)
            act.wait_ge(var_ready, 2)
            nc.scalar.activation(var[:], var[:], ACT.Sqrt).then_inc(std_ready, 1)

            def arrived(semaphore, value):
                act.wait_ge(semaphore, value)
                order.settle()
                order.step(nc.scalar.copy(gate_act[:, 1:2], gate_act[:, 0:1]))

            with order.loop(LAYERS, 3) as l:
                act.wait_ge(xt_copied, l * XB + XB)
                act.dma_start(tab1.rearrange("(b p) c -> p b c", p=P), xt_sb[:, :, 0:HEADS * D]).then_inc(tab1_out, 16)
                act.dma_start(slot_vals[:].rearrange("p h t -> p (h t)"),
                              ce_dram[bass.ds(l, 1)].rearrange("o p c -> (o p) c")).then_inc(ce_in, 16)
                act.wait_ge(fill_out, l * (16 * NB) + 16 * NB)
                act.dma_start(filled[0:NG].rearrange("g s c -> g (s c)"),
                              fill_dram[0:SL].rearrange("(g s) c -> g (s c)", g=NG)).then_inc(fill_in, 16)
                arrived(shifted, l + 1)
                nc.scalar.activation(scores, scores, ACT.Exp)
                nc.scalar.activation(running, running, ACT.Exp).then_inc(exp_done, 1)
                arrived(dens_ready, l + 1)
                nc.scalar.copy(filled[0:NG, :, HEADS:].rearrange("g s h -> g h s"), total).then_inc(stats_ready, 1)
                act.wait_ge(stats_ready, l + 1)
                act.dma_start(stats_dram[0:SL].rearrange("(g s) c -> g (s c)", g=NG),
                              filled[0:NG].rearrange("g s c -> g (s c)")).then_inc(stats_out, 16)
                arrived(loop_shifted, l + 1)
                nc.scalar.activation(loop_w[:, 2, :, :], loop_w[:, 1, :, :], ACT.Exp).then_inc(loop_exp, 1)


_OUTS = [((N, D), "float32")]
_INS = ["x", "src", "dst", "edge_attr_16", "edge_type_8", "edge_weight1", "L0_gnn_weight", "L0_gnn_h_bias",
        "L0_gnn_loop_weight", "L1_gnn_weights", "L1_gnn_biases", "L1_gnn_edge_ws", "L1_gnn_edge_bs", "L1_gnn_atts"]


def kernel(**inputs):
    import numpy as _np
    import concourse.bacc as _bacc
    from concourse import mybir as _mybir
    from concourse.bass_utils import run_bass_kernel_spmd as _run

    nc = _bacc.Bacc("TRN2", target_bir_lowering=False, num_devices=1)
    arrays, args = {}, []
    for name in _INS:
        a = _np.ascontiguousarray(inputs[name])
        arrays[f"in_{name}_dram"] = a
        args.append(nc.dram_tensor(f"in_{name}_dram", a.shape, _mybir.dt.from_np(a.dtype), kind="ExternalInput").ap())
    for i, (shape, dtype) in enumerate(_OUTS):
        dt = _mybir.dt.from_np(_np.dtype(dtype))
        args.append(nc.dram_tensor(f"out_{i}_dram", shape, dt, kind="ExternalOutput").ap())
    build_gnn(nc, *args)
    r = _run(nc, [arrays], core_ids=[0])
    return r.results[0]["out_0_dram"]
```

```python
from contextlib import ExitStack, contextmanager

import concourse.bass as bass
from concourse import mybir

ALU = mybir.AluOpType
ACT = mybir.ActivationFunctionType
AX = mybir.AxisListType.X
F32 = mybir.dt.float32
BF16 = mybir.dt.bfloat16
I32 = mybir.dt.int32
U16 = mybir.dt.uint16

P = 128
N, D = 3125, 64
NB = (N + P - 1) // P
NPAD = NB * P
HALF = P // 2
NFULL = N // P
NREST = N - NFULL * P
E = 103125
R = 8
EF = 16
LAYERS, HEADS = 5, 2
NEG_SLOPE = 0.2
LN_EPS = 1e-5
BIG = 1e30

TE, KE = 125, 11
GE = E // (TE * KE)
BUF3 = 3
assert GE * TE * KE == E and GE % BUF3 == 0

G = 8
NG = 104
NT = NG * G
SL = NT * P
GS = G * P
assert NT >= (E + (P - 1) * NB) // P + 1
TURN = 26
NIT = NG // TURN
assert NIT * TURN == NG
NRB = G
TURNS = 4
BACK = 4
W_PAY = EF + 4
UNITS = W_PAY // TURNS
ACC = 100
PER_BANK = 5
BANK = 512
NBANK = NB // PER_BANK
EA1 = EF + 1
LOOP = D + HEADS * EA1
XC = HEADS * D + 2 * HEADS
LB = 8
LH = LB // 2
PER_LAYER = 226
FILL_ROWS = SL // P // 16
SB = (NB + 3) // 4
HB = ((NB + 7) // 8, (NB + 3) // 8)
TC = (NT + P - 1) // P
CHUNKS = [(c, min(P, NT - c * P)) for c in range(TC)]
NODE_BATCHES = [(b, min(4, NB - b)) for b in range(0, NB, 4)]


class Order:

    def __init__(self, eng, sem):
        self.eng, self.sem, self.base, self.n = eng, sem, 0, 0

    def step(self, ins):
        self.n += 1
        ins.then_inc(self.sem, 1)

    def settle(self):
        self.eng.wait_ge(self.sem, self.base + self.n)

    def link(self, ins):
        self.step(ins)
        self.settle()

    @contextmanager
    def loop(self, count, per):
        base, n = self.base, self.n
        with self.eng.Fori(0, count) as i:
            self.base, self.n = base + n + i * per, 0
            yield i
            assert self.n == per, (self.n, per)
        self.base, self.n = base, n + count * per


def build_gnn(nc, x, src, dst, edge_attr_16, edge_type_8, edge_weight1, L0_gnn_weight, L0_gnn_h_bias,
              L0_gnn_loop_weight, L1_gnn_weights, L1_gnn_biases, L1_gnn_edge_ws, L1_gnn_edge_bs, L1_gnn_atts, out):
    def dram(name, shape, dt=F32):
        return nc.dram_tensor(name, shape, dt, kind="Internal").ap()

    rows_dram = dram("rows_dram", [GE, 2, TE * KE], U16)
    slots = dram("slots", [SL, W_PAY])
    fill_dram = dram("fill_dram", [SL + NPAD, 4])
    ea_dram = dram("ea_dram", [P, NT * EF])
    ce_dram = dram("ce_dram", [LAYERS, P, HEADS * NT])
    lohot_dram = dram("lohot_dram", [NG, P, GS], BF16)
    hihot_dram = dram("hihot_dram", [NG, P, G * NB], BF16)
    lo_dram = dram("lo_dram", [SL], BF16)
    tab0 = dram("tab0", [NPAD, R * D])
    tab1 = dram("tab1", [NPAD, HEADS * D])

    with ExitStack() as ctx:
        def sb(name, shape, dt=F32, where=ctx):
            return where.enter_context(nc.sbuf_tensor(name, shape, dt))

        def sem(name):
            return ctx.enter_context(nc.semaphore(name))

        ps = ctx.enter_context(nc.psum_tensor("ps", [P, 8, BANK], F32))

        ident = sb("ident", [P, P])
        iota_row = sb("iota_row", [P, P])
        iota_col = sb("iota_col", [P, 1])
        ones = sb("ones", [P, P])
        zeros = sb("zeros", [P, BANK])
        nothing16 = sb("nothing16", [P, P], BF16)
        gate = sb("gate", [P, 1], I32)
        gate2 = sb("gate2", [P, 1])
        gate_act = sb("gate_act", [P, 2])

        x_res = sb("x_res", [P, NB, D])
        h_sb = sb("h_sb", [P, NB, D])
        start_row = sb("start_row", [P, NB], I32)
        rel = sb("rel", [P, NT])
        idx = sb("idx", [P, NT + TURN * G], I32)
        tile_off = sb("tile_off", [1, NT], I32)
        lone = sb("lone", [P, NB])
        tile0 = sb("tile0", [P, NB])
        mean = sb("mean", [P, NB])
        var = sb("var", [P, NB])
        w_ext = sb("w_ext", [D, LAYERS, XC])
        w_out = sb("w_out", [LOOP + 1, LAYERS, D])
        w_out_l = sb("w_out_l", [LOOP + 1, D])
        att_bias = sb("att_bias", [P, LAYERS, HEADS])

        with ExitStack() as prep:
            rows16 = sb("rows16", [GE, 2, KE * TE], U16, prep)
            edge_c = sb("edge_c", [TE, 6, GE, KE], F32, prep)
            iota16 = sb("iota16", [P, P], BF16, prep)
            edge_parts = sb("edge_parts", [TE, 4, GE, KE], BF16, prep)
            lo_hot = sb("lo_hot", [TE, BUF3, KE, P], BF16, prep)
            hi_hot = sb("hi_hot", [TE, BUF3, KE, NB], BF16, prep)
            payload = sb("payload", [TE, BUF3, KE * W_PAY], F32, prep)
            snap = sb("snap", [P, BUF3, KE + 1, NB], F32, prep)
            picked = sb("picked", [TE, KE, NB], F32, prep)
            base_at = sb("base_at", [TE, KE], F32, prep)
            pos = sb("pos", [TE, BUF3, KE], I32, prep)
            hist = sb("hist", [P, NB], F32, prep)
            before = sb("before", [P, P], F32, prep)
            tiles_i = sb("tiles_i", [P, NB], I32, prep)
            tiles_f = sb("tiles_f", [P, NB], F32, prep)
            tiles_cum = sb("tiles_cum", [P, NB], F32, prep)
            first = sb("first", [P, NB], F32, prep)
            spare_row = sb("spare_row", [P, NB], F32, prep)
            before16 = sb("before16", [P, P], BF16, prep)
            ones16 = sb("ones16", [P, 1], BF16, prep)
            zeros16 = sb("zeros16", [P, BANK], BF16, prep)
            empty_slots = sb("empty_slots", [P, 4, W_PAY], F32, prep)
            empty_fill = sb("empty_fill", [P, FILL_ROWS, 4], F32, prep)
            w_types = sb("w_types", [D, R * D], F32, prep)
            w_loop = sb("w_loop", [D, D], F32, prep)
            bias_types = sb("bias_types", [P, D], F32, prep)
            tab0_sb = sb("tab0_sb", [P, R * D], F32, prep)
            hT = sb("hT", [D, NPAD], F32, prep)
            hT_block = sb("hT_block", [D, P], F32, prep)
            centred0 = sb("centred0", [P, NB, D], F32, prep)
            with ExitStack() as stage:
                edge_i = sb("edge_i", [GE, 3, KE * TE], I32, stage)
                edge_t = sb("edge_t", [GE, 6, KE, TE], F32, stage)
                part_i = sb("part_i", [GE, 2, KE * TE], I32, stage)
            with ExitStack() as stage:
                row_in = sb("row_in", [P, BUF3, 2, KE * TE], U16, stage)
                lo_hotT = sb("lo_hotT", [P, BUF3, KE, TE], F32, stage)
                same = sb("same", [TE, BUF3, KE, TE], BF16, stage)

        idx_stage = sb("idx_stage", [P, TURN * G], I32)
        ring = sb("ring", [P, TURN * G * P])
        hT_l = ring[0:D, 0:NPAD]
        sumsT = ring[0:LOOP + 1, NPAD:2 * NPAD]
        ring0 = ring[:, 0:TURN * G * D].rearrange("p (t c) -> p t c", c=D)
        left_over = ring[:, TURN * G * D:]
        back = ring[0:NG, 0:BACK * P * W_PAY].rearrange("p (q c) -> p q c", q=BACK)
        rest = left_over[:, 2 * P * W_PAY:]
        iota_tile, blk = rest[:, 0:NT], rest[:, NT:2 * NT]
        off_f = rest[0:1, 2 * NT:4 * NT].rearrange("p (a t) -> p a t", a=2)
        ea_pack = rest[:, 4 * NT:4 * NT + 2 * NG * EF].rearrange("p (q c) -> p q c", q=2)
        ce_size, onehot_size, sums_size = LAYERS * HEADS * NT, 2 * G * P, 2 * G * D
        ce_sb = left_over[:, 0:ce_size].rearrange("p (c t) -> p c t", t=NT)
        onehot0 = left_over[:, ce_size:ce_size + onehot_size].rearrange("p (q t c) -> p q t c", q=2, t=G)
        sums0 = left_over[:, ce_size + onehot_size:ce_size + onehot_size + sums_size].rearrange(
            "p (q t c) -> p q t c", q=2, t=G)
        centred = left_over[:, ce_size + onehot_size + sums_size:][:, 0:NB * D].rearrange("p (b d) -> p b d", d=D)
        ea_in_sb = sb("ea_in_sb", [P, 2, G * EF])
        keep = sb("keep", [NG, GS], BF16)
        keep_neg = sb("keep_neg", [NG, GS], BF16)
        keep_back_neg = sb("keep_back_neg", [NG, GS], BF16)
        head_run = sb("head_run", [NG, GS], BF16)
        head_neg = sb("head_neg", [NG, GS], BF16)
        tail_neg = sb("tail_neg", [NG, GS], BF16)
        row_flags = sb("row_flags", [P, 3, P])
        carry_row = sb("carry_row", [P, P])
        carry_col = sb("carry_col", [P, P])
        carry_in = sb("carry_in", [P, 4])
        with ExitStack() as zero:
            pay = sb("pay", [P, 4, NT], F32, zero)
            idx0 = sb("idx0", [P, NT + TURN * G], I32, zero)
            src_hi = sb("src_hi", [P, NT], F32, zero)
            w_turned = sb("w_turned", [P, LAYERS, D], F32, zero)
            att = sb("att", [P, LAYERS, 2 * HEADS], F32, zero)
            edge_nat = sb("edge_nat", [P, LAYERS, EF], F32, zero)
            edge_bias = sb("edge_bias", [P, LAYERS], F32, zero)
            edge_att = sb("edge_att", [EF, LAYERS * HEADS], F32, zero)
            edge_att8 = sb("edge_att8", [P, G, LAYERS * HEADS], F32, zero)
            with ExitStack() as early:
                idx0_f = sb("idx0_f", [P, NT], F32, early)
                keys = sb("keys", [NG, GS + 2], F32, early)
                keep_back = sb("keep_back", [NG, GS], BF16, early)
                tail_run = sb("tail_run", [NG, GS], BF16, early)
                lo_i = sb("lo_i", [P, TC, P], I32, early)
                hi_i = sb("hi_i", [P, NT], I32, early)
                lo16 = sb("lo16", [P, TC, P], BF16, early)
            ea_turned = sb("ea_turned", [P, 2, P], F32, zero)
            lo_in_sb = sb("lo_in_sb", [P, 2, GS], BF16, zero)
            lo_hot0 = sb("lo_hot0", [P, 2, GS], BF16, zero)
            hi_hot0 = sb("hi_hot0", [P, 2, G * NB], BF16, zero)
        with ExitStack() as zero:
            node_terms = sb("node_terms", [P, NB, 4], F32, zero)
            loop_w = sb("loop_w", [P, NB, HEADS], F32, zero)
            s_src3 = sb("s_src3", [P, 3, HEADS, NB], BF16, zero)
            sj_part = sb("sj_part", [P, HEADS, LH * G], F32, zero)
            slot_vals = sb("slot_vals", [P, HEADS, NT], F32, zero)
            picked_n = sb("picked_n", [P, HEADS * NT], F32, zero)
            with ExitStack() as nodes:
                xt_sb = sb("xt_sb", [P, NB, HEADS * D], F32, nodes)
            filled = sb("filled", [P, GS, 4], F32, zero)
            with ExitStack() as stage:
                s_src = sb("s_src", [P, 2, HEADS, NB], F32, stage)
            with ExitStack() as stage:
                lo_hot_n = sb("lo_hot_n", [P, LB, GS], BF16, stage)
                hi_hot_n = sb("hi_hot_n", [P, LB, G * NB], BF16, stage)
            with ExitStack() as stage:
                scores_all = sb("scores_all", [NG, HEADS, GS], F32, stage)
                run_total = sb("run_total", [NG, 2, HEADS, GS], F32, stage)
            with ExitStack() as stage:
                onehot = sb("onehot", [P, 2, G, P], F32, stage)
                weighted = sb("weighted", [P, 2, G, HEADS, D], F32, stage)
                sums_in = sb("sums_in", [P, 2, G, ACC], F32, stage)
            with ExitStack() as stage:
                sums = sb("sums", [P, NB, ACC], F32, stage)
        loop_vals = picked_n[:].rearrange("p (h t) -> p h t", h=HEADS)
        sj_picked = picked_n[:, 0:LH * G * HEADS * NB].rearrange("p (q u h b) -> p q u h b", q=LH, u=G, h=HEADS)
        loop_messages = picked_n[:, 0:2 * 4 * HEADS * D].rearrange("p (q b h d) -> p q b h d", q=2, h=HEADS, d=D)
        scores, running, total = scores_all[:], run_total[:, 0], run_total[:, 1]

        consts_ready = sem("consts_ready")
        dve_steps = sem("dve_steps")
        act_steps = sem("act_steps")
        pe_steps = sem("pe_steps")
        pool_steps = sem("pool_steps")
        prep_over = sem("prep_over")
        edges_in = sem("edges_in")
        x_in = sem("x_in")
        rows_out = sem("rows_out")
        edge_rows_ready = sem("edge_rows_ready")
        edge_cols_ready = sem("edge_cols_ready")
        edge_turned = sem("edge_turned")
        edge_turn_used = sem("edge_turn_used")
        hist_onehots = sem("hist_onehots")
        hist_used = sem("hist_used")
        hist_read = sem("hist_read")
        prefix_done = sem("prefix_done")
        scat = [sem(f"scat{q}") for q in range(BUF3)]
        rows_in = [sem(f"rows_in{q}") for q in range(BUF3)]
        pos_onehots = sem("pos_onehots")
        pos_masks = sem("pos_masks")
        counts_ready = sem("counts_ready")
        snap_ready = sem("snap_ready")
        looked_up = sem("looked_up")
        pos_ready = sem("pos_ready")
        back_in = [sem(f"back_in{q}") for q in range(BACK)]
        ea_out = [sem(f"ea_out{q}") for q in range(2)]
        staged = sem("staged")
        gathered = [sem(f"gathered{j}") for j in range(TURN)]
        sums_ready = sem("sums_ready")
        sums_used = sem("sums_used")
        hT_turned = sem("hT_turned")
        w0_in = sem("w0_in")
        h_ready = sem("h_ready")
        loop_done = sem("loop_done")
        acc_read = sem("acc_read")
        back_packed = sem("back_packed")
        back_turned = sem("back_turned")
        block_ready = sem("block_ready")
        tiles_ready = sem("tiles_ready")
        tiles_iota = sem("tiles_iota")
        proj_done = sem("proj_done")
        tab0_out = sem("tab0_out")
        tab0_staged = sem("tab0_staged")
        var_ready = sem("var_ready")
        std_ready = sem("std_ready")
        w1_in = sem("w1_in")
        w1_zeroed = sem("w1_zeroed")
        w1_turned = sem("w1_turned")
        w1_copied = sem("w1_copied")
        w1_products = sem("w1_products")
        edge_att_ready = sem("edge_att_ready")
        edge_att8_in = sem("edge_att8_in")
        ea_back_turned = sem("ea_back_turned")
        ea_turned_ready = sem("ea_turned_ready")
        ce_done = sem("ce_done")
        ce_filled = sem("ce_filled")
        ce_out = sem("ce_out")
        ce_in = sem("ce_in")
        xt_back = sem("xt_back")
        hT_ready = [sem(f"hT_ready{q}") for q in range(2)]
        at_done = sem("at_done")
        loops_ready = sem("loops_ready")
        loops_turned = sem("loops_turned")
        loops_copied = sem("loops_copied")
        ea_used = sem("ea_used")
        lo_in = [sem(f"lo_in{q}") for q in range(2)]
        hots_made = sem("hots_made")
        hots_out = [sem(f"hots_out{q}") for q in range(2)]
        hots_in = [sem(f"hots_in{q}") for q in range(LB // 2)]
        keys_turned = sem("keys_turned")
        keys_ready = sem("keys_ready")
        keys_out = sem("keys_out")
        keys_in = sem("keys_in")
        flags_cols = sem("flags_cols")
        flags_turned = sem("flags_turned")
        xt_done = sem("xt_done")
        xt_copied = sem("xt_copied")
        tab1_out = sem("tab1_out")
        fill_ready = sem("fill_ready")
        fill_out = sem("fill_out")
        fill_in = sem("fill_in")
        s_src_ready = sem("s_src_ready")
        sj_done = sem("sj_done")
        sj_read = sem("sj_read")
        vals_ready = sem("vals_ready")
        vals_turned = sem("vals_turned")
        carry_cols = sem("carry_cols")
        carry_turned = sem("carry_turned")
        carry_rows = sem("carry_rows")
        carry_back = sem("carry_back")
        shifted = sem("shifted")
        exp_done = sem("exp_done")
        weights_ready = sem("weights_ready")
        wturned = sem("wturned")
        wcopied = sem("wcopied")
        ea_in = [sem(f"ea_in{q}") for q in range(2)]
        sums_turned = sem("sums_turned")
        sumsT_ready = sem("sumsT_ready")
        sums_full = sem("sums_full")
        hT_done = sem("hT_done")
        outT_done = sem("outT_done")
        last_done = sem("last_done")
        out_done = sem("out_done")
        init_out = sem("init_out")
        payload_free = sem("payload_free")
        x_done = sem("x_done")
        empty_ready = sem("empty_ready")

        block = ctx.enter_context(nc.Block())

        nodes_in = [x[0:NFULL * P].rearrange("(b p) d -> p b d", p=P), x[NFULL * P:N]]
        slots_by_row = slots.rearrange("(g u e) w -> u g (e w)", u=G, e=P)
        tab0_rows = tab0.rearrange("n (r d) -> (n r) d", d=D)
        tab0_blocks = tab0.rearrange("(b p) c -> b p c", p=P)
        ring_rows = ring[:].rearrange("p (t c) -> p t c", c=P)

        def by_tile(line):
            whole = (NT // P) * P * P
            return (line[0:whole].rearrange("(c t e) -> t c e", t=P, e=P),
                    line[whole:SL].rearrange("(t e) -> t e", e=P))

        def bank(b, rows, cols, start=0):
            return ps[0:rows, b, start:start + cols]

        def acc_all(c0, c1):
            return ps[:, 0:NBANK, 0:PER_BANK * ACC].rearrange("p k (b c) -> p k b c", c=ACC)[:, :, :, c0:c1]

        @block.gpsimd
        def _(pool):
            order = Order(pool, pool_steps)
            nc.gpsimd.iota(iota_row[:], [[1, P]], base=0, channel_multiplier=0,
                           allow_small_or_imprecise_dtypes=True)
            nc.gpsimd.iota(iota_col[:], [[1, 1]], base=0, channel_multiplier=1,
                           allow_small_or_imprecise_dtypes=True)
            nc.gpsimd.iota(spare_row[:], [[P, NB]], base=SL, channel_multiplier=1,
                           allow_small_or_imprecise_dtypes=True)
            nc.gpsimd.memset(ones[:], 1.0)
            nc.gpsimd.memset(ones16[:], 1.0)
            nc.gpsimd.memset(zeros[:], 0.0)
            nc.gpsimd.memset(nothing16[:], 0.0)
            nc.gpsimd.memset(zeros16[:], 0.0)
            order.step(nc.gpsimd.memset(gate[:], 0))
            nc.gpsimd.memset(empty_slots[:], 0.0)
            nc.gpsimd.memset(x_res[:, NFULL, :], 0.0).then_inc(consts_ready, 1)
            pool.wait_ge(init_out, 32)
            def arrived(semaphore, value):
                pool.wait_ge(semaphore, value)
                order.settle()
                order.step(nc.gpsimd.tensor_tensor(gate[:], gate[:], gate[:], ALU.add))

            with order.loop(GE // BUF3, BUF3) as i:
                for q in range(BUF3):
                    arrived(pos_ready, i * BUF3 + q + 1)
                    for k in range(KE):
                        pool.indirect_dma_start(
                            slots, bass.IndirectOffsetOnAxis(ap=pos[:, q, k:k + 1], axis=0),
                            payload[:, q, k * W_PAY:(k + 1) * W_PAY], None).then_inc(scat[q], 16)
            pool.wait_ge(prep_over, 1)
            nc.gpsimd.iota(iota_tile[:], [[1, G], [G, NG]], base=0, channel_multiplier=0,
                           allow_small_or_imprecise_dtypes=True).then_inc(tiles_iota, 1)

            def gather(table, ring_rows, it):
                for j in range(TURN):
                    arrived(staged, it * TURN + j + 1)
                    for t in range(j * G, (j + 1) * G):
                        pool.indirect_dma_start(
                            ring_rows[:, t, :], None, table,
                            bass.IndirectOffsetOnAxis(ap=idx_stage[:, t:t + 1], axis=0),
                        ).then_inc(gathered[j], 16)

            pool.wait_ge(tab0_out, 16 * (NB + 1))
            with order.loop(NIT, TURN) as i:
                gather(tab0_rows, ring0, i)

            with order.loop(LAYERS, 2 + NG) as l:
                arrived(fill_ready, l + 1)
                for b in range(NB):
                    pool.indirect_dma_start(
                        fill_dram, bass.IndirectOffsetOnAxis(ap=start_row[:, b:b + 1], axis=0),
                        node_terms[:, b, :], None).then_inc(fill_out, 16)
                arrived(tab1_out, l * 16 + 16)
                with order.loop(NIT, TURN) as i:
                    gather(tab1, ring_rows, (l + 1) * NIT + i)

        @block.sync
        def _(sp):
            sp.dma_start(edge_i[:, 0, :], dst.rearrange("(g k) -> g k", g=GE)).then_inc(edges_in, 16)
            sp.dma_start(edge_i[:, 1, :], src.rearrange("(g k) -> g k", g=GE)).then_inc(edges_in, 16)
            sp.dma_start(edge_i[:, 2, :], edge_type_8.rearrange("(g k) -> g k", g=GE)).then_inc(edges_in, 16)
            sp.dma_start(edge_t[:, 0, :, :].rearrange("g k e -> g (k e)"),
                         edge_weight1.rearrange("(g k) o -> g (k o)", g=GE)).then_inc(edges_in, 16)
            sp.wait_ge(consts_ready, 1)
            sp.dma_start(x_res[:, 0:NFULL, :], nodes_in[0]).then_inc(x_in, 16)
            sp.dma_start(x_res[0:NREST, NFULL, :], nodes_in[1]).then_inc(x_in, 16)
            sp.dma_start(w_types[:].rearrange("i (r o) -> i r o", r=R),
                         L0_gnn_weight.rearrange("r i o -> i r o")).then_inc(w0_in, 16)
            sp.dma_start(w_loop[:], L0_gnn_loop_weight).then_inc(w0_in, 16)
            sp.dma_start(bias_types[:], L0_gnn_h_bias.partition_broadcast(P)).then_inc(w0_in, 16)
            sp.wait_ge(empty_ready, 1)
            sp.dma_start(slots.rearrange("(p r c) w -> p r (c w)", p=P, c=4),
                         empty_slots[:].rearrange("p c w -> p (c w)").unsqueeze(1)
                         .to_broadcast([P, SL // (4 * P), 4 * W_PAY])).then_inc(init_out, 16)
            sp.dma_start(fill_dram[0:SL].rearrange("(p a r) c -> p a (r c)", p=P, r=FILL_ROWS),
                         empty_fill[:].rearrange("p r c -> p (r c)").unsqueeze(1)
                         .to_broadcast([P, SL // P // FILL_ROWS, FILL_ROWS * 4])).then_inc(init_out, 16)
            sp.wait_ge(edge_rows_ready, 2)
            sp.dma_start(rows_dram.rearrange("g a k -> g (a k)"),
                         rows16[:].rearrange("g a k -> g (a k)")).then_inc(rows_out, 16)
            sp.wait_ge(rows_out, 16)
            sp.wait_ge(edge_turn_used, KE)
            rows_flat = rows_dram.rearrange("g a k -> (g a k)")
            with sp.Fori(0, GE // BUF3) as i:
                for q in range(BUF3):
                    sp.wait_ge(payload_free, i * BUF3 + q + 1)
                    sp.dma_start(row_in[:, q, :, :].rearrange("p a k -> p (a k)"),
                                 rows_flat[bass.ds((i * BUF3 + q) * (2 * KE * TE), 2 * KE * TE)]
                                 .partition_broadcast(P)).then_inc(rows_in[q], 16)
                    sp.dma_start(payload[:, q, :].rearrange("e (k w) -> e k w", w=W_PAY)[:, :, 0:EF],
                                 edge_attr_16.rearrange("(g k e) f -> g e k f", k=KE, e=TE)
                                 [bass.ds(i * BUF3 + q, 1)].rearrange("o e k f -> (o e) k f")
                                 ).then_inc(rows_in[q], 16)
            sp.wait_ge(prep_over, 1)
            sp.wait_ge(tab0_out, 16 * (NB + 1))
            with sp.Fori(0, NRB // BACK) as i:
                for q in range(BACK):
                    sp.wait_ge(back_packed, (i * BACK + q + 1) * UNITS)
                    sp.dma_start(back[:, q, :],
                                 slots_by_row[bass.ds(i * BACK + q, 1)].rearrange("o g c -> (o g) c")).then_inc(back_in[q], 16)
            sp.wait_ge(w1_zeroed, 1)
            sp.dma_start(w_ext[:, :, 0:HEADS * D], L1_gnn_weights.rearrange("l i o -> i l o")).then_inc(w1_in, 16)
            sp.dma_start(edge_nat[:], L1_gnn_edge_ws.rearrange("l c f -> c l f")).then_inc(w1_in, 16)
            sp.dma_start(w_out[LOOP:LOOP + 1, :, :], L1_gnn_biases.unsqueeze(0)).then_inc(w1_in, 16)
            with nc.allow_non_contiguous_dma(reason="small weights, turned"):
                sp.dma_start(edge_bias[:], L1_gnn_edge_bs.rearrange("l c -> c l")).then_inc(w1_in, 16)
                for h in range(HEADS):
                    for side in range(2):
                        sp.dma_start(att[h * D:(h + 1) * D, :, side * HEADS + h],
                                     L1_gnn_atts[:, h, side * D:(side + 1) * D].rearrange("l c -> c l")).then_inc(w1_in, 16)
                    for l in range(LAYERS):
                        sp.dma_start(w_out[D + h * EA1:D + h * EA1 + EF, l, :],
                                     L1_gnn_edge_ws[l, h * D:(h + 1) * D, :].rearrange("c f -> f c")).then_inc(w1_in, 16)
                    sp.dma_start(w_out[D + h * EA1 + EF:D + (h + 1) * EA1, :, :],
                                 L1_gnn_edge_bs[:, h * D:(h + 1) * D].unsqueeze(0)).then_inc(w1_in, 16)
            sp.wait_ge(edge_att_ready, 1)
            for k in range(G):
                sp.dma_start(edge_att8[k * EF:(k + 1) * EF, k, :], edge_att[:]).then_inc(edge_att8_in, 16)
            sp.wait_ge(keys_ready, 1)
            whole, left = by_tile(lo_dram)
            sp.dma_start(whole, lo16[:, 0:NT // P, :]).then_inc(keys_out, 16)
            sp.dma_start(left, lo16[0:NT % P, NT // P, :]).then_inc(keys_out, 16)
            with nc.allow_non_contiguous_dma(reason="the slots beside each row"):
                sp.dma_start(keys[1:NG, 0:1], keys[0:NG - 1, GS:GS + 1]).then_inc(keys_in, 16)
                sp.dma_start(keys[0:NG - 1, GS + 1:GS + 2], keys[1:NG, 1:2]).then_inc(keys_in, 16)

            def load_features(turns, i, j):
                sp.wait_ge(ea_used, turns * TURN + j + 1)
                sp.dma_start(ea_in_sb[:, j % 2, :],
                             ea_dram[:, bass.ds(i * (TURN * G * EF) + j * G * EF, G * EF)]).then_inc(ea_in[j % 2], 16)

            lo_rows = lo_dram.rearrange("(g s) -> g s", g=NG)
            sp.wait_ge(keys_out, 32)
            sp.wait_ge(ea_out[0], 16 * (NRB // 2 + 1))
            sp.wait_ge(ea_out[1], 16 * (NRB // 2 + 1))
            with sp.Fori(0, NIT) as i:
                for j in range(TURN):
                    sp.wait_ge(hots_made, i * TURN + j + 1)
                    sp.dma_start(lo_in_sb[:, j % 2, :], lo_rows[bass.ds(i * TURN + j, 1)].rearrange("o s -> (o s)")
                                 .partition_broadcast(P)).then_inc(lo_in[j % 2], 16)
                    load_features(i, i, j)
            sp.wait_ge(hots_out[0], 16 + 32 * (NG // 2))
            sp.wait_ge(hots_out[1], 16 + 32 * (NG // 2))
            with sp.Fori(0, LAYERS) as l:
                with sp.Fori(0, NG // LB) as i:
                    for q in range(LB // 2):
                        if q == 0:
                            sp.wait_ge(s_src_ready, l + 1)
                        sp.wait_ge(sj_read, l * NG + i * LB + 2 * q + 2)
                        pair = slice(2 * q, 2 * q + 2)
                        sp.dma_start(lo_hot_n[:, pair, :],
                                     lohot_dram[bass.ds(i * LB + 2 * q, 2)].rearrange("g p s -> p g s")
                                     ).then_inc(hots_in[q], 16)
                        sp.dma_start(hi_hot_n[:, pair, :],
                                     hihot_dram[bass.ds(i * LB + 2 * q, 2)].rearrange("g p s -> p g s")
                                     ).then_inc(hots_in[q], 16)
                with sp.Fori(0, NIT) as i:
                    for j in range(TURN):
                        load_features((l + 1) * NIT + i, i, j)
            sp.wait_ge(x_done, 1)
            sp.dma_start(out[0:NFULL * P].rearrange("(b p) d -> p b d", p=P), x_res[:, 0:NFULL, :]).then_inc(out_done, 16)
            sp.dma_start(out[NFULL * P:N], x_res[0:NREST, NFULL, :]).then_inc(out_done, 16)
            sp.wait_ge(out_done, 32)

        @block.tensor
        def _(pe):
            order = Order(pe, pe_steps)
            pe.wait_ge(consts_ready, 1)
            pe.wait_ge(edge_cols_ready, 1)
            for k in range(KE):
                if k >= 2:
                    pe.wait_ge(edge_turn_used, k - 1)
                for a in range(6):
                    mm = nc.tensor.transpose(bank(k % 2, TE, GE, a * GE), edge_t[:, a, k, :], ident[0:GE, 0:GE])
                mm.then_inc(edge_turned, 1)
            nc.tensor.matmul(bank(6, HALF, 2 * NB), zeros16[:, 0:HALF], zeros16[:, 0:2 * NB],
                             start=True, stop=True).then_inc(hist_used, BUF3)
            with pe.Fori(0, GE // BUF3) as i:
                for q in range(BUF3):
                    pe.wait_ge(hist_onehots, i * BUF3 + q + 1)
                    for k in range(KE):
                        mm = nc.tensor.matmul(bank(6, HALF, 2 * NB), lo_hot[:, q, k, 0:HALF],
                                              lo_hot[:, q, k, HALF:HALF + 2 * NB],
                                              start=False, stop=True, skip_group_check=True)
                    mm.then_inc(hist_used, 1)
            pe.wait_ge(hist_read, 2)
            nc.tensor.matmul(bank(7, P, NB), before[:], hist[:], start=True, stop=True)
            nc.tensor.matmul(bank(7, P, NB, 32), ones[:], hist[:], start=True, stop=True).then_inc(prefix_done, 1)
            def positions(i):
                for q in range(BUF3):
                    pe.wait_ge(pos_onehots, i * BUF3 + q + 1)
                    nc.tensor.matmul(bank(q, P, (KE + 1) * NB), zeros16[:, 0:P], zeros16[:, 0:(KE + 1) * NB],
                                     start=True, stop=True)
                    for k in range(KE):
                        mm = nc.tensor.matmul(
                            bank(q, P, (KE - k) * NB, (k + 1) * NB).rearrange("p (a b) -> p a b", b=NB),
                            lo_hot[:, q, k, :], hi_hot[:, q, k:k + 1, :].to_broadcast([TE, KE - k, NB]),
                            start=False, stop=True, skip_group_check=True)
                    mm.then_inc(counts_ready, 1)
                    pe.wait_ge(pos_masks, i * BUF3 + q + 1)
                    for k in range(KE):
                        nc.tensor.matmul(bank(3 + q, TE, 1, KE * NB + k), same[:, q, k, :], ones16[0:TE, :],
                                         start=True, stop=True)
                    pe.wait_ge(snap_ready, i * BUF3 + q + 2)
                    for k in range(KE):
                        mm = nc.tensor.matmul(bank(3 + q, TE, NB, k * NB), lo_hotT[:, q, k, :],
                                              snap[:, q, k, :], start=True, stop=True)
                    mm.then_inc(looked_up, 1)

            positions(0)
            pe.wait_ge(w0_in, 48)
            pe.wait_ge(h_ready, 1)
            for n, (b0, nb) in enumerate(NODE_BATCHES):
                if n >= 2:
                    pe.wait_ge(hT_ready[n % 2], n // 2)
                for b in range(b0, b0 + nb):
                    mm = nc.tensor.transpose(bank(6 + n % 2, D, P, (b - b0) * P), h_sb[:, b, :], ident[:])
                mm.then_inc(hT_turned, 1)
            for q in range(2):
                pe.wait_ge(hT_ready[q], HB[q])
            for b in range(NB):
                mm = nc.tensor.matmul(bank(b // 8, P, D, (b % 8) * D), hT[:, b * P:(b + 1) * P], w_loop[:],
                                      start=True, stop=True)
            mm.then_inc(loop_done, 1)
            pe.wait_ge(acc_read, 1)

            def project(b):
                pe.wait_ge(block_ready, b + 1)
                nc.tensor.matmul(bank(7, P, R * D), hT_block[:], w_types[:],
                                 start=True, stop=True).then_inc(proj_done, 1)

            with pe.Fori(0, GE // BUF3 - 1) as i:
                project(i)
                positions(i + 1)
            project(NB - 1)

            def turn_lines(columns, b0, done):
                for c, rows in CHUNKS:
                    mm = nc.tensor.transpose(bank(b0 + c // 4, rows, P, (c % 4) * P), columns[:, c * P:c * P + rows], ident[:])
                mm.then_inc(done, 1)

            def turn_rows(columns, b0, done):
                for u in range(G):
                    mm = nc.tensor.transpose(bank(b0 + u // 4, NG, P, (u % 4) * P), columns[:, u * NG:(u + 1) * NG], ident[:])
                mm.then_inc(done, 1)

            def arrived(semaphore, value, b):
                pe.wait_ge(semaphore, value)
                nc.tensor.matmul(bank(b, P, 1, BANK - 1), nothing16[:], nothing16[:, 0:1], start=True, stop=True)

            columns_of = back.rearrange("g q (e w) -> g q w e", w=W_PAY)
            pe.wait_ge(prep_over, 1)
            with pe.Fori(0, NRB // BACK) as i:
                for q in range(BACK):
                    pe.wait_ge(back_in[q], i * 16 + 16)
                    for k in range(UNITS):
                        arrived(back_packed, (i * BACK + q + BACK - 1) * UNITS + k + 1, k)
                        for w in range(TURNS):
                            mm = nc.tensor.transpose(bank(k, P, NG, w * NG), columns_of[:, q, k * TURNS + w, :],
                                                     ident[0:NG, 0:NG])
                        mm.then_inc(back_turned, 1)

            def zero_acc(waits):
                pe.wait_ge(acc_read, waits)
                for k in range(NBANK):
                    mm = nc.tensor.matmul(bank(k, P, PER_BANK * ACC), zeros[:, 0:P], zeros[:, 0:PER_BANK * ACC],
                                          start=True, stop=True)
                mm.then_inc(sums_used, 2)

            def edge_products(i, j):
                q = j % 2
                pe.wait_ge(ea_in[q], i * (8 * TURN) + (j // 2 + 1) * 16)
                nc.tensor.transpose(bank(5, P, P, q * P), ea_in_sb[:, q, :], ident[:]).then_inc(ea_back_turned, 1)
                arrived(ea_turned_ready, i * TURN + j + 1, 6)
                nc.tensor.matmul(bank(6, P, G * LAYERS * HEADS, q * P), ea_turned[:, q, :],
                                 edge_att8[:].rearrange("p k c -> p (k c)"), start=True, stop=True).then_inc(ce_done, 1)

            def add_up(onehot, sums_in, turn, i):
                for j in range(TURN):
                    q = j % 2
                    width = sums_in.shape[3]
                    if width == D:
                        edge_products(i, j)
                    _, offs = nc.values_load_multi_w_load_instructions(
                        tile_off[0:1, bass.ds(i * (TURN * G) + j * G, G)], engines=[mybir.EngineType.PE],
                        min_val=0, max_val=(NBANK - 1) * BANK + (PER_BANK - 1) * ACC)
                    pe.wait_ge(sums_ready, turn * TURN + j + 1)
                    for u in range(G):
                        mm = nc.tensor.matmul(
                            ps[:].rearrange("p k c -> p (k c)")[:, bass.ds(offs[u], width)],
                            onehot[:, q, u, :], sums_in[:, q, u, :],
                            start=False, stop=True, skip_group_check=True)
                    mm.then_inc(sums_used, 1)

            pe.wait_ge(w1_in, 16 * (4 + 2 * HEADS + HEADS * (LAYERS + 1)))
            pe.wait_ge(back_packed, (NRB + BACK) * UNITS)
            for l in range(LAYERS):
                mm = nc.tensor.transpose(bank(5, P, D, l * D), w_ext[:, l, 0:HEADS * D], ident[0:D, 0:D])
            mm.then_inc(w1_turned, 1)
            pe.wait_ge(w1_copied, 1)
            for l in range(LAYERS):
                nc.tensor.matmul(bank(6, D, 2 * HEADS, l * 2 * HEADS), w_turned[:, l, :], att[:, l, :], start=True, stop=True)
                nc.tensor.matmul(bank(6, EF, HEADS, 32 + l * HEADS), edge_nat[:, l, :], att[:, l, HEADS:2 * HEADS],
                                 start=True, stop=True)
                mm = nc.tensor.matmul(bank(6, P, HEADS, 64 + l * HEADS), edge_bias[:, l:l + 1].to_broadcast([P, P]),
                                      att[:, l, HEADS:2 * HEADS], start=True, stop=True)
            mm.then_inc(w1_products, 1)
            turn_rows(pay[:, 1, :], 0, keys_turned)
            turn_lines(pay[:, 2, :], 2, keys_turned)
            pe.wait_ge(edge_att8_in, 16 * G)
            for k in range(2):
                pe.wait_ge(flags_cols, k + 1)
                nc.tensor.transpose(bank(7, 4, P, k * P), carry_col[:, 0:4], ident[:]).then_inc(flags_turned, 1)

            pe.wait_ge(keys_ready, 1)
            zero_acc(1)
            pe.wait_ge(tiles_ready, 1)
            with pe.Fori(0, NIT) as i:
                add_up(onehot0, sums0, i, i)

            pe.wait_ge(h_ready, 2)
            for n, (b0, nb) in enumerate(NODE_BATCHES):
                if n >= 2:
                    pe.wait_ge(hT_done, n - 1)
                for b in range(b0, b0 + nb):
                    mm = nc.tensor.transpose(bank(5 + n % 2, D, P, (b - b0) * P), h_sb[:, b, :], ident[:])
                mm.then_inc(hT_turned, 1)
            pe.wait_ge(hT_done, 2)
            with pe.Fori(0, LAYERS) as l:
                layer_w = w_ext[:, bass.ds(l, 1), :].rearrange("i o c -> i (o c)")
                for n, (b0, nb) in enumerate(NODE_BATCHES):
                    arrived(hT_done, l * SB + n + 1, 4)
                    for b in range(b0, b0 + nb):
                        mm = nc.tensor.matmul(bank(4, P, 2 * HEADS, b * 2 * HEADS), hT_l[:, b * P:(b + 1) * P],
                                              layer_w[:, HEADS * D:XC], start=True, stop=True)
                mm.then_inc(at_done, 1)
                for n, (b0, nb) in enumerate(NODE_BATCHES):
                    if n >= 4:
                        arrived(xt_copied, l * SB + n - 3, n % 4)
                    for b in range(b0, b0 + nb):
                        mm = nc.tensor.matmul(bank(n % 4, P, HEADS * D, (b - b0) * HEADS * D), hT_l[:, b * P:(b + 1) * P],
                                              layer_w[:, 0:HEADS * D], start=True, stop=True)
                    mm.then_inc(xt_done, 1)
                arrived(s_src_ready, l + 1, 4)
                with pe.Fori(0, NG // LB) as i:
                    for q in range(LB):
                        if q % 2 == 0:
                            pe.wait_ge(hots_in[q // 2], l * (32 * (NG // LB)) + i * 32 + 32)
                        pe.wait_ge(sj_read, l * NG + i * LB + q + 1 + LH)
                        for u in range(G):
                            for k in range(3):
                                mm = nc.tensor.matmul(bank(4 + q % LH, P, HEADS * NB, u * HEADS * NB),
                                                      lo_hot_n[:, q, u * P:(u + 1) * P],
                                                      s_src3[:, k, :, :].rearrange("p h b -> p (h b)"),
                                                      start=(k == 0), stop=(k == 2))
                        mm.then_inc(sj_done, 1)
                pe.wait_ge(xt_copied, l * SB + SB)
                arrived(vals_ready, l + 1, 0)
                for h in range(HEADS):
                    turn_rows(slot_vals[:, h, :], 2 * h, vals_turned)
                for r in range(5):
                    pe.wait_ge(carry_cols, l * 5 + r + 1)
                    nc.tensor.transpose(bank(7, P, P), carry_col[:], ident[:]).then_inc(carry_turned, 1)
                    pe.wait_ge(carry_rows, l * 5 + r + 1)
                    nc.tensor.transpose(bank(7, P, P, P), carry_row[:], ident[:]).then_inc(carry_back, 1)
                for h in range(HEADS):
                    arrived(weights_ready, l * HEADS + h + 1, 2 * h)
                    for u in range(G):
                        mm = nc.tensor.transpose(bank(2 * h + u // 4, P, NG, (u % 4) * NG), scores[:, h, u * P:(u + 1) * P],
                                                 ident[0:NG, 0:NG])
                    mm.then_inc(wturned, 1)
                arrived(loops_ready, l + 1, 4)
                for h in range(HEADS):
                    for u in range(G):
                        mm = nc.tensor.transpose(bank(4 + 2 * h + u // 4, P, NG, (u % 4) * NG),
                                                 filled[0:NG, u * P:(u + 1) * P, HEADS + h], ident[0:NG, 0:NG])
                    mm.then_inc(loops_turned, 1)
                arrived(wcopied, l * HEADS + HEADS, 0)
                arrived(loops_copied, l * HEADS + HEADS, 0)
                for k in range(NBANK):
                    nc.tensor.matmul(bank(k, P, PER_BANK * ACC), zeros[:, 0:P], zeros[:, 0:PER_BANK * ACC],
                                     start=True, stop=True)
                with pe.Fori(0, NIT) as i:
                    add_up(onehot[:], sums_in[:], (l + 1) * NIT + i, i)
                for n in range(SB + 1):
                    if n < SB:
                        b0, nb = NODE_BATCHES[n]
                        if n >= 2:
                            pe.wait_ge(sumsT_ready, l * SB + n - 1)
                        arrived(sums_full, l * SB + n + 1, 5 + n % 2)
                        for b in range(b0, b0 + nb):
                            mm = nc.tensor.transpose(bank(5 + n % 2, LOOP + 1, P, (b - b0) * P),
                                                     sums[:, b, 0:LOOP + 1], ident[:])
                        mm.then_inc(sums_turned, 1)
                    if n > 0:
                        b0, nb = NODE_BATCHES[n - 1]
                        if n > 4:
                            pe.wait_ge(hT_done, (l + 1) * SB + n - 4)
                        arrived(sumsT_ready, l * SB + n, (n - 1) % 4)
                        nc.tensor.matmul(bank((n - 1) % 4, D, nb * P), w_out_l[:], sumsT[:, b0 * P:(b0 + nb) * P],
                                         start=True, stop=True).then_inc(outT_done, 1)
            pe.wait_ge(hT_done, (LAYERS + 1) * SB)
            for b in range(NB):
                mm = nc.tensor.matmul(bank(b // 8, P, D, (b % 8) * D), sumsT[:, b * P:(b + 1) * P],
                                      w_out[:, LAYERS - 1, :], start=True, stop=True)
            mm.then_inc(last_done, 1)

        @block.vector
        def _(dve):
            order = Order(dve, dve_steps)
            V = nc.vector
            V.memset(empty_fill[:, :, 0:2], 0.0)
            V.memset(empty_fill[:, :, 2:4], -BIG)
            dve.wait_ge(consts_ready, 1)
            order.step(V.tensor_scalar(ident[:], iota_row[:], iota_col[:, 0:1], None, ALU.is_equal))
            order.step(V.tensor_scalar(before[:], iota_row[:], iota_col[:, 0:1], None, ALU.is_gt))
            order.link(V.tensor_scalar(before16[:], iota_row[:], iota_col[:, 0:1], None, ALU.is_gt))
            V.memset(empty_slots[:, :, EF + 1:EF + 2], -9999.0).then_inc(empty_ready, 1)
            dve.wait_ge(edges_in, 64)
            order.step(V.tensor_scalar(part_i[:, 0, :], edge_i[:, 0, :], P - 1, None, ALU.bitwise_and))
            order.link(V.tensor_scalar(part_i[:, 1, :], edge_i[:, 0, :], 7, None, ALU.arith_shift_right))
            V.tensor_copy(rows16[:, 0, :], edge_i[:, 0, :]).then_inc(edge_rows_ready, 1)
            V.tensor_copy(rows16[:, 1, :], part_i[:, 0, :]).then_inc(edge_rows_ready, 1)
            V.tensor_copy(edge_t[:, 1:4, :, :].rearrange("g a k e -> g a (k e)"), edge_i[:])
            V.tensor_copy(edge_t[:, 4:6, :, :].rearrange("g a k e -> g a (k e)"), part_i[:]).then_inc(edge_cols_ready, 1)

            def layernorm(x_sums, h_out, centred, n):
                order.link(V.tensor_reduce(mean[:], x_sums[:], AX, ALU.add))
                order.link(V.tensor_scalar(mean[:], mean[:], -1.0 / D, None, ALU.mult))
                order.link(V.tensor_tensor(centred, x_sums[:], mean[:].unsqueeze(2).to_broadcast([P, NB, D]), ALU.add))
                order.link(V.tensor_tensor(h_out[:], centred, centred, ALU.mult))
                order.link(V.tensor_reduce(var[:], h_out[:], AX, ALU.add))
                V.tensor_scalar(var[:], var[:], 1.0 / D, LN_EPS, ALU.mult, ALU.add).then_inc(var_ready, 1)
                dve.wait_ge(std_ready, n)
                order.link(V.reciprocal(var[:], var[:]))
                order.link(V.tensor_tensor(centred, centred, var[:].unsqueeze(2).to_broadcast([P, NB, D]), ALU.mult))
                last = V.tensor_scalar(h_out[:], centred, 0.0, None, ALU.max)
                if n == 1:
                    last.then_inc(h_ready, 1)
                else:
                    order.link(last)

            dve.wait_ge(x_in, 32)
            layernorm(x_res, h_sb, centred0[:], 1)
            for k in range(KE):
                dve.wait_ge(edge_turned, k + 1)
                last = V.tensor_copy(edge_c[:, :, :, k],
                                     bank(k % 2, TE, 6 * GE).rearrange("e (a g) -> e a g", a=6))
                last.then_inc(edge_turn_used, 1)
            dve.wait_ge(edge_turn_used, KE)

            order.step(V.tensor_copy(iota16[:], iota_row[:]))
            order.step(V.tensor_copy(edge_parts[:, 0:2], edge_c[:, 4:6]))
            order.link(V.tensor_scalar(edge_parts[:, 3], edge_c[:, 4], float(HALF), None, ALU.is_ge))
            order.link(V.scalar_tensor_tensor(out=edge_parts[:, 2], in0=edge_parts[:, 3], scalar=-float(HALF),
                                              in1=edge_c[:, 4], op0=ALU.mult, op1=ALU.add))
            order.link(V.scalar_tensor_tensor(out=edge_parts[:, 3], in0=edge_c[:, 5], scalar=2.0,
                                              in1=edge_parts[:, 3], op0=ALU.mult, op1=ALU.add))

            def edge_onehots(g, q):
                V.tensor_tensor(lo_hot[:, q, :, :], iota16[0:TE, :].unsqueeze(1).to_broadcast([TE, KE, P]),
                                edge_parts[:, 0, bass.ds(g, 1), :].rearrange("e o k -> e (o k)")
                                .unsqueeze(2).to_broadcast([TE, KE, P]), ALU.is_equal)
                return V.tensor_tensor(hi_hot[:, q, :, :], iota16[0:TE, 0:NB].unsqueeze(1).to_broadcast([TE, KE, NB]),
                                       edge_parts[:, 1, bass.ds(g, 1), :].rearrange("e o k -> e (o k)")
                                       .unsqueeze(2).to_broadcast([TE, KE, NB]), ALU.is_equal)

            with dve.Fori(0, GE // BUF3) as i:
                for q in range(BUF3):
                    dve.wait_ge(hist_used, i * BUF3 + q + 1)
                    for part, c0, count in ((2, 0, HALF), (3, HALF, 2 * NB)):
                        last = V.tensor_tensor(lo_hot[:, q, :, c0:c0 + count],
                                               iota16[0:TE, 0:count].unsqueeze(1).to_broadcast([TE, KE, count]),
                                               edge_parts[:, part, bass.ds(i * BUF3 + q, 1), :]
                                               .rearrange("e o k -> e (o k)").unsqueeze(2).to_broadcast([TE, KE, count]),
                                               ALU.is_equal)
                    last.then_inc(hist_onehots, 1)
            dve.wait_ge(hist_used, GE + BUF3)
            halves = bank(6, HALF, 2 * NB).rearrange("p (b a) -> p a b", a=2)
            for a in range(2):
                V.tensor_copy(hist[a * HALF:(a + 1) * HALF, :], halves[:, a, :]).then_inc(hist_read, 1)
            dve.wait_ge(prefix_done, 1)
            order.link(V.tensor_scalar(tiles_f[:], bank(7, P, NB, 32), float(P - 1), None, ALU.add))
            order.link(V.tensor_copy(tiles_i[:], tiles_f[:]))
            order.link(V.tensor_scalar(tiles_i[:], tiles_i[:], 7, None, ALU.arith_shift_right))
            order.link(V.tensor_copy(tiles_f[:], tiles_i[:]))
            order.link(V.tensor_tensor_scan(tiles_cum[:], ones[:, 0:NB], tiles_f[:], 0.0, ALU.mult, ALU.add))
            order.link(V.tensor_tensor(tile0[:], tiles_cum[:], tiles_f[:], ALU.subtract))
            order.link(V.scalar_tensor_tensor(out=first[:], in0=tile0[:], scalar=float(P), in1=bank(7, P, NB),
                                              op0=ALU.mult, op1=ALU.add))
            order.step(V.tensor_scalar(lone[:], hist[:], 0.0, None, ALU.is_equal))
            order.link(V.tensor_tensor(tiles_cum[:], spare_row[:], first[:], ALU.subtract))
            order.link(V.tensor_tensor(tiles_cum[:], tiles_cum[:], lone[:], ALU.mult))
            order.link(V.tensor_tensor(start_row[:], tiles_cum[:], first[:], ALU.add))
            V.tensor_copy(snap[:, BUF3 - 1, KE, :], first[:]).then_inc(snap_ready, 1)

            def positions(i):
                for q in range(BUF3):
                    g = i * BUF3 + q
                    prev = (q - 1) % BUF3
                    edge_onehots(g, q).then_inc(pos_onehots, 1)
                    dve.wait_ge(rows_in[q], i * 32 + 32)
                    V.tensor_scalar(lo_hotT[:, q, :, :].rearrange("p k e -> p (k e)"), row_in[:, q, 1, :],
                                    iota_col[:, 0:1], None, ALU.is_equal)
                    order.link(V.tensor_tensor(same[:, q, :, :],
                                               row_in[0:TE, q, 0, :].rearrange("p (k e) -> p k e", e=TE),
                                               edge_c[:, 1, bass.ds(g, 1), :].rearrange("e o k -> e (o k)")
                                               .unsqueeze(2).to_broadcast([TE, KE, TE]), ALU.is_equal))
                    V.tensor_tensor(same[:, q, :, :], same[:, q, :, :],
                                    before16[0:TE, 0:TE].unsqueeze(1).to_broadcast([TE, KE, TE]),
                                    ALU.mult).then_inc(pos_masks, 1)
                    V.tensor_copy(payload[:, q, :].rearrange("e (k w) -> e k w", w=W_PAY)[:, :, EF:W_PAY],
                                  edge_c[:, 0:4, bass.ds(g, 1), :].rearrange("e a o k -> e (o k) a"))
                    dve.wait_ge(counts_ready, g + 1)
                    dve.wait_ge(snap_ready, g + 1)
                    V.tensor_tensor(snap[:, q, :, :], bank(q, P, (KE + 1) * NB).rearrange("p (k b) -> p k b", b=NB),
                                    snap[:, prev, KE:KE + 1, :].to_broadcast([P, KE + 1, NB]),
                                    ALU.add).then_inc(snap_ready, 1)
                    dve.wait_ge(looked_up, g + 1)
                    order.link(V.tensor_tensor(picked[:], bank(3 + q, TE, KE * NB).rearrange("e (k b) -> e k b", b=NB),
                                               hi_hot[:, q, :, :], ALU.mult))
                    order.link(V.tensor_reduce(base_at[:], picked[:], AX, ALU.add))
                    V.tensor_tensor(pos[:, q, :], base_at[:], bank(3 + q, TE, KE, KE * NB),
                                    ALU.add).then_inc(pos_ready, 1)

            positions(0)
            for n, (b0, nb) in enumerate(NODE_BATCHES):
                dve.wait_ge(hT_turned, n + 1)
                V.tensor_copy(hT[:, b0 * P:(b0 + nb) * P], bank(6 + n % 2, D, nb * P)).then_inc(hT_ready[n % 2], 1)
            dve.wait_ge(loop_done, 1)
            V.tensor_tensor(x_res[:].rearrange("p b d -> p (b d)"), x_res[:].rearrange("p b d -> p (b d)"),
                            ps[:].rearrange("p k c -> p (k c)")[:, 0:NB * D], ALU.add).then_inc(acc_read, 1)
            dve.wait_ge(w0_in, 48)
            V.memset(gate2[:], 0.0).then_inc(tab0_out, 16)
            dve.wait_ge(tab0_out, 16)
            V.tensor_copy(hT_block[:], hT[:, 0:P]).then_inc(block_ready, 1)

            def add_bias(b):
                dve.wait_ge(proj_done, b + 1)
                dve.wait_ge(tab0_out, b * 16 + 16)
                V.tensor_tensor(tab0_sb[:].rearrange("p (r d) -> p r d", d=D),
                                bank(7, P, R * D).rearrange("p (r d) -> p r d", d=D),
                                bias_types[:].unsqueeze(1).to_broadcast([P, R, D]), ALU.add).then_inc(tab0_staged, 1)

            with order.loop(GE // BUF3 - 1, 3 * BUF3) as i:
                positions(i + 1)
                add_bias(i)
                V.tensor_scalar(hT_block[:], hT[:, bass.ds((i + 1) * P, P)], 0.0, None, ALU.add).then_inc(block_ready, 1)
            add_bias(NB - 1)

            for q in range(BUF3):
                dve.wait_ge(scat[q], GE // BUF3 * 16 * KE)
            order.link(V.memset(gate2[:], 0.0))
            V.memset(gate2[:], 0.0).then_inc(prep_over, 1)
            dve.wait_ge(prep_over, 1)
            V.memset(edge_att8[:], 0.0)
            V.memset(att[:], 0.0).then_inc(w1_zeroed, 1)

            V.memset(ea_pack[:, :, 0:1], 0.0).then_inc(back_packed, BACK * UNITS)
            for q in range(2):
                V.memset(gate2[:], 0.0).then_inc(ea_out[q], 16)
                dve.wait_ge(ea_out[q], 16)
            with dve.Fori(0, NRB // 2) as i:
                for q in range(2):
                    for k in range(UNITS):
                        u = i * 2 + q
                        dve.wait_ge(back_turned, u * UNITS + k + 1)
                        turned = bank(k, P, TURNS * NG).rearrange("p (w g) -> p w g", g=NG)
                        if k == 0:
                            dve.wait_ge(ea_out[q], i * 16 + 16)
                        if k < EF // TURNS:
                            features = ea_pack[:, q, :].rearrange("p (g f) -> p f g", f=EF)
                            V.tensor_scalar(features[:, k * TURNS:(k + 1) * TURNS, :], turned, 0.0, None,
                                            ALU.add).then_inc(back_packed, 1)
                        else:
                            V.tensor_scalar(pay[:, :, bass.ds(u * NG, NG)], turned, 0.0, None, ALU.add).then_inc(back_packed, 1)
            dve.wait_ge(back_packed, (NRB + BACK) * UNITS)
            order.step(V.scalar_tensor_tensor(out=idx0_f[:], in0=pay[:, 2, :], scalar=float(R), in1=pay[:, 3, :],
                                              op0=ALU.mult, op1=ALU.add))
            order.step(V.tensor_copy(idx[:, 0:NT], pay[:, 2, :]))
            order.step(V.tensor_copy(idx[:, NT:], pay[:, 2, 0:TURN * G]))
            order.link(V.tensor_copy(idx0[:, NT:], pay[:, 2, 0:TURN * G]))
            order.link(V.tensor_copy(idx0[:, 0:NT], idx0_f[:]))
            V.tensor_copy(idx_stage[:], idx0[:, 0:TURN * G]).then_inc(staged, TURN)
            dve.wait_ge(tiles_iota, 1)
            order.link(V.tensor_scalar(blk[:], iota_tile[:], tile0[:, 1:2], None, ALU.is_ge))
            for b in range(2, NB):
                order.link(V.scalar_tensor_tensor(out=blk[:], in0=iota_tile[:], scalar=tile0[:, b:b + 1], in1=blk[:],
                                                  op0=ALU.is_ge, op1=ALU.add))
            order.step(V.scalar_tensor_tensor(out=rel[:], in0=blk[:], scalar=-float(P), in1=pay[:, 1, :],
                                              op0=ALU.mult, op1=ALU.add))
            order.link(V.tensor_scalar(off_f[:, 0, :], blk[0:1, :], float(PER_BANK), None, ALU.is_ge))
            for k in range(2, NBANK):
                order.link(V.scalar_tensor_tensor(out=off_f[:, 0, :], in0=blk[0:1, :], scalar=float(PER_BANK * k),
                                                  in1=off_f[:, 0, :], op0=ALU.is_ge, op1=ALU.add))
            order.link(V.tensor_scalar(off_f[:, 0, :], off_f[:, 0, :], float(BANK - PER_BANK * ACC), None, ALU.mult))
            order.link(V.scalar_tensor_tensor(out=off_f[:, 1, :], in0=blk[0:1, :], scalar=float(ACC),
                                              in1=off_f[:, 0, :], op0=ALU.mult, op1=ALU.add))
            V.tensor_copy(tile_off[:], off_f[:, 1, :]).then_inc(tiles_ready, 1)

            dve.wait_ge(w1_turned, 1)
            V.tensor_copy(w_turned[:].rearrange("p l d -> p (l d)"), bank(5, P, LAYERS * D)).then_inc(w1_copied, 1)
            dve.wait_ge(w1_products, 1)
            V.tensor_copy(w_ext[:, :, HEADS * D:XC], bank(6, D, LAYERS * 2 * HEADS).rearrange("p (l c) -> p l c", l=LAYERS))
            V.tensor_scalar(w_out[0:D, :, :], ident[0:D, 0:D].unsqueeze(1).to_broadcast([D, LAYERS, D]),
                            1.0 / HEADS, None, ALU.mult)
            V.tensor_scalar(w_out[D:LOOP, :, :], w_out[D:LOOP, :, :], 1.0 / HEADS, None, ALU.mult)
            V.tensor_copy(att_bias[:].rearrange("p l h -> p (l h)"), bank(6, P, LAYERS * HEADS, 64))
            V.tensor_copy(edge_att[:], bank(6, EF, LAYERS * HEADS, 32)).then_inc(edge_att_ready, 1)
            order.step(V.memset(keys[:], -1.0))
            order.link(V.tensor_scalar(hi_i[:], idx[:, 0:NT], 7, None, ALU.arith_shift_right))
            order.step(V.tensor_copy(src_hi[:], hi_i[:]))
            dve.wait_ge(keys_turned, 2)
            mine = keys[:, 1:GS + 1]
            order.step(V.tensor_copy(mine.rearrange("g (k c) -> g k c", k=2), ps[0:NG, 0:2, :]))
            rows_of = ps[:, 2:4, :].rearrange("p k c -> p (k c)").rearrange("p (c e) -> p c e", e=P)
            for n, (c0, c1, rows) in enumerate(((0, NT // P, P), (NT // P, TC, NT % P))):
                order.link(V.tensor_copy(lo_i[0:rows, c0:c1, :], rows_of[0:rows, c0:c1, :]))
                order.link(V.tensor_scalar(lo_i[0:rows, c0:c1, :], lo_i[0:rows, c0:c1, :], P - 1, None, ALU.bitwise_and))
                order.link(V.tensor_copy(lo16[0:rows, c0:c1, :], lo_i[0:rows, c0:c1, :]))
            V.memset(gate2[:], 0.0).then_inc(keys_ready, 1)
            dve.wait_ge(keys_in, 32)
            order.step(V.tensor_tensor(keep[:], mine, keys[:, 0:GS], ALU.is_equal))
            order.link(V.tensor_tensor(keep_back[:], mine, keys[:, 2:GS + 2], ALU.is_equal))
            order.step(V.tensor_scalar(keep_neg[:], keep[:], -1.0, BIG, ALU.add, ALU.mult))
            order.step(V.tensor_scalar(keep_back_neg[:], keep_back[:], -1.0, BIG, ALU.add, ALU.mult))
            order.step(V.tensor_tensor_scan(head_run[:], keep[:], keep[:], 1.0, ALU.mult, ALU.mult))
            order.step(V.tensor_tensor_scan(tail_run[:, ::-1], keep_back[:, ::-1], keep_back[:, ::-1], 1.0, ALU.mult, ALU.mult))
            order.step(V.memset(carry_row[:], 0.0))
            order.link(V.memset(carry_col[:], 0.0))
            order.step(V.tensor_scalar(head_neg[:], head_run[:], -1.0, BIG, ALU.add, ALU.mult))
            order.step(V.tensor_scalar(tail_neg[:], tail_run[:], -1.0, BIG, ALU.add, ALU.mult))
            for k, flags in enumerate((head_run[:, GS - 1:GS], tail_run[:, 0:1])):
                V.tensor_copy(carry_col[0:NG, 0:4], flags.to_broadcast([NG, 4])).then_inc(flags_cols, 1)
                dve.wait_ge(flags_turned, k + 1)
                order.link(V.tensor_copy(row_flags[0:4, 2 * k, :], bank(7, 4, P, k * P)))
            order.step(V.tensor_scalar(row_flags[0:4, 1, :], row_flags[0:4, 0, :], -1.0, BIG, ALU.add, ALU.mult))
            order.link(V.tensor_scalar(row_flags[0:4, 2, :], row_flags[0:4, 2, :], -1.0, BIG, ALU.add, ALU.mult))
            for free, count in ((ea_used, 2), (hots_made, 2), (hots_out[0], 16), (hots_out[1], 16)):
                V.memset(gate2[:], 0.0).then_inc(free, count)
                dve.wait_ge(free, count)

            with dve.Fori(0, NIT) as i:
                for j in range(TURN):
                    q = j % 2
                    t0 = i * (TURN * G) + j * G
                    dve.wait_ge(ea_back_turned, i * TURN + j + 1)
                    V.tensor_copy(ea_turned[:, q, :], bank(5, P, P, q * P)).then_inc(ea_turned_ready, 1)
                    dve.wait_ge(lo_in[q], i * (8 * TURN) + (j // 2 + 1) * 16)
                    dve.wait_ge(hots_out[q], i * (16 * TURN) + (j // 2) * 32 + 16)
                    V.tensor_scalar(lo_hot0[:, q, :], lo_in_sb[:, q, :], iota_col[:, 0:1], None, ALU.is_equal)
                    V.tensor_tensor(hi_hot0[:, q, :].rearrange("p (u b) -> p u b", u=G),
                                    iota_row[:, 0:NB].unsqueeze(1).to_broadcast([P, G, NB]),
                                    src_hi[:, bass.ds(t0, G)].unsqueeze(2).to_broadcast([P, G, NB]),
                                    ALU.is_equal).then_inc(hots_made, 1)
                    dve.wait_ge(sums_used, i * TURN + j + 1)
                    V.tensor_tensor(onehot0[:, q, :, :], iota_row[:].unsqueeze(1).to_broadcast([P, G, P]),
                                    rel[:, bass.ds(t0, G)].unsqueeze(2).to_broadcast([P, G, P]), ALU.is_equal)
                    dve.wait_ge(ce_done, i * TURN + j + 1)
                    V.tensor_scalar(ce_sb[:, :, bass.ds(t0, G)],
                                    bank(6, P, G * LAYERS * HEADS, q * P).rearrange("p (u c) -> p c u", u=G),
                                    0.0, None, ALU.add).then_inc(ea_used, 1)
                    r = j * G
                    dve.wait_ge(gathered[j], i * (16 * G) + 16 * G)
                    V.tensor_tensor(sums0[:, q, :, :], ring0[:, r:r + G, :],
                                    pay[:, 0, bass.ds(t0, G)].unsqueeze(2).to_broadcast([P, G, D]),
                                    ALU.mult).then_inc(sums_ready, 1)
                    V.tensor_copy(idx_stage[:, r:r + G], idx0[:, bass.ds(t0 + TURN * G, G)]).then_inc(staged, 1)
            V.memset(gate2[:], 0.0).then_inc(ce_filled, 1)
            dve.wait_ge(sums_used, NG + 2)
            order.link(V.tensor_copy(centred.rearrange("p (k b) d -> p k b d", b=PER_BANK), acc_all(0, D)))
            order.link(V.tensor_tensor(x_res[:], x_res[:], centred, ALU.add))
            layernorm(x_res, h_sb, centred, 2)
            V.memset(gate2[:], 0.0).then_inc(h_ready, 1)
            for n, (b0, nb) in enumerate(NODE_BATCHES):
                dve.wait_ge(hT_turned, SB + n + 1)
                V.tensor_copy(hT_l[:, b0 * P:(b0 + nb) * P], bank(5 + n % 2, D, nb * P)).then_inc(hT_done, 1)
            dve.wait_ge(ce_out, 16)
            V.memset(gate2[:], 0.0).then_inc(sj_read, LB)

            def carry(columns, n, flags, backward, nothing, r, l):
                V.tensor_copy(carry_col[0:NG, 0:n], columns).then_inc(carry_cols, 1)
                dve.wait_ge(carry_turned, l * 5 + r + 1)
                rows = bank(7, n, NG)
                ops = (ALU.add, ALU.max) if nothing else (ALU.mult, ALU.add)
                if backward:
                    order.step(V.memset(carry_row[0:n, NG - 1:NG], nothing))
                    order.link(V.tensor_tensor_scan(carry_row[0:n, 0:NG - 1][:, ::-1], row_flags[0:n, flags, 1:NG][:, ::-1],
                                                    rows[:, 1:NG][:, ::-1], nothing, *ops))
                else:
                    order.step(V.memset(carry_row[0:n, 0:1], nothing))
                    order.link(V.tensor_tensor_scan(carry_row[0:n, 1:NG], row_flags[0:n, flags, 0:NG - 1],
                                                    rows[:, 0:NG - 1], nothing, *ops))
                V.memset(gate2[:], 0.0).then_inc(carry_rows, 1)
                dve.wait_ge(carry_back, l * 5 + r + 1)
                order.link(V.tensor_copy(carry_in[0:NG, 0:n], bank(7, NG, n, P)))

            def spread_back(values, spread, r, l):
                for h in range(HEADS):
                    order.step(V.tensor_tensor_scan(spread[:, h, ::-1], keep_back_neg[:, ::-1], values[:, h, ::-1], -BIG,
                                                    ALU.add, ALU.max))
                order.settle()
                carry(spread[:, :, 0], HEADS, 2, True, -BIG, r, l)
                for h in range(HEADS):
                    order.step(V.scalar_tensor_tensor(out=spread[:, h, :], in0=tail_neg[:], scalar=carry_in[0:NG, h:h + 1],
                                                      in1=spread[:, h, :], op0=ALU.add, op1=ALU.max))
                order.settle()

            with order.loop(LAYERS, PER_LAYER) as l:
                dve.wait_ge(at_done, l + 1)
                at = bank(4, P, NB * 2 * HEADS).rearrange("p (b c) -> p b c", b=NB)
                at_dst, at_src = at[:, :, 0:HEADS], at[:, :, HEADS:]
                order.link(V.tensor_tensor(node_terms[:, :, 0:HEADS], at_dst,
                                           att_bias[:, bass.ds(l, 1), :].to_broadcast([P, NB, HEADS]), ALU.add))
                order.link(V.tensor_tensor(loop_w[:], node_terms[:, :, 0:HEADS], at_src, ALU.add))
                V.scalar_tensor_tensor(out=node_terms[:, :, HEADS:], in0=loop_w[:], scalar=NEG_SLOPE,
                                       in1=loop_w[:], op0=ALU.mult, op1=ALU.max).then_inc(fill_ready, 1)
                at_src_t = at_src.rearrange("p b h -> p h b")
                order.link(V.tensor_copy(s_src3[:, 0, :, :], at_src_t))
                order.link(V.tensor_tensor(s_src[:, 0, :, :], at_src_t, s_src3[:, 0, :, :], ALU.subtract))
                order.link(V.tensor_copy(s_src3[:, 1, :, :], s_src[:, 0, :, :]))
                order.link(V.tensor_tensor(s_src[:, 1, :, :], s_src[:, 0, :, :], s_src3[:, 1, :, :], ALU.subtract))
                dve.wait_ge(ce_in, l * 16 + 16)
                V.tensor_copy(s_src3[:, 2, :, :], s_src[:, 1, :, :]).then_inc(s_src_ready, 1)
                with order.loop(NG // LB, 4) as i:
                    for half in range(2):
                        for q in range(half * LH, half * LH + LH):
                            dve.wait_ge(sj_done, l * NG + i * LB + q + 1)
                            if q % 2 == 0:
                                dve.wait_ge(hots_in[q // 2], l * (32 * (NG // LB)) + i * 32 + 32)
                            V.tensor_tensor(
                                sj_picked[:, q % LH, :, :, :],
                                bank(4 + q % LH, P, G * HEADS * NB).rearrange("p (u h b) -> p u h b", u=G, h=HEADS),
                                hi_hot_n[:, q, :].rearrange("p (u b) -> p u b", u=G).unsqueeze(2)
                                .to_broadcast([P, G, HEADS, NB]), ALU.mult).then_inc(sj_read, 1)
                        dve.wait_ge(sj_read, l * NG + i * LB + half * LH + LH + LB)
                        order.link(V.tensor_reduce(sj_part[:].rearrange("p h t -> p t h"),
                                                   sj_picked.rearrange("p q u h b -> p (q u) h b"), AX, ALU.add))
                        t0 = i * (LB * G) + half * (LH * G)
                        order.step(V.tensor_tensor(slot_vals[:, :, bass.ds(t0, LH * G)], sj_part[:],
                                                   slot_vals[:, :, bass.ds(t0, LH * G)], ALU.add))
                order.settle()
                V.memset(gate2[:], 0.0).then_inc(vals_ready, 1)

                dve.wait_ge(fill_in, l * 16 + 16)
                terms = filled[0:NG]
                for c in range(HEADS):
                    order.step(V.tensor_tensor_scan(terms[:, :, c], keep[:], terms[:, :, c], 0.0, ALU.mult, ALU.add))
                order.settle()
                carry(terms[:, GS - 1, 0:HEADS], HEADS, 0, False, 0.0, 0, l)
                for c in range(HEADS):
                    order.step(V.scalar_tensor_tensor(out=terms[:, :, c], in0=head_run[:], scalar=carry_in[0:NG, c:c + 1],
                                                      in1=terms[:, :, c], op0=ALU.mult, op1=ALU.add))
                order.settle()
                for h in range(HEADS):
                    dve.wait_ge(vals_turned, l * HEADS + h + 1)
                    order.step(V.tensor_tensor(scores[:, h, :], ps[0:NG, 2 * h:2 * h + 2, :].rearrange("p k c -> p (k c)"),
                                               terms[:, :, h], ALU.add))
                order.settle()
                order.link(V.scalar_tensor_tensor(out=scores, in0=scores, scalar=NEG_SLOPE, in1=scores,
                                                  op0=ALU.mult, op1=ALU.max))
                loops = terms[:, :, HEADS:].rearrange("g s h -> g h s")
                order.link(V.tensor_tensor(running, scores, loops, ALU.max))
                for h in range(HEADS):
                    order.step(V.tensor_tensor_scan(running[:, h, :], keep_neg[:], running[:, h, :], -BIG, ALU.add, ALU.max))
                order.settle()
                carry(running[:, :, GS - 1], HEADS, 1, False, -BIG, 1, l)
                for h in range(HEADS):
                    order.step(V.scalar_tensor_tensor(out=running[:, h, :], in0=head_neg[:], scalar=carry_in[0:NG, h:h + 1],
                                                      in1=running[:, h, :], op0=ALU.add, op1=ALU.max))
                order.settle()
                spread_back(running, total, 2, l)
                order.step(V.tensor_tensor(scores, scores, total, ALU.subtract))
                order.link(V.tensor_tensor(loops, loops, total, ALU.subtract))
                V.memset(gate2[:], 0.0).then_inc(shifted, 1)
                dve.wait_ge(exp_done, l + 1)
                order.link(V.tensor_tensor(running, loops, scores, ALU.add))
                for h in range(HEADS):
                    order.step(V.tensor_tensor_scan(running[:, h, :], keep[:], running[:, h, :], 0.0, ALU.mult, ALU.add))
                order.settle()
                carry(running[:, :, GS - 1], HEADS, 0, False, 0.0, 3, l)
                for h in range(HEADS):
                    order.step(V.scalar_tensor_tensor(out=running[:, h, :], in0=head_run[:], scalar=carry_in[0:NG, h:h + 1],
                                                      in1=running[:, h, :], op0=ALU.mult, op1=ALU.add))
                order.settle()
                spread_back(running, total, 4, l)
                for h in range(HEADS):
                    order.link(V.tensor_scalar(running[:, h, :], total[:, h, :], 1e-16, None, ALU.add))
                    order.link(V.reciprocal(running[:, h, :], running[:, h, :]))
                    V.tensor_tensor(scores[:, h, :], scores[:, h, :], running[:, h, :],
                                    ALU.mult).then_inc(weights_ready, 1)
                V.tensor_tensor(loops, loops, running, ALU.mult).then_inc(loops_ready, 1)
                for h in range(HEADS):
                    dve.wait_ge(wturned, l * HEADS + h + 1)
                    V.tensor_copy(slot_vals[:, h, :].rearrange("p (k c) -> p k c", k=2), ps[:, 2 * h:2 * h + 2, 0:NT // 2]
                                  ).then_inc(wcopied, 1)
                with order.loop(NIT, TURN) as i:
                    for j in range(TURN):
                        q = j % 2
                        t0 = i * (TURN * G) + j * G
                        r = j * G
                        w = slot_vals[:, :, bass.ds(t0, G)].rearrange("p h t -> p t h")
                        w_loop_t = loop_vals[:, :, bass.ds(t0, G)].rearrange("p h t -> p t h")
                        if j == 0:
                            dve.wait_ge(wcopied, l * HEADS + HEADS)
                            dve.wait_ge(loops_copied, l * HEADS + HEADS)
                        dve.wait_ge(sums_used, (l + 1) * NG + i * TURN + j + 1)
                        dve.wait_ge(gathered[j], l * (16 * G * NIT) + i * (16 * G) + 16 * G * (NIT + 1))
                        order.step(V.tensor_tensor(
                            weighted[:, q], ring_rows[:, r:r + G, :].rearrange("p t (h d) -> p t h d", h=HEADS),
                            w.unsqueeze(3).to_broadcast([P, G, HEADS, D]), ALU.mult))
                        V.tensor_tensor(onehot[:, q, :, :], iota_row[:].unsqueeze(1).to_broadcast([P, G, P]),
                                        rel[:, bass.ds(t0, G)].unsqueeze(2).to_broadcast([P, G, P]), ALU.is_equal)
                        dve.wait_ge(ea_in[q], (l + 1) * (16 * NG // 2) + i * (8 * TURN) + 16 * (j // 2 + 1))
                        edge_sums = sums_in[:, q, :, D:LOOP].rearrange("p t (h f) -> p t h f", h=HEADS)
                        V.tensor_tensor(edge_sums[:, :, :, 0:EF],
                                        ea_in_sb[:, q, :].rearrange("p (t f) -> p t f", t=G).unsqueeze(2)
                                        .to_broadcast([P, G, HEADS, EF]),
                                        w.unsqueeze(3).to_broadcast([P, G, HEADS, EF]), ALU.mult).then_inc(ea_used, 1)
                        V.tensor_tensor(edge_sums[:, :, :, EF], w, w_loop_t, ALU.add)
                        V.tensor_scalar(sums_in[:, q, :, LOOP:ACC], w_loop_t, 0.0, None, ALU.add)
                        order.settle()
                        V.tensor_tensor(sums_in[:, q, :, 0:D], weighted[:, q, :, 0, :], weighted[:, q, :, 1, :],
                                        ALU.add).then_inc(sums_ready, 1)
                        V.tensor_copy(idx_stage[:, r:r + G],
                                      idx[:, bass.ds(t0 + TURN * G, G)]).then_inc(staged, 1)
                dve.wait_ge(sums_used, (l + 1) * NG + NG + 2)
                order.link(V.tensor_copy(sums[:].rearrange("p (k b) c -> p k b c", b=PER_BANK), acc_all(0, ACC)))
                dve.wait_ge(xt_back, l * 16 + 16)
                no_edges = lone[:].unsqueeze(2).to_broadcast([P, NB, HEADS])
                order.step(V.tensor_tensor(loop_w[:], sums[:, :, LOOP:ACC], no_edges, ALU.add))
                weight_sums = sums[:, :, D:LOOP].rearrange("p b (h f) -> p b h f", h=HEADS)[:, :, :, EF]
                order.link(V.tensor_tensor(weight_sums, weight_sums, no_edges, ALU.add))
                order.link(V.memset(sums[:, :, LOOP:LOOP + 1], 1.0))
                for n, (b0, nb) in enumerate(NODE_BATCHES):
                    blocks = slice(b0, b0 + nb)
                    message = loop_messages[:, n % 2, 0:nb]
                    order.link(V.tensor_tensor(message, xt_sb[:, blocks, :].rearrange("p b (h d) -> p b h d", h=HEADS),
                                               loop_w[:, blocks, :].unsqueeze(3).to_broadcast([P, nb, HEADS, D]), ALU.mult))
                    order.link(V.tensor_tensor(sums[:, blocks, 0:D], sums[:, blocks, 0:D], message[:, :, 0, :], ALU.add))
                    V.tensor_tensor(sums[:, blocks, 0:D], sums[:, blocks, 0:D], message[:, :, 1, :],
                                    ALU.add).then_inc(sums_full, 1)
                for n, (b0, nb) in enumerate(NODE_BATCHES):
                    dve.wait_ge(outT_done, l * SB + n + 1)
                    V.tensor_scalar(hT_l[:, b0 * P:(b0 + nb) * P], bank(n % 4, D, nb * P), 0.0, None,
                                    ALU.max).then_inc(hT_done, 1)
            dve.wait_ge(last_done, 1)
            V.tensor_tensor(x_res[:].rearrange("p b d -> p (b d)"), x_res[:].rearrange("p b d -> p (b d)"),
                            ps[:].rearrange("p k c -> p (k c)")[:, 0:NB * D], ALU.add).then_inc(x_done, 1)

        @block.scalar
        def _(act):
            order = Order(act, act_steps)
            act.wait_ge(consts_ready, 1)
            order.link(nc.scalar.copy(gate_act[:, 0:1], ones[:, 0:1]))
            nc.scalar.copy(gate_act[:, 1:2], gate_act[:, 0:1]).then_inc(payload_free, BUF3)

            def free_payload(i, q):
                act.wait_ge(payload_free, i * BUF3 + q + BUF3)
                act.wait_ge(scat[q], i * (16 * KE) + 16 * KE)
                nc.scalar.copy(gate_act[:, 1:2], gate_act[:, 0:1]).then_inc(payload_free, 1)

            def store_table(b):
                act.wait_ge(tab0_staged, b + 1)
                act.dma_start(tab0_blocks[bass.ds(b, 1)].rearrange("o p c -> (o p) c"), tab0_sb[:]).then_inc(tab0_out, 16)

            act.wait_ge(var_ready, 1)
            nc.scalar.activation(var[:], var[:], ACT.Sqrt).then_inc(std_ready, 1)
            for q in range(BUF3):
                free_payload(0, q)
            with act.Fori(0, GE // BUF3 - 1) as i:
                free_payload(i + 1, 0)
                free_payload(i + 1, 1)
                store_table(i)
                free_payload(i + 1, 2)
            store_table(NB - 1)
            with act.Fori(0, NRB // 2) as i:
                for q in range(2):
                    act.wait_ge(back_packed, (i * 2 + q + BACK + 1) * UNITS)
                    act.dma_start(ea_dram[:, bass.ds((i * 2 + q) * (NG * EF), NG * EF)], ea_pack[:, q, :]).then_inc(ea_out[q], 16)
            with act.Fori(0, NIT) as i:
                for j in range(TURN):
                    act.wait_ge(hots_made, i * TURN + j + 3)
                    act.dma_start(lohot_dram[bass.ds(i * TURN + j, 1)].rearrange("o p s -> (o p) s"),
                                  lo_hot0[:, j % 2, :]).then_inc(hots_out[j % 2], 16)
                    act.dma_start(hihot_dram[bass.ds(i * TURN + j, 1)].rearrange("o p s -> (o p) s"),
                                  hi_hot0[:, j % 2, :]).then_inc(hots_out[j % 2], 16)
            act.wait_ge(ce_filled, 1)
            act.dma_start(ce_dram.rearrange("l p c -> p l c"),
                          ce_sb.rearrange("p (l h) t -> p l (h t)", h=HEADS)).then_inc(ce_out, 16)
            act.wait_ge(var_ready, 2)
            nc.scalar.activation(var[:], var[:], ACT.Sqrt).then_inc(std_ready, 1)

            act.wait_ge(ce_out, 16)
            def arrived(semaphore, value):
                act.wait_ge(semaphore, value)
                order.settle()
                order.step(nc.scalar.copy(gate_act[:, 1:2], gate_act[:, 0:1]))

            with order.loop(LAYERS, 1) as l:
                for n, (b0, nb) in enumerate(NODE_BATCHES):
                    act.wait_ge(xt_done, l * SB + n + 1)
                    nc.scalar.copy(xt_sb[:, b0:b0 + nb, :].rearrange("p b c -> p (b c)"),
                                   bank(n % 4, P, nb * HEADS * D)).then_inc(xt_copied, 1)
                    if n == 0:
                        act.dma_start(slot_vals[:].rearrange("p h t -> p (h t)"),
                                      ce_dram[bass.ds(l, 1)].rearrange("o p c -> (o p) c")).then_inc(ce_in, 16)
                nc.scalar.copy(w_out_l[:], w_out[:, bass.ds(l, 1), :].rearrange("k o c -> k (o c)"))
                act.wait_ge(xt_copied, l * SB + SB)
                act.dma_start(tab1.rearrange("(b p) c -> p b c", p=P), xt_sb[:]).then_inc(tab1_out, 16)
                act.wait_ge(fill_out, l * (16 * NB) + 16 * NB)
                act.wait_ge(tab1_out, l * 16 + 16)
                act.wait_ge(s_src_ready, l + 1)
                act.dma_start(filled[0:NG].rearrange("g s c -> g (s c)"),
                              fill_dram[0:SL].rearrange("(g s) c -> g (s c)", g=NG)).then_inc(fill_in, 16)
                arrived(shifted, l + 1)
                nc.scalar.activation(scores, scores, ACT.Exp)
                loops = filled[0:NG, :, HEADS:]
                nc.scalar.activation(loops, loops, ACT.Exp).then_inc(exp_done, 1)
                for h in range(HEADS):
                    act.wait_ge(loops_turned, l * HEADS + h + 1)
                    nc.scalar.copy(loop_vals[:, h, :].rearrange("p (k c) -> p k c", k=2),
                                   ps[:, 4 + 2 * h:6 + 2 * h, 0:NT // 2]).then_inc(loops_copied, 1)
                act.dma_start(xt_sb[:], tab1.rearrange("(b p) c -> p b c", p=P)).then_inc(xt_back, 16)
                for n, (b0, nb) in enumerate(NODE_BATCHES):
                    act.wait_ge(sums_turned, l * SB + n + 1)
                    nc.scalar.copy(sumsT[:, b0 * P:(b0 + nb) * P],
                                   bank(5 + n % 2, LOOP + 1, nb * P)).then_inc(sumsT_ready, 1)


_OUTS = [((N, D), "float32")]
_INS = ["x", "src", "dst", "edge_attr_16", "edge_type_8", "edge_weight1", "L0_gnn_weight", "L0_gnn_h_bias",
        "L0_gnn_loop_weight", "L1_gnn_weights", "L1_gnn_biases", "L1_gnn_edge_ws", "L1_gnn_edge_bs", "L1_gnn_atts"]


def kernel(**inputs):
    import numpy as _np
    import concourse.bacc as _bacc
    from concourse import mybir as _mybir
    from concourse.bass_utils import run_bass_kernel_spmd as _run

    nc = _bacc.Bacc("TRN2", target_bir_lowering=False, num_devices=1)
    arrays, args = {}, []
    for name in _INS:
        a = _np.ascontiguousarray(inputs[name])
        arrays[f"in_{name}_dram"] = a
        args.append(nc.dram_tensor(f"in_{name}_dram", a.shape, _mybir.dt.from_np(a.dtype), kind="ExternalInput").ap())
    for i, (shape, dtype) in enumerate(_OUTS):
        dt = _mybir.dt.from_np(_np.dtype(dtype))
        args.append(nc.dram_tensor(f"out_{i}_dram", shape, dt, kind="ExternalOutput").ap())
    build_gnn(nc, *args)
    r = _run(nc, [arrays], core_ids=[0])
    return r.results[0]["out_0_dram"]
```
